# Optimizing a Trainium2 kernel written in Bass

```python
import numpy as np
import jax
import jax.numpy as jnp

def _softmax(x, axis=-1):
    return jax.nn.softmax(x, axis=axis)

def _gelu(x):
    return jax.nn.gelu(x, approximate=True)

def _silu(x):
    return jax.nn.silu(x)

def _sigmoid(x):
    return jax.nn.sigmoid(x)

def _layernorm(x, axis=-1, eps=1e-05):
    m = jnp.mean(x, axis=axis, keepdims=True)
    v = jnp.var(x, axis=axis, keepdims=True)
    return (x - m) / jnp.sqrt(v + eps)

def _scatter_add(tgt, idx, src, axis=0):
    return tgt.at[idx].add(src)

def _segment_sum(src, seg, n):
    return jax.ops.segment_sum(src, seg, n)
kernel_name = 'mk_decoder_preln_d2_seqx_r4_2c236e'

def setup_inputs(seed: int=0):
    np.random.seed(seed)
    _w = jnp.asarray

    def _rec_inputs():
        import jax
        import jax.numpy as jnp
        _rk = jax.random.key(seed)
        x = -0.0005146 + 1 * jax.random.normal(jax.random.fold_in(_rk, 1), (2, 1024, 256), jnp.float32)
        _lenS = 1024 - jax.random.randint(jax.random.fold_in(_rk, 7), (2,), 0, max(1, 1024 // 4) + 1, jnp.int32)
        _lenS2 = 64 - jax.random.randint(jax.random.fold_in(_rk, 8), (2,), 0, max(1, 64 // 4) + 1, jnp.int32)
        _ctx_768P = jax.random.normal(jax.random.fold_in(_rk, 11), (2, 16, 192), jnp.float32)
        _ctx_768c = jax.random.dirichlet(jax.random.fold_in(_rk, 511), 0.3 * jnp.ones((16,), jnp.float32), (2, 64))
        _ctx_768t = jnp.einsum('bsk,bkd->bsd', _ctx_768c, _ctx_768P)
        _ctx_768t = _ctx_768t * jax.lax.rsqrt(jnp.mean(jnp.square(_ctx_768t)) + 1e-12) * 0.953939
        ctx_768 = -0.00040386 + 0.999972 * (_ctx_768t + 0.3 * jax.random.normal(jax.random.fold_in(_rk, 611), (2, 64, 192), jnp.float32))
        _validS = jnp.arange(1024)[None, :] < _lenS[:, None]
        _validS2 = jnp.arange(64)[None, :] < _lenS2[:, None]
        _causal = jnp.tril(jnp.ones((1024, 1024), dtype=bool))
        mask_BxS2_bk0 = jnp.logical_not(jnp.broadcast_to(_validS2[:, :], (2, 64)))
        return (x, ctx_768, mask_BxS2_bk0)
    x, ctx_768, mask_BxS2_bk0 = _rec_inputs()

    def _L0_attn_setup():
        import jax, jax.numpy as jnp
        import numpy as np
        B, N, D = (4, 1024, 256)
        HEADS = 4
        DH = D // HEADS
        FF = 4 * D
        EPS = 1e-05

        def layer_norm(x, g, b):
            mu = jnp.mean(x, axis=-1, keepdims=True)
            var = jnp.mean(jnp.square(x - mu), axis=-1, keepdims=True)
            return (x - mu) * jax.lax.rsqrt(var + EPS) * g + b

        def linear_attn(q, k, v):
            scale = DH ** (-0.25)
            q = jax.nn.softmax(q * scale, axis=-1)
            k = jax.nn.softmax(k * scale, axis=-2)
            context = jnp.einsum('bhnd,bhne->bhde', k, v)
            return jnp.einsum('bhnd,bhde->bhne', q, context)
        key = jax.random.key(seed)
        ks = jax.random.split(key, 16)
        s = lambda fan_in: 1.0 / np.sqrt(fan_in)
        inp = {'x': jax.random.normal(ks[0], (B, N, D), jnp.float32), 'ln1_g': jnp.ones((D,), jnp.float32), 'ln1_b': jnp.zeros((D,), jnp.float32), 'wq': jax.random.normal(ks[1], (D, D), jnp.float32) * s(D), 'wk': jax.random.normal(ks[2], (D, D), jnp.float32) * s(D), 'wv': jax.random.normal(ks[3], (D, D), jnp.float32) * s(D), 'wo': jax.random.normal(ks[4], (D, D), jnp.float32) * s(D), 'bo': jnp.zeros((D,), jnp.float32), 'ln2_g': jnp.ones((D,), jnp.float32), 'ln2_b': jnp.zeros((D,), jnp.float32), 'w_ff1': jax.random.normal(ks[5], (D, FF), jnp.float32) * s(D), 'b_ff1': jnp.zeros((FF,), jnp.float32), 'w_ff2': jax.random.normal(ks[6], (FF, D), jnp.float32) * s(FF), 'b_ff2': jnp.zeros((D,), jnp.float32), 'w_d': jax.random.normal(ks[7], (D, D), jnp.float32) * s(D), 'b_d': jnp.zeros((D,), jnp.float32)}
        return inp
    _L0_attn_all = _L0_attn_setup()
    _L0_attn_in = {k: v for k, v in _L0_attn_all.items() if k in ('ln1_g', 'ln1_b', 'wq', 'wk', 'wv', 'wo', 'bo', 'ln2_g', 'ln2_b', 'w_ff1', 'b_ff1', 'w_ff2', 'b_ff2', 'w_d', 'b_d')}
    del _L0_attn_all

    def _L0_xattn_setup():
        import jax, jax.numpy as jnp
        import numpy as np
        DIM_IN, DIM_LAT, DIM_HEAD = (192, 256, 64)
        INNER = max(DIM_LAT, DIM_IN)
        HEADS = INNER // DIM_HEAD
        SCALE = DIM_HEAD ** (-0.5)
        RMS_EPS = 1e-08
        LN_EPS = 1e-05

        def layernorm(x, g, b):
            mu = jnp.mean(x, axis=-1, keepdims=True)
            var = jnp.mean((x - mu) ** 2, axis=-1, keepdims=True)
            return (x - mu) * jax.lax.rsqrt(var + LN_EPS) * g + b

        def rmsnorm(x, gamma):
            norm = jnp.sqrt(jnp.sum(x * x, axis=-1, keepdims=True)) * x.shape[-1] ** (-0.5)
            return x / jnp.maximum(norm, RMS_EPS) * gamma
        key = jax.random.key(seed)
        ks = jax.random.split(key, 12)
        b, n, m = (4, 1024, 128)
        x = jax.random.normal(ks[0], (b, n, DIM_IN), jnp.float32)
        latents = jax.random.normal(ks[1], (b, m, DIM_LAT), jnp.float32)
        mask = jax.random.randint(ks[2], (b, n), 0, 2).astype(bool)
        s = lambda k, sh, fan: jax.random.normal(k, sh, jnp.float32) * fan ** (-0.5)
        return {'x': x, 'latents': latents, 'mask': mask, 'ln_x_g': jnp.ones((DIM_IN,), jnp.float32), 'ln_x_b': jnp.zeros((DIM_IN,), jnp.float32), 'ln_l_g': jnp.ones((DIM_LAT,), jnp.float32), 'ln_l_b': jnp.zeros((DIM_LAT,), jnp.float32), 'qn_g': jnp.ones((DIM_HEAD,), jnp.float32), 'kn_g': jnp.ones((DIM_HEAD,), jnp.float32), 'Wq': s(ks[3], (INNER, DIM_LAT), DIM_LAT), 'Wkv': s(ks[4], (2 * INNER, DIM_IN), DIM_IN), 'Wlkv': s(ks[5], (2 * INNER, DIM_LAT), DIM_LAT), 'Wo': s(ks[6], (DIM_LAT, INNER), INNER), 'bo': jnp.zeros((DIM_LAT,), jnp.float32)}
    _L0_xattn_all = _L0_xattn_setup()
    _L0_xattn_in = {k: v for k, v in _L0_xattn_all.items() if k in ('ln_x_g', 'ln_x_b', 'ln_l_g', 'ln_l_b', 'qn_g', 'kn_g', 'Wq', 'Wkv', 'Wlkv', 'Wo', 'bo')}
    del _L0_xattn_all

    def _L0_ffn_setup():
        import jax, jax.numpy as jnp
        import numpy as np
        from jax import lax
        T, B, I, M, O = (64, 64, 256, 256, 256)

        def _xavier(key, shape):
            fan_out, fan_in = shape
            limit = float(np.sqrt(6.0 / (fan_in + fan_out)))
            return jax.random.uniform(key, shape, jnp.float32, -limit, limit)
        key = jax.random.key(seed)
        ks = jax.random.split(key, 9)
        x = jax.random.normal(ks[0], (T, B, I), jnp.float32)
        return {'x': x, 'wf': _xavier(ks[1], (M, I)), 'uf': _xavier(ks[2], (M, M)), 'bf': jnp.zeros((M,), jnp.float32), 'wi': _xavier(ks[3], (M, I)), 'ui': _xavier(ks[4], (M, M)), 'bi': jnp.zeros((M,), jnp.float32), 'wc': _xavier(ks[5], (M, I)), 'uc': _xavier(ks[6], (M, M)), 'bc': jnp.zeros((M,), jnp.float32), 'wo': _xavier(ks[7], (O, I)), 'uo': _xavier(ks[8], (O, M)), 'bo': jnp.zeros((O,), jnp.float32), 'in_c': jnp.zeros((M,), jnp.float32)}
    _L0_ffn_all = _L0_ffn_setup()
    _L0_ffn_in = {k: v for k, v in _L0_ffn_all.items() if k in ('wf', 'uf', 'bf', 'wi', 'ui', 'bi', 'wc', 'uc', 'bc', 'wo', 'uo', 'bo', 'in_c')}
    del _L0_ffn_all

    def _L1_attn_setup():
        import jax, jax.numpy as jnp
        import numpy as np
        import math
        DIM = 256
        N_HEADS = 16
        HEAD_DIM = DIM // N_HEADS
        B, S = (2, 512)
        key = jax.random.key(seed)
        k_x, k_wqkv, k_bqkv, k_wout, k_bout = jax.random.split(key, 5)
        scale_in = 1.0 / math.sqrt(DIM)
        x = jax.random.normal(k_x, (B, S, DIM), dtype=jnp.float32)
        Wqkv = jax.random.uniform(k_wqkv, (N_HEADS, DIM, 3 * HEAD_DIM), dtype=jnp.float32, minval=-scale_in, maxval=scale_in)
        bqkv = jax.random.uniform(k_bqkv, (N_HEADS, 3 * HEAD_DIM), dtype=jnp.float32, minval=-scale_in, maxval=scale_in)
        Wout = jax.random.uniform(k_wout, (DIM, DIM), dtype=jnp.float32, minval=-scale_in, maxval=scale_in)
        bout = jax.random.uniform(k_bout, (DIM,), dtype=jnp.float32, minval=-scale_in, maxval=scale_in)
        return {'x': x, 'Wqkv': Wqkv, 'bqkv': bqkv, 'Wout': Wout, 'bout': bout}
    _L1_attn_all = _L1_attn_setup()
    _L1_attn_in = {k: v for k, v in _L1_attn_all.items() if k in ('Wqkv', 'bqkv', 'Wout', 'bout')}
    del _L1_attn_all

    def _L1_xattn_setup():
        import jax, jax.numpy as jnp
        import numpy as np
        N_HEADS = 16
        DIM_EMBED = 256
        DIM_CROSS = 192
        DIM_HEAD = DIM_EMBED // N_HEADS
        key = jax.random.key(seed)
        ks = jax.random.split(key, 10)
        B, Sq, Sk = (8, 1024, 77)
        s_e = 1.0 / np.sqrt(DIM_EMBED)
        s_c = 1.0 / np.sqrt(DIM_CROSS)
        return {'x': jax.random.normal(ks[0], (B, Sq, DIM_EMBED), jnp.float32), 'y': jax.random.normal(ks[1], (B, Sk, DIM_CROSS), jnp.float32), 'wq': jax.random.normal(ks[2], (DIM_EMBED, DIM_EMBED), jnp.float32) * s_e, 'bq': jax.random.normal(ks[3], (DIM_EMBED,), jnp.float32) * 0.01, 'wk': jax.random.normal(ks[4], (DIM_CROSS, DIM_EMBED), jnp.float32) * s_c, 'bk': jax.random.normal(ks[5], (DIM_EMBED,), jnp.float32) * 0.01, 'wv': jax.random.normal(ks[6], (DIM_CROSS, DIM_EMBED), jnp.float32) * s_c, 'bv': jax.random.normal(ks[7], (DIM_EMBED,), jnp.float32) * 0.01, 'wo': jax.random.normal(ks[8], (DIM_EMBED, DIM_EMBED), jnp.float32) * s_e, 'bo': jax.random.normal(ks[9], (DIM_EMBED,), jnp.float32) * 0.01}
    _L1_xattn_all = _L1_xattn_setup()
    _L1_xattn_in = {k: v for k, v in _L1_xattn_all.items() if k in ('wq', 'bq', 'wk', 'bk', 'wv', 'bv', 'wo', 'bo')}
    del _L1_xattn_all

    def _L1_ffn_setup():
        import jax, jax.numpy as jnp
        import numpy as np
        B, L, M = (4, 512, 256)
        G, E = (8, 8)
        CAP_FACTOR = 2.0

        def _ffn_size(m, widening=8.0):
            f = int(widening * m) * 2 // 3
            return f + (8 - f) % 8
        H = _ffn_size(M)

        def _gating_top2(logits, C):
            Gd, Sd, Ed = logits.shape
            raw = jax.nn.softmax(logits, axis=-1)
            idx1 = jnp.argmax(raw, axis=-1)
            m1 = jax.nn.one_hot(idx1, Ed, dtype=logits.dtype)
            gate1 = jnp.sum(raw * m1, axis=-1)
            rest = raw * (1.0 - m1)
            idx2 = jnp.argmax(rest, axis=-1)
            m2 = jax.nn.one_hot(idx2, Ed, dtype=logits.dtype)
            gate2 = jnp.sum(rest * m2, axis=-1)
            p1 = jnp.cumsum(m1, axis=-2) - m1
            m1 = m1 * (p1 < C).astype(m1.dtype)
            p1 = jnp.sum(p1 * m1, axis=-1)
            m1_flat = jnp.sum(m1, axis=-1)
            m1_count = jnp.sum(m1, axis=-2)
            p2 = jnp.cumsum(m2, axis=-2) - m2 + m1_count[:, None, :]
            m2 = m2 * (p2 < C).astype(m2.dtype)
            p2 = jnp.sum(p2 * m2, axis=-1)
            m2_flat = jnp.sum(m2, axis=-1)
            gate1 = gate1 * m1_flat
            gate2 = gate2 * m2_flat
            c1 = (gate1[..., None] * jax.nn.one_hot(idx1, Ed, dtype=jnp.float32))[..., None] * jax.nn.one_hot(p1.astype(jnp.int32), C, dtype=jnp.float32)[:, :, None, :]
            c2 = (gate2[..., None] * jax.nn.one_hot(idx2, Ed, dtype=jnp.float32))[..., None] * jax.nn.one_hot(p2.astype(jnp.int32), C, dtype=jnp.float32)[:, :, None, :]
            combine = (c1 + c2).astype(logits.dtype)
            dispatch = (combine != 0).astype(logits.dtype)
            return (dispatch, combine)
        key = jax.random.key(seed)
        k0, k1, k2, k3, k4 = jax.random.split(key, 5)
        return {'inputs': jax.random.normal(k0, (B, L, M), jnp.float32), 'router_w': jax.random.normal(k1, (M, E), jnp.float32) * 0.02, 'w0_kernel': jax.random.normal(k2, (E, M, H), jnp.float32) * 0.02, 'w1_kernel': jax.random.normal(k3, (E, M, H), jnp.float32) * 0.02, 'wo_kernel': jax.random.normal(k4, (E, H, M), jnp.float32) * 0.02}
    _L1_ffn_all = _L1_ffn_setup()
    _L1_ffn_in = {k: v for k, v in _L1_ffn_all.items() if k in ('router_w', 'w0_kernel', 'w1_kernel', 'wo_kernel')}
    del _L1_ffn_all
    return {'x': x, 'ctx_768': ctx_768, 'mask_BxS2_bk0': mask_BxS2_bk0, 'L0_attn_ln1_g': _L0_attn_in['ln1_g'], 'L0_attn_ln1_b': _L0_attn_in['ln1_b'], 'L0_attn_wq': _L0_attn_in['wq'], 'L0_attn_wk': _L0_attn_in['wk'], 'L0_attn_wv': _L0_attn_in['wv'], 'L0_attn_wo': _L0_attn_in['wo'], 'L0_attn_bo': _L0_attn_in['bo'], 'L0_attn_ln2_g': _L0_attn_in['ln2_g'], 'L0_attn_ln2_b': _L0_attn_in['ln2_b'], 'L0_attn_w_ff1': _L0_attn_in['w_ff1'], 'L0_attn_b_ff1': _L0_attn_in['b_ff1'], 'L0_attn_w_ff2': _L0_attn_in['w_ff2'], 'L0_attn_b_ff2': _L0_attn_in['b_ff2'], 'L0_attn_w_d': _L0_attn_in['w_d'], 'L0_attn_b_d': _L0_attn_in['b_d'], 'L0_xattn_ln_x_g': _L0_xattn_in['ln_x_g'], 'L0_xattn_ln_x_b': _L0_xattn_in['ln_x_b'], 'L0_xattn_ln_l_g': _L0_xattn_in['ln_l_g'], 'L0_xattn_ln_l_b': _L0_xattn_in['ln_l_b'], 'L0_xattn_qn_g': _L0_xattn_in['qn_g'], 'L0_xattn_kn_g': _L0_xattn_in['kn_g'], 'L0_xattn_Wq': _L0_xattn_in['Wq'], 'L0_xattn_Wkv': _L0_xattn_in['Wkv'], 'L0_xattn_Wlkv': _L0_xattn_in['Wlkv'], 'L0_xattn_Wo': _L0_xattn_in['Wo'], 'L0_xattn_bo': _L0_xattn_in['bo'], 'L0_ffn_wf': _L0_ffn_in['wf'], 'L0_ffn_uf': _L0_ffn_in['uf'], 'L0_ffn_bf': _L0_ffn_in['bf'], 'L0_ffn_wi': _L0_ffn_in['wi'], 'L0_ffn_ui': _L0_ffn_in['ui'], 'L0_ffn_bi': _L0_ffn_in['bi'], 'L0_ffn_wc': _L0_ffn_in['wc'], 'L0_ffn_uc': _L0_ffn_in['uc'], 'L0_ffn_bc': _L0_ffn_in['bc'], 'L0_ffn_wo': _L0_ffn_in['wo'], 'L0_ffn_uo': _L0_ffn_in['uo'], 'L0_ffn_bo': _L0_ffn_in['bo'], 'L0_ffn_in_c': _L0_ffn_in['in_c'], 'L1_attn_Wqkv': _L1_attn_in['Wqkv'], 'L1_attn_bqkv': _L1_attn_in['bqkv'], 'L1_attn_Wout': _L1_attn_in['Wout'], 'L1_attn_bout': _L1_attn_in['bout'], 'L1_xattn_wq': _L1_xattn_in['wq'], 'L1_xattn_bq': _L1_xattn_in['bq'], 'L1_xattn_wk': _L1_xattn_in['wk'], 'L1_xattn_bk': _L1_xattn_in['bk'], 'L1_xattn_wv': _L1_xattn_in['wv'], 'L1_xattn_bv': _L1_xattn_in['bv'], 'L1_xattn_wo': _L1_xattn_in['wo'], 'L1_xattn_bo': _L1_xattn_in['bo'], 'L1_ffn_router_w': _L1_ffn_in['router_w'], 'L1_ffn_w0_kernel': _L1_ffn_in['w0_kernel'], 'L1_ffn_w1_kernel': _L1_ffn_in['w1_kernel'], 'L1_ffn_wo_kernel': _L1_ffn_in['wo_kernel']}

def reference(x, ctx_768, mask_BxS2_bk0, L0_attn_ln1_g, L0_attn_ln1_b, L0_attn_wq, L0_attn_wk, L0_attn_wv, L0_attn_wo, L0_attn_bo, L0_attn_ln2_g, L0_attn_ln2_b, L0_attn_w_ff1, L0_attn_b_ff1, L0_attn_w_ff2, L0_attn_b_ff2, L0_attn_w_d, L0_attn_b_d, L0_xattn_ln_x_g, L0_xattn_ln_x_b, L0_xattn_ln_l_g, L0_xattn_ln_l_b, L0_xattn_qn_g, L0_xattn_kn_g, L0_xattn_Wq, L0_xattn_Wkv, L0_xattn_Wlkv, L0_xattn_Wo, L0_xattn_bo, L0_ffn_wf, L0_ffn_uf, L0_ffn_bf, L0_ffn_wi, L0_ffn_ui, L0_ffn_bi, L0_ffn_wc, L0_ffn_uc, L0_ffn_bc, L0_ffn_wo, L0_ffn_uo, L0_ffn_bo, L0_ffn_in_c, L1_attn_Wqkv, L1_attn_bqkv, L1_attn_Wout, L1_attn_bout, L1_xattn_wq, L1_xattn_bq, L1_xattn_wk, L1_xattn_bk, L1_xattn_wv, L1_xattn_bv, L1_xattn_wo, L1_xattn_bo, L1_ffn_router_w, L1_ffn_w0_kernel, L1_ffn_w1_kernel, L1_ffn_wo_kernel):
    import jax
    import jax.numpy as jnp

    def _L0_attn_ref(x, ln1_g, ln1_b, wq, wk, wv, wo, bo, ln2_g, ln2_b, w_ff1, b_ff1, w_ff2, b_ff2, w_d, b_d):
        import jax, jax.numpy as jnp
        import numpy as np
        B, N, D = (4, 1024, 256)
        HEADS = 4
        DH = D // HEADS
        FF = 4 * D
        EPS = 1e-05

        def layer_norm(x, g, b):
            mu = jnp.mean(x, axis=-1, keepdims=True)
            var = jnp.mean(jnp.square(x - mu), axis=-1, keepdims=True)
            return (x - mu) * jax.lax.rsqrt(var + EPS) * g + b

        def linear_attn(q, k, v):
            scale = DH ** (-0.25)
            q = jax.nn.softmax(q * scale, axis=-1)
            k = jax.nn.softmax(k * scale, axis=-2)
            context = jnp.einsum('bhnd,bhne->bhde', k, v)
            return jnp.einsum('bhnd,bhde->bhne', q, context)
        b, n, d = x.shape
        h = layer_norm(x, ln1_g, ln1_b)
        q = (h @ wq).reshape(b, n, HEADS, DH).transpose(0, 2, 1, 3)
        k = (h @ wk).reshape(b, n, HEADS, DH).transpose(0, 2, 1, 3)
        v = (h @ wv).reshape(b, n, HEADS, DH).transpose(0, 2, 1, 3)
        attn = linear_attn(q, k, v)
        attn = attn.transpose(0, 2, 1, 3).reshape(b, n, d)
        x = x + attn @ wo + bo
        h = layer_norm(x, ln2_g, ln2_b)
        x = x + jax.nn.gelu(h @ w_ff1 + b_ff1) @ w_ff2 + b_ff2
        return x @ w_d + b_d

    def _L0_xattn_ref(x, latents, mask, ln_x_g, ln_x_b, ln_l_g, ln_l_b, qn_g, kn_g, Wq, Wkv, Wlkv, Wo, bo):
        import jax, jax.numpy as jnp
        import numpy as np
        DIM_IN, DIM_LAT, DIM_HEAD = (192, 256, 64)
        INNER = max(DIM_LAT, DIM_IN)
        HEADS = INNER // DIM_HEAD
        SCALE = DIM_HEAD ** (-0.5)
        RMS_EPS = 1e-08
        LN_EPS = 1e-05

        def layernorm(x, g, b):
            mu = jnp.mean(x, axis=-1, keepdims=True)
            var = jnp.mean((x - mu) ** 2, axis=-1, keepdims=True)
            return (x - mu) * jax.lax.rsqrt(var + LN_EPS) * g + b

        def rmsnorm(x, gamma):
            norm = jnp.sqrt(jnp.sum(x * x, axis=-1, keepdims=True)) * x.shape[-1] ** (-0.5)
            return x / jnp.maximum(norm, RMS_EPS) * gamma
        b, n, _ = x.shape
        m = latents.shape[1]
        xn = layernorm(x, ln_x_g, ln_x_b)
        ln = layernorm(latents, ln_l_g, ln_l_b)
        q = ln @ Wq.T
        kv = jnp.concatenate([xn @ Wkv.T, ln @ Wlkv.T], axis=1)
        k, v = (kv[..., :INNER], kv[..., INNER:])
        split_heads = lambda t: t.reshape(t.shape[0], t.shape[1], HEADS, DIM_HEAD).transpose(0, 2, 1, 3)
        q, k, v = (split_heads(q), split_heads(k), split_heads(v))
        qn = rmsnorm(q, qn_g) * SCALE
        kn = rmsnorm(k, kn_g)
        attn = jnp.einsum('bhid,bhjd->bhij', qn, kn)
        full_mask = jnp.pad(mask, ((0, 0), (0, m)), constant_values=True)
        attn = jnp.where(full_mask[:, None, None, :], attn, -jnp.finfo(attn.dtype).max)
        attn = jax.nn.softmax(attn, axis=-1)
        out = jnp.einsum('bhij,bhjd->bhid', attn, v)
        out = out.transpose(0, 2, 1, 3).reshape(b, m, INNER)
        return out @ Wo.T + bo

    def _L0_ffn_ref(x, wf, uf, bf, wi, ui, bi, wc, uc, bc, wo, uo, bo, in_c):
        import jax, jax.numpy as jnp
        import numpy as np
        from jax import lax
        T, B, I, M, O = (64, 64, 256, 256, 256)

        def _xavier(key, shape):
            fan_out, fan_in = shape
            limit = float(np.sqrt(6.0 / (fan_in + fan_out)))
            return jax.random.uniform(key, shape, jnp.float32, -limit, limit)
        batch = x.shape[1]
        c0 = jnp.broadcast_to(in_c, (batch, in_c.shape[0]))

        def step(c, xt):
            ft = jax.nn.sigmoid(xt @ wf.T + c @ uf.T + bf)
            it = jax.nn.sigmoid(xt @ wi.T + c @ ui.T + bi)
            gt = jnp.tanh(xt @ wc.T + c @ uc.T + bc)
            c = ft * c + it * gt
            return (c, None)
        c_final, _ = lax.scan(step, c0, x)
        h = jnp.tanh(jnp.einsum('tbi,oi->tbo', x, wo) + c_final @ uo.T + bo)
        return h

    def _L1_attn_ref(x, Wqkv, bqkv, Wout, bout):
        import jax, jax.numpy as jnp
        import numpy as np
        import math
        DIM = 256
        N_HEADS = 16
        HEAD_DIM = DIM // N_HEADS
        B, S = (2, 512)
        b, s, d = x.shape
        qkv = jnp.einsum('bsd,hde->bhse', x, Wqkv) + bqkv[None, :, None, :]
        q, k, v = jnp.split(qkv, 3, axis=-1)
        score = jnp.einsum('bhsd,bhtd->bhst', q, k)
        causal = jnp.tril(jnp.ones((s, s), dtype=bool))
        score = jnp.where(causal[None, None], score, -jnp.inf)
        attn = jax.nn.softmax(score / jnp.sqrt(jnp.asarray(HEAD_DIM, x.dtype)), axis=-1)
        y = jnp.einsum('bhst,bhtd->bhsd', attn, v)
        y = jnp.transpose(y, (0, 2, 1, 3)).reshape(b, s, d)
        out = y @ Wout + bout
        return out

    def _L1_xattn_ref(x, y, wq, bq, wk, bk, wv, bv, wo, bo):
        import jax, jax.numpy as jnp
        import numpy as np
        N_HEADS = 16
        DIM_EMBED = 256
        DIM_CROSS = 192
        DIM_HEAD = DIM_EMBED // N_HEADS
        B, Sq, E = x.shape
        H, D = (N_HEADS, DIM_HEAD)
        q = (x @ wq + bq).reshape(B, Sq, H, D).transpose(0, 2, 1, 3)
        k = (y @ wk + bk).reshape(B, -1, H, D).transpose(0, 2, 1, 3)
        v = (y @ wv + bv).reshape(B, -1, H, D).transpose(0, 2, 1, 3)
        scores = jnp.einsum('bhqd,bhkd->bhqk', q, k) / jnp.sqrt(jnp.asarray(D, x.dtype))
        attn = jax.nn.softmax(scores, axis=-1)
        out = jnp.einsum('bhqk,bhkd->bhqd', attn, v)
        out = out.transpose(0, 2, 1, 3).reshape(B, Sq, E)
        return out @ wo + bo

    def _L1_ffn_ref(inputs, router_w, w0_kernel, w1_kernel, wo_kernel):
        import jax, jax.numpy as jnp
        import numpy as np
        B, L, M = (4, 512, 256)
        G, E = (8, 8)
        CAP_FACTOR = 2.0

        def _ffn_size(m, widening=8.0):
            f = int(widening * m) * 2 // 3
            return f + (8 - f) % 8
        H = _ffn_size(M)

        def _gating_top2(logits, C):
            Gd, Sd, Ed = logits.shape
            raw = jax.nn.softmax(logits, axis=-1)
            idx1 = jnp.argmax(raw, axis=-1)
            m1 = jax.nn.one_hot(idx1, Ed, dtype=logits.dtype)
            gate1 = jnp.sum(raw * m1, axis=-1)
            rest = raw * (1.0 - m1)
            idx2 = jnp.argmax(rest, axis=-1)
            m2 = jax.nn.one_hot(idx2, Ed, dtype=logits.dtype)
            gate2 = jnp.sum(rest * m2, axis=-1)
            p1 = jnp.cumsum(m1, axis=-2) - m1
            m1 = m1 * (p1 < C).astype(m1.dtype)
            p1 = jnp.sum(p1 * m1, axis=-1)
            m1_flat = jnp.sum(m1, axis=-1)
            m1_count = jnp.sum(m1, axis=-2)
            p2 = jnp.cumsum(m2, axis=-2) - m2 + m1_count[:, None, :]
            m2 = m2 * (p2 < C).astype(m2.dtype)
            p2 = jnp.sum(p2 * m2, axis=-1)
            m2_flat = jnp.sum(m2, axis=-1)
            gate1 = gate1 * m1_flat
            gate2 = gate2 * m2_flat
            c1 = (gate1[..., None] * jax.nn.one_hot(idx1, Ed, dtype=jnp.float32))[..., None] * jax.nn.one_hot(p1.astype(jnp.int32), C, dtype=jnp.float32)[:, :, None, :]
            c2 = (gate2[..., None] * jax.nn.one_hot(idx2, Ed, dtype=jnp.float32))[..., None] * jax.nn.one_hot(p2.astype(jnp.int32), C, dtype=jnp.float32)[:, :, None, :]
            combine = (c1 + c2).astype(logits.dtype)
            dispatch = (combine != 0).astype(logits.dtype)
            return (dispatch, combine)
        Bb, Ll, Mm = inputs.shape
        S = Bb * Ll // G
        x = inputs.reshape(G, S, Mm)
        logits = jnp.einsum('GSM,ME->GSE', x, router_w)
        cap = int(CAP_FACTOR * S / E)
        C = (cap + 3) // 4 * 4
        dispatch, combine = _gating_top2(logits, C)
        expert_inputs = jnp.einsum('GSEC,GSM->EGCM', dispatch, x)
        layer_w0 = jnp.einsum('EGCM,EMH->EGCH', expert_inputs, w0_kernel)
        layer_w1 = jnp.einsum('EGCM,EMH->EGCH', expert_inputs, w1_kernel)
        hidden = jax.nn.gelu(layer_w0, approximate=True) * layer_w1
        expert_outputs = jnp.einsum('EGCH,EHM->EGCM', hidden, wo_kernel)
        out = jnp.einsum('EGCM,GSEC->GSM', expert_outputs, combine)
        return out.reshape(Bb, Ll, Mm)
    x = x + _L0_attn_ref(_layernorm(x, axis=-1), L0_attn_ln1_g, L0_attn_ln1_b, L0_attn_wq, L0_attn_wk, L0_attn_wv, L0_attn_wo, L0_attn_bo, L0_attn_ln2_g, L0_attn_ln2_b, L0_attn_w_ff1, L0_attn_b_ff1, L0_attn_w_ff2, L0_attn_b_ff2, L0_attn_w_d, L0_attn_b_d)
    x = x + _L0_xattn_ref(ctx_768, _layernorm(x, axis=-1), mask_BxS2_bk0, L0_xattn_ln_x_g, L0_xattn_ln_x_b, L0_xattn_ln_l_g, L0_xattn_ln_l_b, L0_xattn_qn_g, L0_xattn_kn_g, L0_xattn_Wq, L0_xattn_Wkv, L0_xattn_Wlkv, L0_xattn_Wo, L0_xattn_bo)
    x = x + _L0_ffn_ref(_layernorm(x, axis=-1), L0_ffn_wf, L0_ffn_uf, L0_ffn_bf, L0_ffn_wi, L0_ffn_ui, L0_ffn_bi, L0_ffn_wc, L0_ffn_uc, L0_ffn_bc, L0_ffn_wo, L0_ffn_uo, L0_ffn_bo, L0_ffn_in_c)
    x = x + _L1_attn_ref(_layernorm(x, axis=-1), L1_attn_Wqkv, L1_attn_bqkv, L1_attn_Wout, L1_attn_bout)
    x = x + _L1_xattn_ref(_layernorm(x, axis=-1), ctx_768, L1_xattn_wq, L1_xattn_bq, L1_xattn_wk, L1_xattn_bk, L1_xattn_wv, L1_xattn_bv, L1_xattn_wo, L1_xattn_bo)
    x = x + _L1_ffn_ref(_layernorm(x, axis=-1), L1_ffn_router_w, L1_ffn_w0_kernel, L1_ffn_w1_kernel, L1_ffn_wo_kernel)
    return x

_drawn_inputs = setup_inputs


def setup_inputs(seed=0):
    import zlib

    import numpy as np

    out = dict(_drawn_inputs(seed))
    spreads = {'L0_attn_ln1_g': (1.0, 0.6),
     'L0_attn_ln1_b': (0.0, 0.1),
     'L0_attn_bo': (0.0, 0.1),
     'L0_attn_ln2_g': (1.0, 0.2),
     'L0_attn_ln2_b': (0.0, 0.1),
     'L0_attn_b_ff1': (0.0, 0.1),
     'L0_attn_b_ff2': (0.0, 0.1),
     'L0_attn_b_d': (0.0, 0.1),
     'L0_xattn_ln_x_g': (1.0, 0.6),
     'L0_xattn_ln_x_b': (0.0, 0.8),
     'L0_xattn_ln_l_g': (1.0, 0.2),
     'L0_xattn_ln_l_b': (0.0, 0.1),
     'L0_xattn_qn_g': (1.0, 0.6),
     'L0_xattn_kn_g': (1.0, 0.6),
     'L0_xattn_bo': (0.0, 0.1),
     'L0_ffn_bf': (0.0, 0.8),
     'L0_ffn_bi': (0.0, 0.8),
     'L0_ffn_bc': (0.0, 0.513),
     'L0_ffn_bo': (0.0, 0.1),
     'L0_ffn_in_c': (0.0, 0.54)}
    factors = {'L0_attn_wq': 8.0,
     'L0_attn_wk': 8.0,
     'L0_xattn_Wkv': 7.532,
     'L0_ffn_uf': 7.457,
     'L0_ffn_ui': 3.979,
     'L1_attn_bqkv': 5.148,
     'L1_attn_bout': 3.179,
     'L1_xattn_bq': 8.0,
     'L1_xattn_bk': 8.0,
     'L1_xattn_bv': 8.0,
     'L1_xattn_bo': 8.0,
     'L1_ffn_router_w': 8.0,
     'L1_ffn_w0_kernel': 8.0,
     'L1_ffn_w1_kernel': 8.0,
     'L1_ffn_wo_kernel': 8.0}
    for name, (base, spread) in spreads.items():
        noise = np.random.default_rng([zlib.crc32(name.encode()), seed]).standard_normal(out[name].shape)
        drawn = base * np.exp(spread * noise) if base else spread * noise
        out[name] = jnp.asarray(drawn.astype(out[name].dtype))
    for name, factor in factors.items():
        out[name] = (out[name] * factor).astype(out[name].dtype)
    return out
```

```python
from contextlib import ExitStack

import concourse.bass as bass
from concourse import mybir

F32 = mybir.dt.float32
BF16 = mybir.dt.bfloat16
U8 = mybir.dt.uint8
ALU = mybir.AluOpType
ACT = mybir.ActivationFunctionType
AX = mybir.AxisListType.X

P = 128
B, S, D = 2, 1024, 256
T = B * S
FT = D // P
CH = 512
NCH = S // CH
TT = S // P
LN_EPS = 1e-5
NEG = -1e30

MATS = {
    "a_wq": (256, 256), "a_wk": (256, 256), "a_wv": (256, 256), "a_wo": (256, 256),
    "a_w1": (256, 1024), "a_w2": (1024, 256), "a_wd": (256, 256),
    "x_wq": (256, 256), "x_wkv": (192, 512), "x_wlkv": (256, 512), "x_wo": (256, 256),
    "f_wf": (256, 256), "f_uf": (256, 256), "f_wi": (256, 256), "f_ui": (256, 256),
    "f_wc": (256, 256), "f_uc": (256, 256), "f_wo": (256, 256), "f_uo": (256, 256),
    "b_wq": (256, 256), "b_wk": (256, 256), "b_wv": (256, 256), "b_wo": (256, 256),
    "y_wq": (256, 256), "y_wk": (192, 256), "y_wv": (192, 256), "y_wo": (256, 256),
    "router": (256, 8),
}
VECS = {
    "a_g1": 2, "a_b1": 2, "a_bo": 2, "a_g2": 2, "a_b2": 2, "a_bf1": 8, "a_bf2": 2, "a_bd": 2,
    "x_gx": 2, "x_bx": 2, "x_gl": 2, "x_bl": 2, "x_gq": 1, "x_gk": 1, "x_bo": 2,
    "f_bf": 2, "f_bi": 2, "f_bc": 2, "f_bo": 2, "f_c0": 2,
    "b_bq": 2, "b_bk": 2, "b_bv": 2, "b_bo": 2,
    "y_bq": 2, "y_bk": 2, "y_bv": 2, "y_bo": 2,
}
KEYS = 64
CF = 192
EXP, HID, CAP, GR = 8, 1368, 64, 8
HT = -(-HID // P)
HLAST = HID - (HT - 1) * P


def mat_offsets():
    off, at = {}, 0
    for name, (rows, cols) in MATS.items():
        tiles = -(-rows // P)
        off[name] = (at, tiles, cols)
        at += tiles * cols
    return off, at


def vec_offsets():
    off, at = {}, 0
    for name, n in VECS.items():
        off[name] = (at, n)
        at += n
    return off, at


class Sig:

    def __init__(self, sem, per_round):
        self.sem, self.per_round, self.round = sem, per_round, 0

    def __call__(self, n):
        return self.sem, self.round * self.per_round + n


class Chip:

    def __init__(self, nc, ctx):
        sb = lambda name, shape, dt=F32: ctx.enter_context(nc.sbuf_tensor(name, shape, dt))
        self.mats, n_mat = mat_offsets()
        self.vecs, n_vec = vec_offsets()
        self.xT = sb("xT", [P, FT, T])
        self.weights = sb("weights_sb", [P, n_mat])
        self.vectors = sb("vectors_sb", [P, n_vec])
        self.ident = sb("ident", [P, P])
        self.mean_w = sb("mean_w", [P, P])
        self.eps = sb("eps", [P, 1])
        self.arena = sb("arena", [P, 6 * FT * S])
        self.ln_s = sb("ln_s", [P, NCH, CH])
        self.ln_d = sb("ln_d", [P, NCH, CH])
        self.ln_r = sb("ln_r", [P, NCH, CH])
        self.psum = [ctx.enter_context(nc.psum_tensor(f"psum{i}", [P, 2 * CH], F32)) for i in range(4)]

    def slot(self, i):
        n = FT * S
        return self.arena[:, i * n:(i + 1) * n].rearrange("p (m t) -> p m t", m=FT)

    def bank(self, i):
        return self.psum[i // 2][:, (i % 2) * CH:(i % 2 + 1) * CH]

    def w(self, name, k, first, n, rows=P):
        at, _, cols = self.mats[name]
        return self.weights[0:rows, at + k * cols + first:at + k * cols + first + n]

    def v(self, name, k):
        return self.vectors[:, self.vecs[name][0] + k:self.vecs[name][0] + k + 1]


def layer_norm_pe(pe, c, s, var_banks=(2, 3)):
    for j in range(NCH):
        pe.wait_ge(*s["ln_sum"](j + 1))
        pe.matmul(c.bank(j), c.mean_w[:], c.ln_s[:, j, :], start=True, stop=True).then_inc(s["ln_mean"].sem)
    for j in range(NCH):
        pe.wait_ge(*s["ln_sq"](j + 1))
        for k in range(FT):
            mm = pe.matmul(c.bank(2 + j), c.mean_w[:], c.slot(3)[:, k, j * CH:(j + 1) * CH],
                           start=(k == 0), stop=(k == FT - 1))
        mm.then_inc(s["ln_var"].sem)


def layer_norm_act(act, c, s, twice):
    for j in range(NCH):
        act.wait_ge(*s["ln_cent"](j + 1))
        act.activation(c.slot(3)[:, :, j * CH:(j + 1) * CH], c.slot(2)[:, :, j * CH:(j + 1) * CH],
                       ACT.Square).then_inc(s["ln_sq"].sem)
    for j in range(NCH):
        act.wait_ge(*s["ln_var"](j + 1))
        act.activation(c.ln_d[:, j, :], c.bank(2 + j), ACT.Ln, bias=c.eps[:, 0:1]).then_inc(s["ln_log"].sem)
    for j in range(NCH):
        act.wait_ge(*s["ln_log"](j + 1))
        act.activation(c.ln_r[:, j, :], c.ln_d[:, j, :], ACT.Exp, scale=-0.5).then_inc(s["ln_rstd"].sem)
    if twice:
        for j in range(NCH):
            act.wait_ge(*s["ln_var2"](j + 1))
            act.activation(c.ln_d[:, j, :], c.ln_s[:, j, :], ACT.Ln, bias=c.eps[:, 0:1]).then_inc(s["ln_log2"].sem)
        for j in range(NCH):
            act.wait_ge(*s["ln_log2"](j + 1))
            act.activation(c.ln_r[:, j, :], c.ln_d[:, j, :], ACT.Exp, scale=-0.5).then_inc(s["ln_rstd2"].sem)


def layer_norm_dve(dve, c, s, x, out, gain, bias, once_out=None):
    for j in range(NCH):
        dve.tensor_tensor(c.ln_s[:, j, :], x(0, j), x(1, j), ALU.add).then_inc(s["ln_sum"].sem)
    for j in range(NCH):
        dve.wait_ge(*s["ln_mean"](j + 1))
        for k in range(FT):
            ins = dve.tensor_tensor(c.slot(2)[:, k, j * CH:(j + 1) * CH], x(k, j), c.bank(j), ALU.subtract)
        ins.then_inc(s["ln_cent"].sem)
    for j in range(NCH):
        dve.wait_ge(*s["ln_rstd"](j + 1))
        if once_out is None:
            if gain is None:
                for k in range(FT):
                    ins = dve.tensor_tensor(out(k, j), c.slot(2)[:, k, j * CH:(j + 1) * CH], c.ln_r[:, j, :], ALU.mult)
                ins.then_inc(s["ln_out"].sem)
            else:
                for k in range(FT):
                    ins = dve.scalar_tensor_tensor(out=out(k, j), in0=c.slot(2)[:, k, j * CH:(j + 1) * CH],
                                                   scalar=gain(k), in1=c.ln_r[:, j, :], op0=ALU.mult, op1=ALU.mult)
                ins.then_inc(s["ln_scaled"].sem)
                dve.wait_ge(*s["ln_scaled"](j + 1))
                for k in range(FT):
                    ins = dve.tensor_scalar(out(k, j), out(k, j), bias(k), None, ALU.add)
                ins.then_inc(s["ln_out"].sem)
        else:
            dve.tensor_tensor(c.ln_s[:, j, :], c.bank(2 + j), c.ln_r[:, j, :], ALU.mult).then_inc(s["ln_vr"].sem)
            for k in range(FT):
                dve.tensor_tensor(once_out(k, j), c.slot(2)[:, k, j * CH:(j + 1) * CH], c.ln_r[:, j, :], ALU.mult)
            dve.wait_ge(*s["ln_vr"](j + 1))
            dve.tensor_tensor(c.ln_s[:, j, :], c.ln_s[:, j, :], c.ln_r[:, j, :], ALU.mult).then_inc(s["ln_var2"].sem)
    if once_out is not None:
        for j in range(NCH):
            dve.wait_ge(*s["ln_rstd2"](j + 1))
            for k in range(FT):
                if gain is None:
                    ins = dve.tensor_tensor(out(k, j), once_out(k, j), c.ln_r[:, j, :], ALU.mult)
                else:
                    ins = dve.scalar_tensor_tensor(out=out(k, j), in0=once_out(k, j), scalar=gain(k),
                                                   in1=c.ln_r[:, j, :], op0=ALU.mult, op1=ALU.mult)
            ins.then_inc(s["ln_scaled"].sem)
            dve.wait_ge(*s["ln_scaled"](j + 1))
            for k in range(FT):
                ins = dve.tensor_scalar(out(k, j), out(k, j), bias(k), None, ALU.add)
            ins.then_inc(s["ln_out"].sem)


LN_SIGNALS = ["ln_sum", "ln_mean", "ln_cent", "ln_sq", "ln_var", "ln_log", "ln_rstd", "ln_vr", "ln_var2",
              "ln_log2", "ln_rstd2", "ln_scaled", "ln_out"]


def clear_signals(nc, *groups, also=()):
    with nc.Block() as block:

        @block.gpsimd
        def _(pool):
            for sem in [sig.sem for group in groups for sig in group.values()] + list(also):
                pool.sem_clear(sem)


def signals(nc, ctx, layer, counts):
    return {name: Sig(ctx.enter_context(nc.semaphore(f"{layer}_{name}")), n) for name, n in counts.items()}


def set_round(b, *groups):
    for group in groups:
        for sig in group.values():
            sig.round = b


def linear_attention_layer(nc, c):
    H, DH = 4, 64
    SCALE = float(DH) ** -0.25
    with ExitStack() as ctx:
        ln_n = {name: NCH for name in LN_SIGNALS}
        s = signals(nc, ctx, "a", dict(
            ln_n, k_proj=4, k_max=4, k_shift=1, k_max_all=1, k_added=1, k_inv=1, zeroed=1, k_exp=4, k_turned=4, k_copied=4, v_proj=4, v_copied=4,
            q_proj=4, q_max=4, q_shift=4, q_exp=4, q_sum=4, q_inv=4, q_norm=4, q_turned=4, q_copied=4,
            ctx_done=1, ctx_copied=1, at_done=4, at_copied=4, o_done=4, y_done=4,
            ff_done=16, ff_gelu=16, f2_done=4, y2_done=4, d_done=4, x_done=4))
        s2 = signals(nc, ctx, "a2", ln_n)
        sb = lambda name, shape: ctx.enter_context(nc.sbuf_tensor(name, shape, F32))
        k_mx = sb("a_k_mx", [P, FT, NCH])
        k_m = sb("a_k_m", [P, FT])
        k_s = sb("a_k_s", [P, FT, NCH])
        k_r = sb("a_k_r", [P, FT])
        q_m = sb("a_q_m", [P, 4, 8])
        q_s = sb("a_q_s", [P, 4, 8])
        context = sb("a_context", [P, FT, P])
        h1, h2, ek, v, ekt, qn = (c.slot(i) for i in range(6))
        v_t = v.rearrange("p a n -> p (a n)").rearrange("p (t n) -> p t n", t=TT)
        ekt_t = ekt.rearrange("p a n -> p (a n)").rearrange("p (t n) -> p t n", t=TT)
        q_t = qn.rearrange("p a n -> p (a n)").rearrange("p (u n) -> p u n", u=4)
        qt, at = c.slot(2), c.slot(5)
        y = h1
        hid = [c.arena[:, (2 + 2 * j) * 2048:(4 + 2 * j) * 2048].rearrange("p (f n) -> p f n", f=8) for j in range(NCH)]
        with nc.Fori(0, B) as b:
            set_round(b, s, s2)
            x = lambda k, j: c.xT[:, k, bass.ds(b * S + j * CH, CH)]
            col = lambda t: (lambda k, j: t[:, k, j * CH:(j + 1) * CH])
            with nc.Block() as block:

                @block.gpsimd
                def _(pool):
                    pool.memset(context[:], 0.0).then_inc(s["zeroed"].sem)

                @block.tensor
                def _(pe):
                    layer_norm_pe(pe, c, s)
                    pe.wait_ge(*s["ln_out"](NCH))
                    for m in range(FT):
                        for j in range(NCH):
                            for k in range(FT):
                                mm = pe.matmul(c.bank(2 * m + j), c.w("a_wk", k, m * P, P), h2[:, k, j * CH:(j + 1) * CH],
                                               start=(k == 0), stop=(k == 1))
                            mm.then_inc(s["k_proj"].sem)
                    for u in range(4):
                        for t in (0, 1):
                            for k in range(FT):
                                mm = pe.matmul(c.bank(4 + u)[:, t * D:(t + 1) * D], h2[:, k, (2 * u + t) * P:(2 * u + t + 1) * P],
                                               c.w("a_wv", k, 0, D), start=(k == 0), stop=(k == 1))
                        mm.then_inc(s["v_proj"].sem)
                    for u in range(4):
                        pe.wait_ge(*s["v_copied"](u + 1))
                        for t in (0, 1):
                            for k in range(FT):
                                mm = pe.matmul(c.bank(4 + u)[:, t * D:(t + 1) * D], h2[:, k, (2 * u + t) * P:(2 * u + t + 1) * P],
                                               c.w("a_wq", k, 0, D), start=(k == 0), stop=(k == 1))
                        mm.then_inc(s["q_proj"].sem)
                    pe.wait_ge(*s["k_exp"](4))
                    for u in range(4):
                        for t in (0, 1):
                            for m in range(FT):
                                mm = pe.transpose(c.bank(u)[:, t * D + m * P:t * D + (m + 1) * P],
                                                  ek[:, m, (2 * u + t) * P:(2 * u + t + 1) * P], c.ident[:])
                        mm.then_inc(s["k_turned"].sem)
                    pe.wait_ge(*s["k_copied"](4))
                    for m in range(FT):
                        for t in range(TT):
                            mm = pe.matmul(c.bank(0)[:, m * P:(m + 1) * P], ekt_t[:, t, m * P:(m + 1) * P],
                                           v_t[:, t, m * P:(m + 1) * P], start=(t == 0), stop=(t == TT - 1))
                    mm.then_inc(s["ctx_done"].sem)
                    for u in range(4):
                        pe.wait_ge(*s["q_norm"](u + 1))
                        for m in range(FT):
                            for t in (0, 1):
                                mm = pe.transpose(c.bank(4 + u)[:, m * D + t * P:m * D + (t + 1) * P],
                                                  q_t[:, u, t * D + m * P:t * D + (m + 1) * P], c.ident[:])
                        mm.then_inc(s["q_turned"].sem)
                    pe.wait_ge(*s["ctx_copied"](1))
                    pe.wait_ge(*s["q_copied"](4))
                    for m in range(FT):
                        for j in range(NCH):
                            pe.matmul(c.bank(2 * m + j), context[:, m, :], qt[:, m, j * CH:(j + 1) * CH],
                                      start=True, stop=True).then_inc(s["at_done"].sem)
                    pe.wait_ge(*s["at_copied"](4))
                    for m in range(FT):
                        for j in range(NCH):
                            for k in range(FT):
                                mm = pe.matmul(c.bank(4 + 2 * m + j), c.w("a_wo", k, m * P, P), at[:, k, j * CH:(j + 1) * CH],
                                               start=(k == 0), stop=(k == 1))
                            mm.then_inc(s["o_done"].sem)
                    layer_norm_pe(pe, c, s2)
                    n = 0
                    for j in range(NCH):
                        pe.wait_ge(*s2["ln_out"](NCH))
                        for f in range(8):
                            if n >= 4:
                                pe.wait_ge(*s["ff_gelu"](n - 3))
                            for k in range(FT):
                                mm = pe.matmul(c.bank(4 + n % 4), c.w("a_w1", k, f * P, P), h2[:, k, j * CH:(j + 1) * CH],
                                               start=(k == 0), stop=(k == 1))
                            mm.then_inc(s["ff_done"].sem)
                            n += 1
                    for j in range(NCH):
                        pe.wait_ge(*s["ff_gelu"](8 * (j + 1)))
                        for m in range(FT):
                            for f in range(8):
                                mm = pe.matmul(c.bank(2 * m + j), c.w("a_w2", f, m * P, P), hid[j][:, f, :],
                                               start=(f == 0), stop=(f == 7))
                            mm.then_inc(s["f2_done"].sem)
                    pe.wait_ge(*s["ff_gelu"](16))
                    for j in range(NCH):
                        pe.wait_ge(*s["y2_done"](2 * (j + 1)))
                        for m in range(FT):
                            for k in range(FT):
                                mm = pe.matmul(c.bank(4 + 2 * m + j), c.w("a_wd", k, m * P, P), y[:, k, j * CH:(j + 1) * CH],
                                               start=(k == 0), stop=(k == 1))
                            mm.then_inc(s["d_done"].sem)

                @block.scalar
                def _(act):
                    layer_norm_act(act, c, s, True)
                    act.wait_ge(*s["k_shift"](1))
                    for m in range(FT):
                        for j in range(NCH):
                            act.activation(ek[:, m, j * CH:(j + 1) * CH], c.bank(2 * m + j), ACT.Exp, bias=k_m[:, m:m + 1],
                                           scale=SCALE, accum_out=k_s[:, m, j:j + 1]).then_inc(s["k_exp"].sem)
                    for u in range(4):
                        act.wait_ge(*s["q_shift"](u + 1))
                        act.activation(q_t[:, u, :], q_t[:, u, :], ACT.Exp, scale=SCALE).then_inc(s["q_exp"].sem)
                    for u in range(4):
                        act.wait_ge(*s["k_turned"](u + 1))
                        act.activation(ekt_t[:, 2 * u:2 * u + 2, :].rearrange("p t n -> p (t n)"), c.bank(u), ACT.Copy)\
                           .then_inc(s["k_copied"].sem)
                    for u in range(4):
                        act.wait_ge(*s["q_turned"](u + 1))
                        act.activation(qt[:, :, u * D:(u + 1) * D], c.bank(4 + u).rearrange("p (m n) -> p m n", m=FT),
                                       ACT.Copy).then_inc(s["q_copied"].sem)
                    for m in range(FT):
                        for j in range(NCH):
                            act.wait_ge(*s["at_done"](2 * m + j + 1))
                            act.activation(at[:, m, j * CH:(j + 1) * CH], c.bank(2 * m + j), ACT.Copy)\
                               .then_inc(s["at_copied"].sem)
                    layer_norm_act(act, c, s2, False)
                    n = 0
                    act.wait_ge(*s2["ln_out"](NCH))
                    for j in range(NCH):
                        for f in range(8):
                            act.wait_ge(*s["ff_done"](n + 1))
                            act.activation(hid[j][:, f, :], c.bank(4 + n % 4), ACT.Gelu_apprx_tanh,
                                           bias=c.v("a_bf1", f)).then_inc(s["ff_gelu"].sem)
                            n += 1

                @block.vector
                def _(dve):
                    layer_norm_dve(dve, c, s, x, col(h2), lambda k: c.v("a_g1", k), lambda k: c.v("a_b1", k), col(h1))
                    for m in range(FT):
                        for j in range(NCH):
                            dve.wait_ge(*s["k_proj"](2 * m + j + 1))
                            dve.tensor_reduce(k_mx[:, m, j:j + 1], c.bank(2 * m + j), AX, ALU.max).then_inc(s["k_max"].sem)
                    dve.wait_ge(*s["k_max"](4))
                    dve.tensor_reduce(k_m[:], k_mx[:], AX, ALU.max).then_inc(s["k_max_all"].sem)
                    dve.wait_ge(*s["k_max_all"](1))
                    dve.tensor_scalar(k_m[:], k_m[:], -SCALE, None, ALU.mult).then_inc(s["k_shift"].sem)
                    for u in range(4):
                        dve.wait_ge(*s["v_proj"](u + 1))
                        dve.tensor_copy(v_t[:, 2 * u:2 * u + 2, :].rearrange("p t n -> p (t n)"), c.bank(4 + u))\
                           .then_inc(s["v_copied"].sem)
                    heads = lambda ap: ap.rearrange("p (h d) -> p h d", d=DH)
                    wide = lambda ap: ap.unsqueeze(2).to_broadcast([P, 8, DH])
                    for u in range(4):
                        dve.wait_ge(*s["q_proj"](u + 1))
                        dve.tensor_reduce(q_m[:, u, :], heads(c.bank(4 + u)), AX, ALU.max).then_inc(s["q_max"].sem)
                        dve.wait_ge(*s["q_max"](u + 1))
                        dve.tensor_tensor(heads(q_t[:, u, :]), heads(c.bank(4 + u)), wide(q_m[:, u, :]), ALU.subtract)\
                           .then_inc(s["q_shift"].sem)
                    for u in range(4):
                        dve.wait_ge(*s["q_exp"](u + 1))
                        dve.tensor_reduce(q_s[:, u, :], heads(q_t[:, u, :]), AX, ALU.add).then_inc(s["q_sum"].sem)
                        dve.wait_ge(*s["q_sum"](u + 1))
                        dve.reciprocal(q_s[:, u, :], q_s[:, u, :]).then_inc(s["q_inv"].sem)
                        dve.wait_ge(*s["q_inv"](u + 1))
                        dve.tensor_tensor(heads(q_t[:, u, :]), heads(q_t[:, u, :]), wide(q_s[:, u, :]), ALU.mult)\
                           .then_inc(s["q_norm"].sem)
                    dve.wait_ge(*s["k_exp"](4))
                    dve.tensor_tensor(k_r[:], k_s[:, :, 0], k_s[:, :, 1], ALU.add).then_inc(s["k_added"].sem)
                    dve.wait_ge(*s["k_added"](1))
                    dve.reciprocal(k_r[:], k_r[:]).then_inc(s["k_inv"].sem)
                    dve.wait_ge(*s["k_inv"](1))
                    dve.wait_ge(*s["zeroed"](1))
                    dve.wait_ge(*s["ctx_done"](1))
                    for m in range(FT):
                        for h in (0, DH):
                            ins = dve.tensor_scalar(context[h:h + DH, m, h:h + DH], c.bank(0)[h:h + DH, m * P + h:m * P + h + DH],
                                                    k_r[h:h + DH, m:m + 1], None, ALU.mult)
                    ins.then_inc(s["ctx_copied"].sem)
                    for m in range(FT):
                        for j in range(NCH):
                            dve.wait_ge(*s["o_done"](2 * m + j + 1))
                            dve.scalar_tensor_tensor(out=y[:, m, j * CH:(j + 1) * CH], in0=c.bank(4 + 2 * m + j),
                                                     scalar=c.v("a_bo", m), in1=h1[:, m, j * CH:(j + 1) * CH],
                                                     op0=ALU.add, op1=ALU.add).then_inc(s["y_done"].sem)
                    dve.wait_ge(*s["y_done"](4))
                    layer_norm_dve(dve, c, s2, col(y), col(h2), lambda k: c.v("a_g2", k), lambda k: c.v("a_b2", k))
                    for j in range(NCH):
                        for m in range(FT):
                            dve.wait_ge(*s["f2_done"](2 * j + m + 1))
                            dve.scalar_tensor_tensor(out=y[:, m, j * CH:(j + 1) * CH], in0=c.bank(2 * m + j),
                                                     scalar=c.v("a_bf2", m), in1=y[:, m, j * CH:(j + 1) * CH],
                                                     op0=ALU.add, op1=ALU.add).then_inc(s["y2_done"].sem)
                    for j in range(NCH):
                        for m in range(FT):
                            dve.wait_ge(*s["d_done"](2 * j + m + 1))
                            dve.scalar_tensor_tensor(out=x(m, j), in0=c.bank(4 + 2 * m + j), scalar=c.v("a_bd", m),
                                                     in1=x(m, j), op0=ALU.add, op1=ALU.add).then_inc(s["x_done"].sem)
        clear_signals(nc, s, s2)


def cross_attention_layer(nc, c):
    H, DH = 4, 64
    SCALE = DH ** -0.5
    HP = H // FT
    NB = TT + 1
    UNITS = TT * H
    TILES = 3 * UNITS + 2 * TT
    KC = [P, CF - P]
    with ExitStack() as ctx:
        ln_n = {name: NCH for name in LN_SIGNALS}
        s = signals(nc, ctx, "x", dict(
            ln_n, q_proj=4, k_proj=4, v_proj=4, raw=8, square=8, ms=8, ms_max=8, ms_log=8, inv=8, scaled=8, v_copied=4,
            ctx_v=1, scores=UNITS, shift=UNITS, ctx_max=TT, row_max=UNITS, expd=UNITS,
            padded=1, turned=TILES, copied=TILES, av=UNITS, den=TT, den_inv=TT, normed=TT, o_done=4, x_done=4))
        g = signals(nc, ctx, "xc", dict(load=1, made=4, sum_s=1, mean=1, cent=1, sq=1, var=1, log=1, rstd=1, scaled=1,
                                        out=1, k=1, v=1, raw=1, square=1, ms=1, ms_max=1, ms_log=1, inv=1, kn=1, vc=1,
                                        mask=1, mask2=1))
        set_round(0, g)
        sb = lambda name, shape, dt=F32: ctx.enter_context(nc.sbuf_tensor(name, shape, dt))
        same_head = sb("x_same_head", [P, P])
        ctx_mean = sb("x_ctx_mean", [P, P])
        mask_u8 = sb("x_mask_u8", [P, B * KEYS], U8)
        mask_add = sb("x_mask_add", [P, B * KEYS])
        cx = sb("x_cx", [P, 2, B * KEYS])
        cs = sb("x_cs", [P, 2, B * KEYS])
        cr = sb("x_cr", [P, 2, B * KEYS])
        k_ctx = sb("x_k_ctx", [P, FT, B * KEYS])
        v_ctx_all = sb("x_v_ctx_all", [KEYS, B, D])
        k_ctx_now = sb("x_k_ctx_now", [P, FT, P])
        mask_sel = sb("x_mask_sel", [P, H * KEYS])
        v_ctx = sb("x_v_ctx", [KEYS, D])
        turned = [sb(f"x_turned{i}", [P, NB, P]) for i in range(2)]
        o = sb("x_o", [P, 2, D])
        ctx_s = sb("x_ctx_s", [P, 2, H * KEYS])
        mxc = sb("x_mxc", [P, 2, H])
        mx = sb("x_mx", [P, 2])
        nm = sb("x_nm", [P, 2])
        rs = sb("x_rs", [P, 2, H, 2])
        rr = sb("x_rr", [P, 2, H])
        ln, qt, scr, inv, kt, v = c.slot(0), c.slot(1), c.slot(2), c.slot(3), c.slot(4), c.slot(5)
        ot = c.slot(0)
        v_t = v.rearrange("p a n -> p (a n)").rearrange("p (t n) -> p t n", t=TT)
        probs = [c.arena[:, (2 + i) * 2048:(2 + i) * 2048 + NB * P] for i in range(2)]

        with nc.Block() as block:

            @block.sync
            def _(sync):
                sync.dma_start(cx[:], c.ctx_t).then_inc(g["load"].sem, 16)
                sync.dma_start(mask_u8[:], c.mask[0, :].partition_broadcast(P)).then_inc(g["load"].sem, 16)

            @block.gpsimd
            def _(pool):
                pool.memset(ctx_mean[:], 1.0 / CF)
                pool.memset(k_ctx_now[:], 0.0)
                pool.memset(same_head[:], 0.0).then_inc(g["made"].sem)
                pool.wait_ge(*g["made"](1))
                pool.memset(same_head[0:DH, 0:DH], 1.0 / DH)
                pool.memset(same_head[DH:P, DH:P], 1.0 / DH).then_inc(g["made"].sem)

            @block.tensor
            def _(pe):
                pe.wait_ge(*g["made"](2))
                pe.wait_ge(g["load"].sem, 32)
                for k in range(2):
                    mm = pe.matmul(c.bank(0)[:, 0:P], ctx_mean[0:KC[k], :], cx[0:KC[k], k, :], start=(k == 0), stop=(k == 1))
                mm.then_inc(g["mean"].sem)
                pe.wait_ge(*g["sq"](1))
                for k in range(2):
                    mm = pe.matmul(c.bank(1)[:, 0:P], ctx_mean[0:KC[k], :], cs[0:KC[k], k, :], start=(k == 0), stop=(k == 1))
                mm.then_inc(g["var"].sem)
                pe.wait_ge(*g["out"](1))
                for m in range(FT):
                    for k in range(2):
                        mm = pe.matmul(c.bank(2)[:, m * P:(m + 1) * P], c.w("x_wkv", k, m * P, P, KC[k]), cx[0:KC[k], k, :],
                                       start=(k == 0), stop=(k == 1))
                mm.then_inc(g["k"].sem)
                for b in range(B):
                    for k in range(2):
                        mm = pe.matmul(c.bank(3)[0:KEYS, b * D:(b + 1) * D], cx[0:KC[k], k, b * KEYS:(b + 1) * KEYS],
                                       c.w("x_wkv", k, D, D, KC[k]), start=(k == 0), stop=(k == 1))
                mm.then_inc(g["v"].sem)
                pe.wait_ge(*g["square"](1))
                pe.matmul(c.bank(4)[:, 0:D], same_head[:], cs[:].rearrange("p m n -> p (m n)"), start=True, stop=True)\
                  .then_inc(g["ms"].sem)

            @block.scalar
            def _(act):
                act.wait_ge(*g["cent"](1))
                for k in range(2):
                    ins = act.activation(cs[0:KC[k], k, :], cx[0:KC[k], k, :], ACT.Square)
                ins.then_inc(g["sq"].sem)
                act.wait_ge(*g["var"](1))
                act.activation(cr[:, 0, :], c.bank(1)[:, 0:P], ACT.Ln, bias=c.eps[:, 0:1]).then_inc(g["log"].sem)
                act.wait_ge(*g["log"](1))
                act.activation(cr[:, 1, :], cr[:, 0, :], ACT.Exp, scale=-0.5).then_inc(g["rstd"].sem)
                act.wait_ge(*g["k"](1))
                act.activation(k_ctx[:].rearrange("p m n -> p (m n)"), c.bank(2)[:, 0:D], ACT.Copy).then_inc(g["raw"].sem)
                act.activation(cs[:].rearrange("p m n -> p (m n)"), c.bank(2)[:, 0:D], ACT.Square).then_inc(g["square"].sem)
                act.wait_ge(*g["ms_max"](1))
                act.activation(cr[:], cr[:], ACT.Ln).then_inc(g["ms_log"].sem)
                act.wait_ge(*g["ms_log"](1))
                act.activation(cr[:], cr[:], ACT.Exp, scale=-0.5).then_inc(g["inv"].sem)

            @block.vector
            def _(dve):
                dve.wait_ge(*g["mean"](1))
                for k in range(2):
                    ins = dve.tensor_tensor(cx[0:KC[k], k, :], cx[0:KC[k], k, :], c.bank(0)[0:KC[k], 0:P], ALU.subtract)
                ins.then_inc(g["cent"].sem)
                dve.wait_ge(*g["rstd"](1))
                for k in range(2):
                    ins = dve.scalar_tensor_tensor(out=cx[0:KC[k], k, :], in0=cx[0:KC[k], k, :], scalar=c.v("x_gx", k)[0:KC[k], :],
                                                   in1=cr[0:KC[k], 1, :], op0=ALU.mult, op1=ALU.mult)
                ins.then_inc(g["scaled"].sem)
                dve.wait_ge(*g["scaled"](1))
                for k in range(2):
                    ins = dve.tensor_scalar(cx[0:KC[k], k, :], cx[0:KC[k], k, :], c.v("x_bx", k)[0:KC[k], :], None, ALU.add)
                ins.then_inc(g["out"].sem)
                dve.tensor_copy(mask_add[:], mask_u8[:]).then_inc(g["mask"].sem)
                dve.wait_ge(*g["mask"](1))
                dve.tensor_scalar(mask_add[:], mask_add[:], -1.0, -NEG, ALU.add, ALU.mult).then_inc(g["mask2"].sem)
                dve.wait_ge(*g["v"](1))
                dve.tensor_copy(v_ctx_all[:].rearrange("p b n -> p (b n)"), c.bank(3)[0:KEYS, :]).then_inc(g["vc"].sem)
                dve.wait_ge(*g["ms"](1))
                dve.tensor_scalar(cr[:].rearrange("p m n -> p (m n)"), c.bank(4)[:, 0:D], 1e-16, None, ALU.max)\
                   .then_inc(g["ms_max"].sem)
                dve.wait_ge(*g["inv"](1))
                dve.scalar_tensor_tensor(out=k_ctx[:], in0=k_ctx[:], scalar=c.v("x_gk", 0), in1=cr[:],
                                         op0=ALU.mult, op1=ALU.mult).then_inc(g["kn"].sem)

        with nc.Fori(0, B) as b:
            set_round(b, s)
            x = lambda k, j: c.xT[:, k, bass.ds(b * S + j * CH, CH)]
            col = lambda t: (lambda k, j: t[:, k, j * CH:(j + 1) * CH])
            order = [("c", 0, 0)]
            for u in range(UNITS + 2):
                if (u + 1) % H == 0 and u + 1 < UNITS:
                    order.append(("c", (u + 1) // H, 0))
                if u < UNITS:
                    order += [("p", u, 0), ("p", u, 1)]
                if u >= 2 and (u - 2) % H == H - 1:
                    order.append(("o", (u - 2) // H, 0))
                if u < UNITS:
                    order.append(("p", u, 2))
            nth = {what: n for n, what in enumerate(order)}
            assert len(order) == TILES
            turn_bank = lambda what: c.bank(5 + nth[what] % 2)
            score = lambda u: c.psum[u % 2]
            out_bank = lambda qi: c.bank(4 if qi % 2 else 7)
            with nc.Block() as block:

                @block.tensor
                def _(pe):
                    layer_norm_pe(pe, c, s)
                    pe.wait_ge(*s["ln_out"](NCH))
                    for name, base, first, done in (("x_wq", 0, 0, s["q_proj"]), ("x_wlkv", 4, 0, s["k_proj"])):
                        for m in range(FT):
                            for j in range(NCH):
                                for k in range(FT):
                                    mm = pe.matmul(c.bank(base + 2 * m + j), c.w(name, k, m * P, P),
                                                   ln[:, k, j * CH:(j + 1) * CH], start=(k == 0), stop=(k == 1))
                                mm.then_inc(done.sem)
                    for n in range(8):
                        pe.wait_ge(*s["square"](n + 1))
                        pe.wait_ge(*s["raw"](n + 1))
                        m, j = (n % 4) // 2, n % 2
                        pe.matmul(c.bank(n), same_head[:], scr[:, m, j * CH:(j + 1) * CH] if n < 4 else
                                  v[:, m, j * CH:(j + 1) * CH], start=True, stop=True).then_inc(s["ms"].sem)
                    for t2 in range(4):
                        if t2 == 0:
                            pe.wait_ge(*s["ms_max"](8))
                        for t in (0, 1):
                            for k in range(FT):
                                mm = pe.matmul(c.bank(t2)[:, t * D:(t + 1) * D], ln[:, k, (2 * t2 + t) * P:(2 * t2 + t + 1) * P],
                                               c.w("x_wlkv", k, D, D), start=(k == 0), stop=(k == 1))
                        mm.then_inc(s["v_proj"].sem)

                    def scores(u):
                        qi, h = divmod(u, H)
                        m, at = h // HP, (h % HP) * DH
                        if u == 0:
                            pe.wait_ge(*s["scaled"](8))
                            pe.wait_ge(*s["v_copied"](4))
                        if h == 0:
                            n = nth["c", qi, 0]
                            half = turn_bank(("c", qi, 0))[:, 0:D]
                            if n >= 2:
                                pe.wait_ge(*s["copied"](n - 1))
                            pe.matmul(half, c.ident[:], mask_sel[:], start=True, stop=False)
                            for i in range(FT):
                                mm = pe.matmul(half[:, i * P:(i + 1) * P], qt[:, i, qi * P:(qi + 1) * P],
                                               k_ctx_now[:, i, :], start=False, stop=(i == 1))
                            mm.then_inc(s["turned"].sem)
                        if u >= 2:
                            pe.wait_ge(*s["expd"](u - 1))
                        for j in range(NCH):
                            mm = pe.matmul(score(u)[:, j * CH:(j + 1) * CH], qt[at:at + DH, m, qi * P:(qi + 1) * P],
                                           kt[at:at + DH, m, j * CH:(j + 1) * CH], start=True, stop=True)
                        mm.then_inc(s["scores"].sem)

                    def turn(u, i):
                        n = nth["p", u, i]
                        pe.wait_ge(*s["expd"](u + 1))
                        if u == 0:
                            pe.wait_ge(*s["padded"](1))
                        if n >= 2:
                            pe.wait_ge(*s["copied"](n - 1))
                        blocks = range(4 * i, min(4 * i + 4, NB))
                        for kb in blocks:
                            mm = pe.transpose(turn_bank(("p", u, i))[:, (kb % 4) * P:(kb % 4 + 1) * P],
                                              probs[u % 2][:, kb * P:(kb + 1) * P], c.ident[:])
                        mm.then_inc(s["turned"].sem)

                    def turn_outputs(qi):
                        n = nth["o", qi, 0]
                        pe.wait_ge(*s["normed"](qi + 1))
                        pe.wait_ge(*s["copied"](n - 1))
                        for m in range(FT):
                            mm = pe.transpose(turn_bank(("o", qi, 0))[:, m * P:(m + 1) * P], o[:, qi % 2, m * P:(m + 1) * P], c.ident[:])
                        mm.then_inc(s["turned"].sem)

                    def values(u):
                        qi, h = divmod(u, H)
                        pe.wait_ge(*s["copied"](nth["p", u, 2] + 1))
                        if h == 0 and qi >= 2:
                            pe.wait_ge(*s["normed"](qi - 1))
                        out = out_bank(qi)[:, h * DH:(h + 1) * DH]
                        for kb in range(TT):
                            pe.matmul(out, turned[u % 2][:, kb, :], v_t[:, kb, h * DH:(h + 1) * DH], start=(kb == 0), stop=False)
                        pe.matmul(out, turned[u % 2][0:KEYS, TT, :], v_ctx[:, h * DH:(h + 1) * DH], start=False, stop=True)\
                          .then_inc(s["av"].sem)

                    pe.wait_ge(*s["ctx_v"](1))
                    scores(0)
                    for u in range(UNITS + 2):
                        if u + 1 < UNITS:
                            scores(u + 1)
                        if u < UNITS:
                            turn(u, 0)
                            turn(u, 1)
                        if u >= 2 and (u - 2) % H == H - 1:
                            turn_outputs((u - 2) // H)
                        if 1 <= u <= UNITS:
                            values(u - 1)
                        if u < UNITS:
                            turn(u, 2)
                    pe.wait_ge(*s["copied"](TILES))
                    for m in range(FT):
                        for j in range(NCH):
                            for k in range(FT):
                                mm = pe.matmul(c.bank(2 * m + j), c.w("x_wo", k, m * P, P), ot[:, k, j * CH:(j + 1) * CH],
                                               start=(k == 0), stop=(k == 1))
                            mm.then_inc(s["o_done"].sem)

                @block.scalar
                def _(act):
                    layer_norm_act(act, c, s, True)
                    for n in range(8):
                        m, j = (n % 4) // 2, n % 2
                        done = s["q_proj"] if n < 4 else s["k_proj"]
                        act.wait_ge(*done(n % 4 + 1))
                        if n == 0:
                            act.wait_ge(*s["ln_out"](NCH))
                        act.activation((qt if n < 4 else kt)[:, m, j * CH:(j + 1) * CH], c.bank(n), ACT.Copy).then_inc(s["raw"].sem)
                        act.activation((scr if n < 4 else v)[:, m, j * CH:(j + 1) * CH], c.bank(n), ACT.Square)\
                           .then_inc(s["square"].sem)
                    for f, ready, done in ((ACT.Ln, s["ms_max"], s["ms_log"]), (ACT.Exp, s["ms_log"], s["inv"])):
                        for n in range(8):
                            m, j = (n % 4) // 2, n % 2
                            act.wait_ge(*ready(n + 1))
                            half = (inv if n < 4 else scr)[:, m, j * CH:(j + 1) * CH]
                            act.activation(half, half, f, scale=1.0 if f == ACT.Ln else -0.5).then_inc(done.sem)

                    def exps(u):
                        qi, h = divmod(u, H)
                        act.wait_ge(*s["shift"](u + 1))
                        if u == 0:
                            act.wait_ge(*s["scaled"](8))
                        if u >= 2:
                            act.wait_ge(*s["turned"](nth["p", u - 2, 2] + 1))
                        act.activation(probs[u % 2][:, 0:S], score(u)[:], ACT.Exp, bias=nm[:, u % 2:u % 2 + 1], scale=SCALE,
                                       accum_out=rs[:, qi % 2, h, 0:1])
                        act.activation(probs[u % 2][:, S:S + KEYS], ctx_s[:, qi % 2, h * KEYS:(h + 1) * KEYS],
                                       ACT.Exp, bias=nm[:, u % 2:u % 2 + 1], scale=SCALE,
                                       accum_out=rs[:, qi % 2, h, 1:2]).then_inc(s["expd"].sem)

                    for u in range(UNITS):
                        exps(u)

                @block.vector
                def _(dve):
                    layer_norm_dve(dve, c, s, x, col(ln), lambda k: c.v("x_gl", k), lambda k: c.v("x_bl", k), col(qt))
                    for h in range(HP):
                        dve.tensor_copy(k_ctx_now[h * DH:(h + 1) * DH, :, h * KEYS:(h + 1) * KEYS],
                                        k_ctx[h * DH:(h + 1) * DH, :, bass.ds(b * KEYS, KEYS)])
                    for h in range(H):
                        dve.tensor_copy(mask_sel[:, h * KEYS:(h + 1) * KEYS], mask_add[:, bass.ds(b * KEYS, KEYS)])
                    dve.tensor_copy(v_ctx[:], v_ctx_all[:].rearrange("p b n -> p (b n)")[:, bass.ds(b * D, D)]).then_inc(s["ctx_v"].sem)
                    for n in range(8):
                        m, j = (n % 4) // 2, n % 2
                        dve.wait_ge(*s["ms"](n + 1))
                        if n == 4:
                            dve.wait_ge(*s["ms"](8))
                        dve.tensor_scalar((inv if n < 4 else scr)[:, m, j * CH:(j + 1) * CH], c.bank(n), 1e-16, None, ALU.max)\
                           .then_inc(s["ms_max"].sem)
                    for t2 in range(4):
                        dve.wait_ge(*s["v_proj"](t2 + 1))
                        dve.tensor_copy(v_t[:, 2 * t2:2 * t2 + 2, :].rearrange("p t n -> p (t n)"), c.bank(t2)).then_inc(s["v_copied"].sem)
                    for n in range(8):
                        m, j = (n % 4) // 2, n % 2
                        dve.wait_ge(*s["inv"](n + 1))
                        t = (qt if n < 4 else kt)[:, m, j * CH:(j + 1) * CH]
                        dve.scalar_tensor_tensor(out=t, in0=t, scalar=c.v("x_gq" if n < 4 else "x_gk", 0),
                                                 in1=(inv if n < 4 else scr)[:, m, j * CH:(j + 1) * CH],
                                                 op0=ALU.mult, op1=ALU.mult).then_inc(s["scaled"].sem)

                    def shift(u):
                        qi, h = divmod(u, H)
                        if h == 0:
                            dve.wait_ge(*s["turned"](nth["c", qi, 0] + 1))
                            if qi >= 2:
                                dve.wait_ge(*s["expd"](H * (qi - 1)))
                            bank = turn_bank(("c", qi, 0))[:, 0:D]
                            dve.tensor_reduce(mxc[:, qi % 2, :], bank.rearrange("p (h n) -> p h n", h=H), AX, ALU.max)\
                               .then_inc(s["ctx_max"].sem)
                            dve.tensor_copy(ctx_s[:, qi % 2, :], bank).then_inc(s["copied"].sem)
                            dve.wait_ge(*s["ctx_max"](qi + 1))
                        dve.wait_ge(*s["scores"](u + 1))
                        dve.tensor_reduce(mx[:, u % 2:u % 2 + 1], score(u)[:], AX, ALU.max).then_inc(s["row_max"].sem)
                        dve.wait_ge(*s["row_max"](u + 1))
                        dve.tensor_scalar(nm[:, u % 2:u % 2 + 1], mx[:, u % 2:u % 2 + 1], mxc[:, qi % 2, h:h + 1], -SCALE,
                                          ALU.max, ALU.mult).then_inc(s["shift"].sem)

                    def copy_turned(u, i):
                        n = nth["p", u, i]
                        dve.wait_ge(*s["turned"](n + 1))
                        if u >= 2 and i == 0:
                            dve.wait_ge(*s["av"](u - 1))
                        blocks = range(4 * i, min(4 * i + 4, NB))
                        rows = P if i < 2 else KEYS
                        dve.tensor_copy(turned[u % 2][0:rows, blocks[0]:blocks[-1] + 1, :].rearrange("p k n -> p (k n)"),
                                        turn_bank(("p", u, i))[0:rows, 0:len(blocks) * P]).then_inc(s["copied"].sem)

                    def copy_outputs(qi):
                        n = nth["o", qi, 0]
                        dve.wait_ge(*s["turned"](n + 1))
                        dve.tensor_copy(ot[:, :, qi * P:(qi + 1) * P], turn_bank(("o", qi, 0))[:, 0:D].rearrange("p (m n) -> p m n", m=FT))\
                           .then_inc(s["copied"].sem)

                    def norm(qi):
                        dve.wait_ge(*s["av"](H * (qi + 1)))
                        dve.wait_ge(*s["expd"](H * (qi + 1)))
                        dve.tensor_reduce(rr[:, qi % 2, :], rs[:, qi % 2, :, :], AX, ALU.add).then_inc(s["den"].sem)
                        dve.wait_ge(*s["den"](qi + 1))
                        dve.reciprocal(rr[:, qi % 2, :], rr[:, qi % 2, :]).then_inc(s["den_inv"].sem)
                        dve.wait_ge(*s["den_inv"](qi + 1))
                        dve.tensor_tensor(o[:, qi % 2, :].rearrange("p (h d) -> p h d", h=H),
                                          out_bank(qi)[:, 0:D].rearrange("p (h d) -> p h d", h=H),
                                          rr[:, qi % 2, :].unsqueeze(2).to_broadcast([P, H, DH]), ALU.mult).then_inc(s["normed"].sem)

                    dve.wait_ge(*s["scaled"](8))
                    for i in range(2):
                        ins = dve.memset(probs[i][:, S + KEYS:], 0.0)
                    ins.then_inc(s["padded"].sem)
                    shift(0)
                    for u in range(UNITS + 2):
                        if u + 1 < UNITS:
                            shift(u + 1)
                        if u < UNITS:
                            copy_turned(u, 0)
                            copy_turned(u, 1)
                        if u >= 2 and (u - 2) % H == H - 1:
                            copy_outputs((u - 2) // H)
                        if 1 <= u <= UNITS and (u - 1) % H == H - 1:
                            norm((u - 1) // H)
                        if u < UNITS:
                            copy_turned(u, 2)
                    for m in range(FT):
                        for j in range(NCH):
                            dve.wait_ge(*s["o_done"](2 * m + j + 1))
                            dve.scalar_tensor_tensor(out=x(m, j), in0=c.bank(2 * m + j), scalar=c.v("x_bo", m),
                                                     in1=x(m, j), op0=ALU.add, op1=ALU.add).then_inc(s["x_done"].sem)
        clear_signals(nc, s, g)


def gated_recurrence_layer(nc, c):
    GATES = (("f_wf", "f_uf", "f_bf"), ("f_wi", "f_ui", "f_bi"), ("f_wc", "f_uc", "f_bc"))
    NG = len(GATES)
    N = NG * FT * NCH
    with ExitStack() as ctx:
        s = signals(nc, ctx, "f", dict({name: NCH for name in LN_SIGNALS}, gate_in=N, gate=N, fed=4, kept=4, cell=4))
        s2 = signals(nc, ctx, "f2", dict(o_done=4, tanh=4, x_done=4))
        first = ctx.enter_context(nc.semaphore("f_first_cell"))
        xn_all = ctx.enter_context(nc.sbuf_tensor("f_xn_all", [P, FT, T], F32))
        xn, cell, fed = c.slot(0), c.slot(1), c.slot(5)
        gates = [c.slot(i) for i in (2, 3, 4)]
        col = lambda t: (lambda k, j: t[:, k, j * CH:(j + 1) * CH])
        with nc.Block() as block:

            @block.vector
            def _(dve):
                dve.memset(cell, 0.0).then_inc(first)
                dve.wait_ge(first, 1)
                for k in range(FT):
                    dve.tensor_scalar(cell[:, k, :], cell[:, k, :], c.v("f_c0", k), None, ALU.add)

        with nc.Fori(0, B) as b:
            set_round(b, s)
            x = lambda k, j: c.xT[:, k, bass.ds(b * S + j * CH, CH)]
            with nc.Block() as block:

                @block.gpsimd
                def _(pool):
                    for j in range(NCH):
                        pool.wait_ge(*s["ln_out"](j + 1))
                        for k in range(FT):
                            pool.tensor_copy(xn_all[:, k, bass.ds(b * S + j * CH, CH)], xn[:, k, j * CH:(j + 1) * CH])

                @block.tensor
                def _(pe):
                    layer_norm_pe(pe, c, s)
                    pe.wait_ge(*s["ln_out"](NCH))
                    n = 0
                    for j in range(NCH):
                        for m in range(FT):
                            for w, u, _ in GATES:
                                if n >= 8:
                                    pe.wait_ge(*s["gate"](n - 7))
                                for k in range(FT):
                                    pe.matmul(c.bank(n % 8), c.w(w, k, m * P, P), xn[:, k, j * CH:(j + 1) * CH],
                                              start=(k == 0), stop=False)
                                for k in range(FT):
                                    mm = pe.matmul(c.bank(n % 8), c.w(u, k, m * P, P), cell[:, k, j * CH:(j + 1) * CH],
                                                   start=False, stop=(k == 1))
                                mm.then_inc(s["gate_in"].sem)
                                n += 1

                @block.scalar
                def _(act):
                    layer_norm_act(act, c, s, False)
                    act.wait_ge(*s["ln_out"](NCH))
                    n = 0
                    for j in range(NCH):
                        for m in range(FT):
                            for i, (_, _, bias) in enumerate(GATES):
                                act.wait_ge(*s["gate_in"](n + 1))
                                act.activation(gates[i][:, m, j * CH:(j + 1) * CH], c.bank(n % 8),
                                               ACT.Tanh if i == 2 else ACT.Sigmoid, bias=c.v(bias, m)).then_inc(s["gate"].sem)
                                n += 1

                @block.vector
                def _(dve):
                    layer_norm_dve(dve, c, s, x, col(xn), None, None)
                    f, i, g = gates
                    for j in range(NCH):
                        dve.wait_ge(*s["gate"](NG * FT * (j + 1)))
                        for m in range(FT):
                            at = lambda t: t[:, m, j * CH:(j + 1) * CH]
                            n = FT * j + m + 1
                            dve.tensor_tensor(at(fed), at(i), at(g), ALU.mult).then_inc(s["fed"].sem)
                            dve.tensor_tensor(at(cell), at(f), at(cell), ALU.mult).then_inc(s["kept"].sem)
                            dve.wait_ge(*s["fed"](n))
                            dve.wait_ge(*s["kept"](n))
                            dve.tensor_tensor(at(cell), at(cell), at(fed), ALU.add).then_inc(s["cell"].sem)

        with nc.Fori(0, B) as b:
            set_round(b, s2)
            with nc.Block() as block:

                @block.tensor
                def _(pe):
                    for m in range(FT):
                        for j in range(NCH):
                            for k in range(FT):
                                pe.matmul(c.bank(2 * m + j), c.w("f_wo", k, m * P, P), xn_all[:, k, bass.ds(b * S + j * CH, CH)],
                                          start=(k == 0), stop=False)
                            for k in range(FT):
                                mm = pe.matmul(c.bank(2 * m + j), c.w("f_uo", k, m * P, P), cell[:, k, j * CH:(j + 1) * CH],
                                               start=False, stop=(k == 1))
                            mm.then_inc(s2["o_done"].sem)

                @block.scalar
                def _(act):
                    for n in range(FT * NCH):
                        act.wait_ge(*s2["o_done"](n + 1))
                        m, j = divmod(n, NCH)
                        act.activation(fed[:, m, j * CH:(j + 1) * CH], c.bank(n), ACT.Tanh, bias=c.v("f_bo", m)).then_inc(s2["tanh"].sem)

                @block.vector
                def _(dve):
                    for n in range(FT * NCH):
                        dve.wait_ge(*s2["tanh"](n + 1))
                        m, j = divmod(n, NCH)
                        xs = c.xT[:, m, bass.ds(b * S + j * CH, CH)]
                        dve.tensor_tensor(xs, xs, fed[:, m, j * CH:(j + 1) * CH], ALU.add).then_inc(s2["x_done"].sem)
        clear_signals(nc, s, s2, also=[first])


def causal_attention_layer(nc, c):
    H, DH = 16, 16
    SCALE = DH ** -0.5
    QPART = (0, 0, 0, 1, 1, 1, 2, 2)
    KPART = (0, 1, 2, 0, 1, 2, 0, 1)
    RING = 4
    LOADS = 6
    UNITS = H * TT
    with ExitStack() as ctx:
        order = []
        for u in range(UNITS + 1):
            if u < UNITS:
                order.append((u, 0))
            if u < UNITS and u % TT >= 4:
                order.append((u, 1))
        nth = {what: n for n, what in enumerate(order)}
        TILES = len(order) + TT
        s = signals(nc, ctx, "b", dict(
            {name: NCH for name in LN_SIGNALS}, q_proj=4, k_proj=4, v_proj=4, q_raw=4, k_raw=4, v_copied=4,
            part=6, rest=4, stored=2 * 16, **{f"loaded{i}": LOADS * 16 * (H // RING) for i in range(RING)}, scores=UNITS, row_max=UNITS,
            shift=UNITS, expd=UNITS, turned=TILES, copied=TILES, av=UNITS, den_inv=H, normed=H, o_done=4, x_done=4))
        loaded = [s["loaded0"], s["loaded1"], s["loaded2"], s["loaded3"]]
        made = ctx.enter_context(nc.semaphore("b_made"))
        sb = lambda name, shape, dt=F32: ctx.enter_context(nc.sbuf_tensor(name, shape, dt))
        ident16 = sb("b_ident16", [P, P], BF16)
        future = sb("b_future", [P, P], BF16)
        q_parts = sb("b_q_parts", [P, 3, FT, S], BF16)
        k_parts = sb("b_k_parts", [P, 3, FT, S], BF16)
        q_stack = sb("b_q_stack", [P, RING, S], BF16)
        k_stack = sb("b_k_stack", [P, RING, S], BF16)
        rs = sb("b_rs", [P, 2, TT])
        mx = sb("b_mx", [P, 2])
        nm = sb("b_nm", [P, 2])
        q_dram = nc.dram_tensor("b_q_dram", (3, D, S), BF16, kind="Internal").ap()
        k_dram = nc.dram_tensor("b_k_dram", (3, D, S), BF16, kind="Internal").ap()
        xn, q, k_, v, o = c.slot(0), c.slot(1), c.slot(4), c.slot(5), c.slot(1)
        ot = c.slot(0)
        v_t = v.rearrange("p a n -> p (a n)").rearrange("p (t n) -> p t n", t=TT)
        o_t = o.rearrange("p a n -> p (a n)").rearrange("p (t n) -> p t n", t=TT)
        half = lambda i: c.arena[:, 2 * 2048 + i * S:2 * 2048 + (i + 1) * S]
        probs = [half(0), half(1)]
        turned = [half(i).rearrange("p (k n) -> p k n", k=TT) for i in (2, 3)]
        col = lambda t: (lambda k, j: t[:, k, j * CH:(j + 1) * CH])
        with nc.Block() as block:

            @block.gpsimd
            def _(pool):
                pool.tensor_copy(ident16[:], c.ident[:])
                pool.memset(future[:], 0.0).then_inc(made)
                pool.wait_ge(made, 1)
                pool.affine_select(out=future[:], in_=future[:], compare_op=ALU.is_ge, fill=NEG, base=0,
                                   pattern=[[-1, P]], channel_multiplier=1)

        with nc.Fori(0, B) as b:
            set_round(b, s)
            x = lambda k, j: c.xT[:, k, bass.ds(b * S + j * CH, CH)]
            turn_bank = lambda n: c.bank(5 + n % 2)
            score = lambda u: c.psum[u % 2]
            out_bank = lambda h: c.bank(4 if h % 2 else 7)
            with nc.Block() as block:

                @block.sync
                def _(sync):
                    sync.wait_ge(*s["part"](6))
                    for parts, dram in ((q_parts, q_dram), (k_parts, k_dram)):
                        sync.dma_start(dram.rearrange("a (m p) n -> p (a m) n", p=P),
                                       parts[:].rearrange("p a m n -> p (a m) n")).then_inc(s["stored"].sem, 16)
                    sync.wait_ge(*s["stored"](32))
                    for h in range(H):
                        if h >= RING:
                            sync.wait_ge(*s["scores"](TT * (h - RING + 1)))
                        rows = slice(h * DH, (h + 1) * DH)
                        at = h % RING
                        for i in range(3):
                            first, n = QPART.index(i) * DH, QPART.count(i)
                            sync.dma_start(q_stack[first:first + n * DH, at, :],
                                           q_dram[i, rows, :].partition_broadcast(n)).then_inc(loaded[at].sem, 16)
                        for first in (0, 3, 6):
                            n = min(3, len(KPART) - first)
                            sync.dma_start(k_stack[first * DH:(first + n) * DH, at, :],
                                           k_dram[0:n, rows, :]).then_inc(loaded[at].sem, 16)

                @block.tensor
                def _(pe):
                    layer_norm_pe(pe, c, s)
                    pe.wait_ge(*s["ln_out"](NCH))
                    for name, base, done in (("b_wq", 0, s["q_proj"]), ("b_wk", 4, s["k_proj"])):
                        for m in range(FT):
                            for j in range(NCH):
                                for k in range(FT):
                                    mm = pe.matmul(c.bank(base + 2 * m + j), c.w(name, k, m * P, P),
                                                   xn[:, k, j * CH:(j + 1) * CH], start=(k == 0), stop=(k == 1))
                                mm.then_inc(done.sem)
                    for t2 in range(4):
                        pe.wait_ge(*s["q_raw"](t2 + 1))
                        for t in (0, 1):
                            for k in range(FT):
                                mm = pe.matmul(c.bank(t2)[:, t * D:(t + 1) * D], xn[:, k, (2 * t2 + t) * P:(2 * t2 + t + 1) * P],
                                               c.w("b_wv", k, 0, D), start=(k == 0), stop=(k == 1))
                        mm.then_inc(s["v_proj"].sem)

                    def scores(u):
                        h, qi = divmod(u, TT)
                        if u == 0:
                            pe.wait_ge(*s["v_copied"](4))
                            pe.wait_ge(*s["k_raw"](4))
                        if qi == 0:
                            pe.wait_ge(*loaded[h % RING](LOADS * 16 * (h // RING + 1)))
                        if u >= 2:
                            pe.wait_ge(*s["expd"](u - 1))
                        for first in range(0, (qi + 1) * P, CH):
                            n = min(CH, (qi + 1) * P - first)
                            last = first + n == (qi + 1) * P
                            pe.matmul(score(u)[:, first:first + n], q_stack[:, h % RING, qi * P:(qi + 1) * P],
                                      k_stack[:, h % RING, first:first + n], start=True, stop=not last)
                        pe.matmul(score(u)[:, qi * P:(qi + 1) * P], ident16[:], future[:], start=False, stop=True)\
                          .then_inc(s["scores"].sem)

                    def turn(u, i):
                        n = nth[u, i]
                        pe.wait_ge(*s["expd"](u + 1))
                        if n >= 2:
                            pe.wait_ge(*s["copied"](n - 1))
                        for kb in range(4 * i, min(4 * i + 4, u % TT + 1)):
                            mm = pe.transpose(turn_bank(n)[:, (kb % 4) * P:(kb % 4 + 1) * P],
                                              probs[u % 2][:, kb * P:(kb + 1) * P], c.ident[:])
                        mm.then_inc(s["turned"].sem)

                    def values(u):
                        h, qi = divmod(u, TT)
                        pe.wait_ge(*s["copied"](nth[u, 1 if qi >= 4 else 0] + 1))
                        if qi == 0 and h >= 2:
                            pe.wait_ge(*s["normed"](h - 1))
                        for kb in range(qi + 1):
                            mm = pe.matmul(out_bank(h)[:, qi * DH:(qi + 1) * DH], turned[u % 2][:, kb, :],
                                           v_t[:, kb, h * DH:(h + 1) * DH], start=(kb == 0), stop=(kb == qi))
                        mm.then_inc(s["av"].sem)

                    scores(0)
                    for u in range(UNITS + 1):
                        if u + 1 < UNITS:
                            scores(u + 1)
                        if u < UNITS:
                            turn(u, 0)
                        if u >= 1:
                            values(u - 1)
                        if u < UNITS and u % TT >= 4:
                            turn(u, 1)
                    pe.wait_ge(*s["normed"](H))
                    for qi in range(TT):
                        n = len(order) + qi
                        pe.wait_ge(*s["copied"](n - 1))
                        for m in range(FT):
                            mm = pe.transpose(turn_bank(n)[:, m * P:(m + 1) * P], o_t[:, qi, m * P:(m + 1) * P], c.ident[:])
                        mm.then_inc(s["turned"].sem)
                    pe.wait_ge(*s["copied"](TILES))
                    for m in range(FT):
                        for j in range(NCH):
                            for k in range(FT):
                                mm = pe.matmul(c.bank(2 * m + j), c.w("b_wo", k, m * P, P), ot[:, k, j * CH:(j + 1) * CH],
                                               start=(k == 0), stop=(k == 1))
                            mm.then_inc(s["o_done"].sem)

                @block.scalar
                def _(act):
                    layer_norm_act(act, c, s, False)
                    act.wait_ge(*s["ln_out"](NCH))
                    for t, bias, ready, done, base in ((q, "b_bq", s["q_proj"], s["q_raw"], 0), (k_, "b_bk", s["k_proj"], s["k_raw"], 4)):
                        for n in range(4):
                            m, j = divmod(n, NCH)
                            act.wait_ge(*ready(n + 1))
                            act.activation(t[:, m, j * CH:(j + 1) * CH], c.bank(base + n), ACT.Identity, bias=c.v(bias, m))\
                               .then_inc(done.sem)
                    for i in range(3):
                        for n, (t, parts) in enumerate(((q, q_parts), (k_, k_parts))):
                            if i == 0:
                                act.wait_ge(*(s["k_raw"] if n else s["q_raw"])(4))
                            else:
                                act.wait_ge(*s["rest"](2 * (i - 1) + n + 1))
                            act.activation(parts[:, i, :, :], t, ACT.Copy).then_inc(s["part"].sem)
                    for u in range(UNITS):
                        h, qi = divmod(u, TT)
                        act.wait_ge(*s["shift"](u + 1))
                        if u >= 2:
                            act.wait_ge(*s["turned"](nth[u - 2, 1 if (u - 2) % TT >= 4 else 0] + 1))
                        n = (qi + 1) * P
                        act.activation(probs[u % 2][:, 0:n], score(u)[:, 0:n], ACT.Exp, bias=nm[:, u % 2:u % 2 + 1],
                                       scale=SCALE, accum_out=rs[:, h % 2, qi:qi + 1]).then_inc(s["expd"].sem)

                @block.vector
                def _(dve):
                    layer_norm_dve(dve, c, s, x, col(xn), None, None)
                    for t2 in range(4):
                        dve.wait_ge(*s["v_proj"](t2 + 1))
                        dve.tensor_copy(v_t[:, 2 * t2:2 * t2 + 2, :].rearrange("p t n -> p (t n)"), c.bank(t2)).then_inc(s["v_copied"].sem)
                    for i in range(2):
                        for n, (t, parts) in enumerate(((q, q_parts), (k_, k_parts))):
                            dve.wait_ge(*s["part"](2 * i + n + 1))
                            dve.tensor_tensor(t, t, parts[:, i, :, :], ALU.subtract).then_inc(s["rest"].sem)

                    def shift(u):
                        h, qi = divmod(u, TT)
                        at = u % 2
                        dve.wait_ge(*s["scores"](u + 1))
                        dve.tensor_reduce(mx[:, at:at + 1], score(u)[:, 0:(qi + 1) * P], AX, ALU.max).then_inc(s["row_max"].sem)
                        dve.wait_ge(*s["row_max"](u + 1))
                        dve.tensor_scalar(nm[:, at:at + 1], mx[:, at:at + 1], -SCALE, None, ALU.mult).then_inc(s["shift"].sem)

                    def copy_turned(u, i):
                        n = nth[u, i]
                        dve.wait_ge(*s["turned"](n + 1))
                        if u >= 2 and i == 0:
                            dve.wait_ge(*s["av"](u - 1))
                        first, last = 4 * i, min(4 * i + 4, u % TT + 1)
                        dve.tensor_copy(turned[u % 2][:, first:last, :].rearrange("p k n -> p (k n)"),
                                        turn_bank(n)[:, 0:(last - first) * P]).then_inc(s["copied"].sem)

                    def norm(h):
                        if h == 0:
                            dve.wait_ge(*s["part"](6))
                        dve.wait_ge(*s["av"](TT * (h + 1)))
                        dve.wait_ge(*s["expd"](TT * (h + 1)))
                        dve.reciprocal(rs[:, h % 2, :], rs[:, h % 2, :]).then_inc(s["den_inv"].sem)
                        dve.wait_ge(*s["den_inv"](h + 1))
                        dve.tensor_tensor(o_t[:, :, h * DH:(h + 1) * DH], out_bank(h)[:, 0:TT * DH].rearrange("p (t d) -> p t d", t=TT),
                                          rs[:, h % 2, :].unsqueeze(2).to_broadcast([P, TT, DH]), ALU.mult).then_inc(s["normed"].sem)

                    shift(0)
                    for u in range(UNITS + 1):
                        if u + 1 < UNITS:
                            shift(u + 1)
                        if u < UNITS:
                            copy_turned(u, 0)
                        if u >= 1 and (u - 1) % TT == TT - 1:
                            norm((u - 1) // TT)
                        if u < UNITS and u % TT >= 4:
                            copy_turned(u, 1)
                    for qi in range(TT):
                        n = len(order) + qi
                        dve.wait_ge(*s["turned"](n + 1))
                        for m in range(FT):
                            ins = dve.tensor_scalar(ot[:, m, qi * P:(qi + 1) * P], turn_bank(n)[:, m * P:(m + 1) * P],
                                                    c.v("b_bv", m), None, ALU.add)
                        ins.then_inc(s["copied"].sem)
                    for m in range(FT):
                        for j in range(NCH):
                            dve.wait_ge(*s["o_done"](2 * m + j + 1))
                            dve.scalar_tensor_tensor(out=x(m, j), in0=c.bank(2 * m + j), scalar=c.v("b_bo", m),
                                                     in1=x(m, j), op0=ALU.add, op1=ALU.add).then_inc(s["x_done"].sem)
        clear_signals(nc, s, also=[made])


def context_attention_layer(nc, c):
    H, DH = 16, 16
    SCALE = DH ** -0.5
    HT8 = H // FT
    PAIRS = H // 2
    KC = [P, CF - P]
    with ExitStack() as ctx:
        s = signals(nc, ctx, "y", dict(
            {name: NCH for name in LN_SIGNALS}, q_proj=4, q_raw=4, scores=TT, row_max=TT, shifted=TT, expd=TT,
            den=TT, den_inv=TT, turned=3 * TT, copied=3 * TT, av=TT, normed=TT, o_done=4, x_done=4))
        g = signals(nc, ctx, "yc", dict(load=1, made=3, k=1, v=1, kb=1, out=1))
        set_round(0, g)
        sb = lambda name, shape, dt=F32: ctx.enter_context(nc.sbuf_tensor(name, shape, dt))
        of_head = sb("y_of_head", [P, HT8])
        cx = sb("y_cx", [P, 2, B * KEYS])
        kc = sb("y_kc", [P, FT, B * KEYS])
        k_diag = sb("y_k_diag", [P, B, FT, CH])
        v_diag = sb("y_v_diag", [P, B, PAIRS, 2 * DH])
        mx = sb("y_mx", [P, 2, H])
        rs = sb("y_rs", [P, 2, H])
        o = sb("y_o", [P, 2, D])
        xn, q, ot = c.slot(0), c.slot(1), c.slot(4)
        quarter = lambda first, i: c.arena[:, first * 2048 + i * S:first * 2048 + (i + 1) * S]
        probs = [quarter(2, 0), quarter(2, 1)]
        turned = [quarter(3, i).rearrange("p (k n) -> p k n", k=PAIRS) for i in range(2)]
        col = lambda t: (lambda k, j: t[:, k, j * CH:(j + 1) * CH])
        with nc.Block() as block:

            @block.sync
            def _(sync):
                sync.dma_start(cx[:], c.ctx_t).then_inc(g["load"].sem, 16)

            @block.gpsimd
            def _(pool):
                pool.memset(v_diag[:], 0.0).then_inc(g["made"].sem)
                pool.memset(of_head[:], 1.0).then_inc(g["made"].sem)
                pool.wait_ge(*g["made"](2))
                pool.affine_select(out=of_head[:], in_=of_head[:], compare_op=ALU.is_ge, fill=0.0, base=0,
                                   pattern=[[-DH, HT8]], channel_multiplier=1).then_inc(g["made"].sem)
                pool.wait_ge(*g["made"](3))
                pool.affine_select(out=of_head[:], in_=of_head[:], compare_op=ALU.is_ge, fill=0.0, base=DH - 1,
                                   pattern=[[DH, HT8]], channel_multiplier=-1).then_inc(g["made"].sem)

            @block.tensor
            def _(pe):
                pe.wait_ge(g["load"].sem, 16)
                for m in range(FT):
                    for k in range(2):
                        mm = pe.matmul(c.bank(0)[:, m * P:(m + 1) * P], c.w("y_wk", k, m * P, P, KC[k]), cx[0:KC[k], k, :],
                                       start=(k == 0), stop=(k == 1))
                mm.then_inc(g["k"].sem)
                for b in range(B):
                    for k in range(2):
                        mm = pe.matmul(c.bank(1)[0:KEYS, b * D:(b + 1) * D], cx[0:KC[k], k, b * KEYS:(b + 1) * KEYS],
                                       c.w("y_wv", k, 0, D, KC[k]), start=(k == 0), stop=(k == 1))
                mm.then_inc(g["v"].sem)

            @block.vector
            def _(dve):
                dve.wait_ge(*g["k"](1))
                for m in range(FT):
                    ins = dve.tensor_scalar(kc[:, m, :], c.bank(0)[:, m * P:(m + 1) * P], c.v("y_bk", m), None, ALU.add)
                ins.then_inc(g["kb"].sem)
                dve.wait_ge(*g["kb"](1))
                dve.wait_ge(*g["made"](4))
                for b in range(B):
                    for m in range(FT):
                        dve.tensor_tensor(k_diag[:, b, m, :].rearrange("p (h n) -> p h n", h=HT8),
                                          kc[:, m, b * KEYS:(b + 1) * KEYS].unsqueeze(1).to_broadcast([P, HT8, KEYS]),
                                          of_head[:].unsqueeze(2).to_broadcast([P, HT8, KEYS]), ALU.mult)
                dve.wait_ge(*g["v"](1))
                for b in range(B):
                    pairs = c.bank(1)[0:KEYS, b * D:(b + 1) * D].rearrange("p (r d) -> p r d", r=PAIRS)
                    for i in (0, 1):
                        dve.tensor_copy(v_diag[i * KEYS:(i + 1) * KEYS, b, :, i * DH:(i + 1) * DH], pairs[:, :, i * DH:(i + 1) * DH])

        with nc.Fori(0, B) as b:
            set_round(b, s)
            x = lambda k, j: c.xT[:, k, bass.ds(b * S + j * CH, CH)]
            kd = k_diag[:].rearrange("p b m n -> p (b m n)")
            vd = v_diag[:].rearrange("p b r d -> p (b r d)")
            score = lambda u: c.psum[u % 2]
            turn_bank = lambda n: c.bank(5 + n % 2)
            out_bank = lambda u: c.bank(4 if u % 2 else 7)
            order = []
            for u in range(TT + 2):
                if u < TT:
                    order += [(u, 0), (u, 1)]
                if u >= 2:
                    order.append((u - 2, "o"))
            nth = {what: n for n, what in enumerate(order)}
            with nc.Block() as block:

                @block.tensor
                def _(pe):
                    layer_norm_pe(pe, c, s)
                    pe.wait_ge(*s["ln_out"](NCH))
                    for m in range(FT):
                        for j in range(NCH):
                            for k in range(FT):
                                mm = pe.matmul(c.bank(4 + 2 * m + j), c.w("y_wq", k, m * P, P),
                                               xn[:, k, j * CH:(j + 1) * CH], start=(k == 0), stop=(k == 1))
                            mm.then_inc(s["q_proj"].sem)

                    def scores(u):
                        if u == 0:
                            pe.wait_ge(*s["q_raw"](4))
                        if u >= 2:
                            pe.wait_ge(*s["shifted"](u - 1))
                        for m in range(FT):
                            mm = pe.matmul(score(u)[:, m * CH:(m + 1) * CH], q[:, m, u * P:(u + 1) * P],
                                           kd[:, bass.ds(b * (FT * CH) + m * CH, CH)], start=True, stop=True)
                        mm.then_inc(s["scores"].sem)

                    def turn(u, i):
                        n = nth[u, i]
                        pe.wait_ge(*s["expd"](u + 1))
                        if n >= 2:
                            pe.wait_ge(*s["copied"](n - 1))
                        for r in range(4):
                            mm = pe.transpose(turn_bank(n)[:, r * P:(r + 1) * P], probs[u % 2][:, (4 * i + r) * P:(4 * i + r + 1) * P],
                                              c.ident[:])
                        mm.then_inc(s["turned"].sem)

                    def values(u):
                        pe.wait_ge(*s["copied"](nth[u, 1] + 1))
                        if u >= 2:
                            pe.wait_ge(*s["normed"](u - 1))
                        for r in range(PAIRS):
                            mm = pe.matmul(out_bank(u)[:, r * 2 * DH:(r + 1) * 2 * DH], turned[u % 2][:, r, :],
                                           vd[:, bass.ds(b * D + r * 2 * DH, 2 * DH)], start=True, stop=True)
                        mm.then_inc(s["av"].sem)

                    def turn_outputs(u):
                        n = nth[u, "o"]
                        pe.wait_ge(*s["normed"](u + 1))
                        pe.wait_ge(*s["copied"](n - 1))
                        for m in range(FT):
                            mm = pe.transpose(turn_bank(n)[:, m * P:(m + 1) * P], o[:, u % 2, m * P:(m + 1) * P], c.ident[:])
                        mm.then_inc(s["turned"].sem)

                    scores(0)
                    for u in range(TT + 2):
                        if u + 1 < TT:
                            scores(u + 1)
                        if u < TT:
                            turn(u, 0)
                            turn(u, 1)
                        if u >= 2:
                            turn_outputs(u - 2)
                        if 1 <= u <= TT:
                            values(u - 1)
                    pe.wait_ge(*s["copied"](len(order)))
                    for m in range(FT):
                        for j in range(NCH):
                            for k in range(FT):
                                mm = pe.matmul(c.bank(2 * m + j), c.w("y_wo", k, m * P, P), ot[:, k, j * CH:(j + 1) * CH],
                                               start=(k == 0), stop=(k == 1))
                            mm.then_inc(s["o_done"].sem)

                @block.scalar
                def _(act):
                    layer_norm_act(act, c, s, False)
                    for n in range(4):
                        m, j = divmod(n, NCH)
                        act.wait_ge(*s["q_proj"](n + 1))
                        act.activation(q[:, m, j * CH:(j + 1) * CH], c.bank(4 + n), ACT.Identity, bias=c.v("y_bq", m)).then_inc(s["q_raw"].sem)
                    for u in range(TT):
                        act.wait_ge(*s["shifted"](u + 1))
                        act.activation(probs[u % 2], probs[u % 2], ACT.Exp, scale=SCALE).then_inc(s["expd"].sem)

                @block.vector
                def _(dve):
                    layer_norm_dve(dve, c, s, x, col(xn), None, None)
                    heads = lambda ap: ap.rearrange("p (h n) -> p h n", h=H)
                    wide = lambda ap, n: ap.unsqueeze(2).to_broadcast([P, H, n])

                    def shift(u):
                        if u == 0:
                            dve.wait_ge(*s["ln_out"](NCH))
                        dve.wait_ge(*s["scores"](u + 1))
                        dve.tensor_reduce(mx[:, u % 2, :], heads(score(u)[:]), AX, ALU.max).then_inc(s["row_max"].sem)
                        dve.wait_ge(*s["row_max"](u + 1))
                        if u >= 2:
                            dve.wait_ge(*s["turned"](nth[u - 2, 1] + 1))
                        dve.tensor_tensor(heads(probs[u % 2]), heads(score(u)[:]), wide(mx[:, u % 2, :], KEYS), ALU.subtract)\
                           .then_inc(s["shifted"].sem)

                    def copy_turned(u, i):
                        n = nth[u, i]
                        dve.wait_ge(*s["turned"](n + 1))
                        if u >= 2 and i == 0:
                            dve.wait_ge(*s["av"](u - 1))
                        dve.tensor_copy(turned[u % 2][:, 4 * i:4 * i + 4, :].rearrange("p k n -> p (k n)"), turn_bank(n))\
                           .then_inc(s["copied"].sem)

                    def den(u):
                        dve.wait_ge(*s["expd"](u + 1))
                        if u >= 2:
                            dve.wait_ge(*s["normed"](u - 1))
                        dve.tensor_reduce(rs[:, u % 2, :], heads(probs[u % 2]), AX, ALU.add).then_inc(s["den"].sem)
                        dve.wait_ge(*s["den"](u + 1))
                        dve.reciprocal(rs[:, u % 2, :], rs[:, u % 2, :]).then_inc(s["den_inv"].sem)

                    def norm(u):
                        dve.wait_ge(*s["av"](u + 1))
                        dve.wait_ge(*s["den_inv"](u + 1))
                        dve.tensor_tensor(heads(o[:, u % 2, :]), heads(out_bank(u)[:, 0:D]), wide(rs[:, u % 2, :], DH), ALU.mult)\
                           .then_inc(s["normed"].sem)

                    def copy_outputs(u):
                        n = nth[u, "o"]
                        dve.wait_ge(*s["turned"](n + 1))
                        for m in range(FT):
                            ins = dve.tensor_scalar(ot[:, m, u * P:(u + 1) * P], turn_bank(n)[:, m * P:(m + 1) * P],
                                                    c.v("y_bv", m), None, ALU.add)
                        ins.then_inc(s["copied"].sem)

                    shift(0)
                    for u in range(TT + 2):
                        if u < TT:
                            den(u)
                        if u + 1 < TT:
                            shift(u + 1)
                        if u < TT:
                            copy_turned(u, 0)
                            copy_turned(u, 1)
                        if u >= 2:
                            copy_outputs(u - 2)
                        if 1 <= u <= TT:
                            norm(u - 1)
                    for m in range(FT):
                        for j in range(NCH):
                            dve.wait_ge(*s["o_done"](2 * m + j + 1))
                            dve.scalar_tensor_tensor(out=x(m, j), in0=c.bank(2 * m + j), scalar=c.v("y_bo", m),
                                                     in1=x(m, j), op0=ALU.add, op1=ALU.add).then_inc(s["x_done"].sem)
        clear_signals(nc, s, g)


def expert_layer(nc, c):
    TIL = T // P
    GP = GR // 2
    NP_ = TIL * EXP
    RN = FT + GP + 2 + FT * GP
    NEXT = EXP + 2
    with ExitStack() as ctx:
        sb = lambda name, shape, dt=F32: ctx.enter_context(nc.sbuf_tensor(name, shape, dt))
        s = signals(nc, ctx, "m", dict({name: NCH for name in LN_SIGNALS}, turned=4, copied=4, logits=1, logits_read=1))
        r = signals(nc, ctx, "r", dict(made=4, step=40, prep=5, cum1=1, cnt=2, cum2=1))
        set_round(0, r)
        e = signals(nc, ctx, "e", dict(
            made=2 * RN, read=2 * RN, w0_done=2 * HT, w1_done=2 * HT, gelu=2 * HT, hidden=2 * HT, prep=10, prepared=2))
        w_sig = [ctx.enter_context(nc.semaphore(f"e_weights{i}")) for i in range(2)]
        xn_tok = c.arena[:, 4 * FT * S:].rearrange("p (t n) -> p t n", t=TIL)
        logits = sb("m_logits", [P, TIL, EXP])
        tab = {n: sb(f"m_{n}", [P, TIL, EXP]) for n in ("raw", "rest", "m1", "m2", "p1", "p2", "t")}
        order8 = sb("m_order", [P, EXP])
        col16 = {n: sb(f"m_{n}", [P, TIL]) for n in ("mx", "sm", "g1", "g2", "pick")}
        pos = [sb(f"m_pos{i}", [P, NEXT * TIL]) for i in (1, 2)]
        before = sb("m_before", [P, P])
        ones = sb("m_ones", [P, P])
        iota_i = sb("m_iota_i", [P, CAP], mybir.dt.int32)
        iota = sb("m_iota", [P, CAP])
        disp = [sb(f"m_disp{i}", [P, TIL, CAP]) for i in range(2)]
        comb = [sb(f"m_comb{i}", [P, TIL, P]) for i in range(2)]
        one = sb("m_one", [P, TIL, CAP])
        two = sb("m_two", [P, TIL, CAP])
        back = sb("m_back", [P, TIL, P])
        x_in = sb("m_x_in", [P, FT, CH])
        gelu = c.arena[:, (HT + 2) * CH:(HT + 4) * CH].rearrange("p (i n) -> p i n", i=2)
        hidden = c.arena[:, 0:HT * CH].rearrange("p (h n) -> p h n", h=HT)
        e_out = c.arena[:, HT * CH:(HT + 2) * CH].rearrange("p (g n) -> p g n", g=GP)
        xn = c.slot(0)
        n_w = FT * HID
        per = 2 * n_w + HT * D
        assert 2 * per <= c.mats["router"][0]
        wbuf = [c.weights[:, i * per:(i + 1) * per] for i in range(2)]
        w0 = [w[:, 0:n_w].rearrange("p (k h) -> p k h", k=FT) for w in wbuf]
        w1 = [w[:, n_w:2 * n_w].rearrange("p (k h) -> p k h", k=FT) for w in wbuf]
        wo = [w[:, 2 * n_w:].rearrange("p (h n) -> p h n", h=HT) for w in wbuf]
        FULL = (HT - 1) * P
        col = lambda t: (lambda k, j: t[:, k, j * CH:(j + 1) * CH])

        def load_expert(sync, i, ex):
            pick = lambda m: m[bass.ds(ex, 1)].rearrange("e a b c -> (e a) b c") if len(m.shape) == 4 else \
                m[bass.ds(ex, 1)].rearrange("e a b -> (e a) b")
            sync.dma_start(w0[i], pick(c.w0)).then_inc(w_sig[i], 16)
            sync.dma_start(w1[i], pick(c.w1)).then_inc(w_sig[i], 16)
            rows = pick(c.wo)
            sync.dma_start(wo[i][:, 0:HT - 1, :], rows[0:FULL, :].rearrange("(h p) n -> p h n", p=P)).then_inc(w_sig[i], 16)
            sync.dma_start(wo[i][0:HLAST, HT - 1, :], rows[FULL:HID, :]).then_inc(w_sig[i], 16)

        W_LOAD = 4 * 16
        with nc.Block() as block:

            @block.sync
            def _(sync):
                for i in range(2):
                    load_expert(sync, i, i)

            @block.gpsimd
            def _(pool):
                for i in range(2):
                    pool.memset(comb[i][:], 0.0)
                    pool.memset(pos[i][:], -1.0)
                pool.iota(iota_i[:], pattern=[[1, CAP]], base=0, channel_multiplier=0).then_inc(r["made"].sem)
                pool.memset(ones[:], 1.0).then_inc(r["made"].sem)
                pool.wait_ge(*r["made"](2))
                pool.affine_select(out=before[:], in_=ones[:], compare_op=ALU.is_gt, fill=0.0, base=0,
                                   pattern=[[1, P]], channel_multiplier=-1)
                for i in range(EXP):
                    pool.memset(order8[:, i:i + 1], float(EXP - i))
                pool.tensor_copy(iota[:], iota_i[:]).then_inc(r["made"].sem)

        with nc.Fori(0, B) as b:
            set_round(b, s)
            x = lambda k, j: c.xT[:, k, bass.ds(b * S + j * CH, CH)]
            with nc.Block() as block:

                @block.tensor
                def _(pe):
                    layer_norm_pe(pe, c, s)
                    pe.wait_ge(*s["ln_out"](NCH))
                    for t in range(TT):
                        for k in range(FT):
                            mm = pe.matmul(c.bank(7)[:, t * EXP:(t + 1) * EXP], xn[:, k, t * P:(t + 1) * P],
                                           c.w("router", k, 0, EXP), start=(k == 0), stop=(k == 1))
                    mm.then_inc(s["logits"].sem)
                    for t2 in range(4):
                        for t in (0, 1):
                            for k in range(FT):
                                mm = pe.transpose(c.bank(t2)[:, t * D + k * P:t * D + (k + 1) * P],
                                                  xn[:, k, (2 * t2 + t) * P:(2 * t2 + t + 1) * P], c.ident[:])
                        mm.then_inc(s["turned"].sem)

                @block.scalar
                def _(act):
                    layer_norm_act(act, c, s, False)
                    flat = xn_tok.rearrange("p t n -> p (t n)")
                    for t2 in range(4):
                        act.wait_ge(*s["turned"](t2 + 1))
                        act.activation(flat[:, bass.ds(b * (TT * D) + t2 * CH, CH)], c.bank(t2), ACT.Copy).then_inc(s["copied"].sem)

                @block.vector
                def _(dve):
                    layer_norm_dve(dve, c, s, x, col(xn), None, None)
                    dve.wait_ge(*s["logits"](1))
                    dve.tensor_copy(logits[:].rearrange("p t e -> p (t e)")[:, bass.ds(b * (TT * EXP), TT * EXP)],
                                    c.bank(7)[:, 0:TT * EXP]).then_inc(s["logits_read"].sem)

        def prepare(dve, i, ex, done, sig):
            wide_pos = lambda p: p[:, bass.ds(ex * TIL, TIL)].unsqueeze(2).to_broadcast([P, TIL, CAP])
            wide_iota = iota[:].unsqueeze(1).to_broadcast([P, TIL, CAP])
            wide16 = lambda t: t[:].unsqueeze(2).to_broadcast([P, TIL, CAP])
            n = [0]

            def step(f):
                def go():
                    n[0] += 1
                    f().then_inc(sig.sem)
                    dve.wait_ge(*sig(5 * done + n[0]))
                return go
            return [
                step(lambda: dve.tensor_tensor(one[:], wide_pos(pos[0]), wide_iota, ALU.is_equal)),
                step(lambda: dve.tensor_tensor(two[:], wide_pos(pos[1]), wide_iota, ALU.is_equal)),
                step(lambda: dve.tensor_tensor(disp[i][:], one[:], two[:], ALU.add)),
                step(lambda: dve.tensor_tensor(one[:], one[:], wide16(col16["g1"]), ALU.mult)),
                step(lambda: dve.tensor_tensor(two[:], two[:], wide16(col16["g2"]), ALU.mult)),
            ], lambda: combine_halves(dve, i)

        def combine_halves(dve, i):
            for g in range(2):
                for q in range(GP):
                    tiles = slice(4 * q + 2 * g, 4 * q + 2 * g + 2)
                    ins = dve.tensor_tensor(comb[i][:, tiles, g * CAP:(g + 1) * CAP], one[:, tiles, :], two[:, tiles, :], ALU.add)
            return ins

        with nc.Block() as block:

            @block.tensor
            def _(pe):
                even = lambda t: t.rearrange("p (g t) e -> p g t e", t=2)[:, :, 0, :]
                odd = lambda t: t.rearrange("p (g t) e -> p g t e", t=2)[:, :, 1, :]
                table = lambda i: c.bank(i)[:, 0:NP_].rearrange("p (t e) -> p t e", t=TIL)
                pe.wait_ge(*r["made"](3))
                pe.wait_ge(*r["cum1"](1))
                pe.matmul(table(0), before[:], tab["m1"][:], start=True, stop=False)
                pe.matmul(odd(table(0)), ones[:], even(tab["m1"][:]), start=False, stop=True).then_inc(r["cnt"].sem)
                pe.wait_ge(*r["cum2"](1))
                pe.matmul(table(1), before[:], tab["m2"][:], start=True, stop=False)
                pe.matmul(odd(table(1)), ones[:], even(tab["m2"][:]), start=False, stop=False)
                for to in (even, odd):
                    for of in (even, odd):
                        mm = pe.matmul(to(table(1)), ones[:], of(tab["m1"][:]), start=False, stop=(to is odd and of is odd))
                mm.then_inc(r["cnt"].sem)

            @block.scalar
            def _(act):
                act.wait_ge(*r["step"](2))
                act.activation(tab["raw"][:], tab["raw"][:], ACT.Exp).then_inc(r["step"].sem)

            @block.vector
            def _(dve):
                n = [0]

                def do(ins):
                    n[0] += 1
                    ins.then_inc(r["step"].sem)
                    dve.wait_ge(*r["step"](n[0]))

                wide = lambda t: t[:].unsqueeze(2).to_broadcast([P, TIL, EXP])
                order_w = order8[:].unsqueeze(1).to_broadcast([P, TIL, EXP])
                raw, rest, t = tab["raw"], tab["rest"], tab["t"]
                dve.wait_ge(*r["made"](3))
                do(dve.tensor_reduce(col16["mx"][:], logits[:], AX, ALU.max))
                do(dve.tensor_tensor(raw[:], logits[:], wide(col16["mx"]), ALU.subtract))
                n[0] += 1
                dve.wait_ge(*r["step"](n[0]))
                do(dve.tensor_reduce(col16["sm"][:], raw[:], AX, ALU.add))
                do(dve.reciprocal(col16["sm"][:], col16["sm"][:]))
                do(dve.tensor_tensor(raw[:], raw[:], wide(col16["sm"]), ALU.mult))

                def first_max(values, gate, chosen):
                    do(dve.tensor_reduce(gate[:], values[:], AX, ALU.max))
                    do(dve.tensor_tensor(t[:], values[:], wide(gate), ALU.is_equal))
                    do(dve.tensor_tensor(t[:], t[:], order_w, ALU.mult))
                    do(dve.tensor_reduce(col16["pick"][:], t[:], AX, ALU.max))
                    do(dve.tensor_tensor(chosen[:], t[:], wide(col16["pick"]), ALU.is_equal))

                first_max(raw, col16["g1"], tab["m1"])
                do(dve.tensor_tensor(t[:], raw[:], tab["m1"][:], ALU.mult))
                do(dve.tensor_tensor(rest[:], raw[:], t[:], ALU.subtract))
                first_max(rest, col16["g2"], tab["m2"])
                dve.tensor_copy(t[:], t[:]).then_inc(r["cum1"].sem)

                def keep(i, m, p, bank):
                    do(dve.tensor_copy(p[:].rearrange("p t e -> p (t e)"), c.bank(bank)[:, 0:NP_]))
                    do(dve.tensor_scalar(t[:], p[:], float(CAP), None, ALU.is_lt))
                    do(dve.tensor_tensor(m[:], m[:], t[:], ALU.mult))
                    do(dve.tensor_scalar(p[:], p[:], 1.0, None, ALU.add))
                    do(dve.tensor_tensor(p[:], p[:], m[:], ALU.mult))
                    do(dve.tensor_scalar(pos[i][:, 0:NP_].rearrange("p (e t) -> p t e", t=TIL), p[:], -1.0, None, ALU.add))

                dve.wait_ge(*r["cnt"](1))
                keep(0, tab["m1"], tab["p1"], 0)
                dve.tensor_copy(t[:], t[:]).then_inc(r["cum2"].sem)
                dve.wait_ge(r["cnt"].sem, 2)
                keep(1, tab["m2"], tab["p2"], 1)
                steps, last = prepare(dve, 0, 0, 0, r["prep"])
                for go in steps:
                    go()
                last()

        def expert_round(rd, load):
            with nc.Block() as block:
                H_N = lambda h: P if h < HT - 1 else HLAST

                @block.sync
                def _(sync):
                    if load:
                        for i in range(2):
                            sync.wait_ge(*e["made"](RN * i + 8))
                            load_expert(sync, i, 2 * rd + 2 + i)

                @block.tensor
                def _(pe):
                    ring = [0]

                    def reuse():
                        n = ring[0]
                        ring[0] += 1
                        if n >= 4:
                            pe.wait_ge(*e["read"](n - 3))
                        return c.bank(4 + n % 4)

                    for i in range(2):
                        if i == 1:
                            pe.wait_ge(*e["prepared"](1))
                        for m in range(FT):
                            bank = reuse()
                            for g in range(GR):
                                for t in range(2):
                                    mm = pe.matmul(bank[:, g * CAP:(g + 1) * CAP], xn_tok[:, 2 * g + t, m * P:(m + 1) * P],
                                                   disp[i][:, 2 * g + t, :], start=(t == 0), stop=(t == 1))
                            mm.then_inc(e["made"].sem)
                        for q in range(GP):
                            bank = reuse()
                            for t in range(4):
                                mm = pe.transpose(bank[:, t * P:(t + 1) * P], comb[i][:, 4 * q + t, :], c.ident[:])
                            mm.then_inc(e["made"].sem)
                        pe.wait_ge(w_sig[i], w_value(rd))
                        pe.wait_ge(*e["read"](RN * i + 2))
                        for h in range(HT):
                            n = HT * i + h
                            for w, base, free, done in ((w0, 0, e["gelu"], e["w0_done"]), (w1, 2, e["hidden"], e["w1_done"])):
                                if n >= 2:
                                    pe.wait_ge(*free(n - 1))
                                for k in range(FT):
                                    mm = pe.matmul(c.bank(base + n % 2)[0:H_N(h), :], w[i][:, k, h * P:h * P + H_N(h)],
                                                   x_in[:, k, :], start=(k == 0), stop=(k == 1))
                                mm.then_inc(done.sem)
                        pe.wait_ge(*e["hidden"](HT * (i + 1)))
                        for q2 in range(2):
                            bank = reuse()
                            for q in (0, 1):
                                for h in range(HT):
                                    mm = pe.matmul(bank[:, q * D:(q + 1) * D],
                                                   hidden[0:H_N(h), h, (2 * q2 + q) * P:(2 * q2 + q + 1) * P],
                                                   wo[i][0:H_N(h), h, :], start=(h == 0), stop=(h == HT - 1))
                            mm.then_inc(e["made"].sem)
                        pe.wait_ge(*e["read"](RN * i + 8))
                        for m in range(FT):
                            for q in range(GP):
                                bank = reuse()
                                pe.matmul(bank, e_out[:, q, m * P:(m + 1) * P],
                                          back[:, 4 * q:4 * q + 4, :].rearrange("p t n -> p (t n)"), start=True, stop=True)\
                                  .then_inc(e["made"].sem)

                @block.scalar
                def _(act):
                    for n in range(2 * HT):
                        h = n % HT
                        act.wait_ge(*e["w0_done"](n + 1))
                        if n >= 2:
                            act.wait_ge(*e["hidden"](n - 1))
                        act.activation(gelu[0:H_N(h), n % 2, :], c.bank(n % 2)[0:H_N(h), :], ACT.Gelu_apprx_tanh).then_inc(e["gelu"].sem)

                @block.vector
                def _(dve):
                    n = [0]

                    def take(f):
                        n[0] += 1
                        dve.wait_ge(*e["made"](n[0]))
                        f(c.bank(4 + (n[0] - 1) % 4)).then_inc(e["read"].sem)

                    for i in range(2):
                        for m in range(FT):
                            take(lambda bank: dve.tensor_copy(x_in[:, m, :], bank))
                        for q in range(GP):
                            take(lambda bank: dve.tensor_copy(back[:, 4 * q:4 * q + 4, :].rearrange("p t n -> p (t n)"), bank))
                        steps, last = prepare(dve, 1 - i, 2 * rd + 1 + i, i, e["prep"])
                        for h in range(HT):
                            k = HT * i + h
                            dve.wait_ge(*e["gelu"](k + 1))
                            dve.wait_ge(*e["w1_done"](k + 1))
                            dve.tensor_tensor(hidden[0:H_N(h), h, :], gelu[0:H_N(h), k % 2, :], c.bank(2 + k % 2)[0:H_N(h), :],
                                              ALU.mult).then_inc(e["hidden"].sem)
                            if h < len(steps):
                                steps[h]()
                            if h == len(steps):
                                last().then_inc(e["prepared"].sem)
                        for q2 in range(2):
                            take(lambda bank: dve.tensor_copy(e_out[:, 2 * q2:2 * q2 + 2, :].rearrange("p q n -> p (q n)"), bank))
                        for m in range(FT):
                            for q in range(GP):
                                xs = c.xT[:, m, q * CH:(q + 1) * CH]
                                take(lambda bank: dve.tensor_tensor(xs, bank, xs, ALU.add))

        w_value = lambda rd: W_LOAD * (rd + 1)
        ROUNDS = EXP // 2
        with nc.Fori(0, ROUNDS - 1) as rd:
            set_round(rd, e)
            expert_round(rd, True)
        set_round(ROUNDS - 1, e)
        expert_round(ROUNDS - 1, False)
        clear_signals(nc, s, r, e, also=w_sig)


def load_everything(nc, ctx, c, x_t, weights, vectors):
    loaded = ctx.enter_context(nc.semaphore("loaded"))
    made = ctx.enter_context(nc.semaphore("made"))
    with nc.Block() as block:

        @block.sync
        def _(sync):
            sync.dma_start(c.xT[:], x_t).then_inc(loaded, 16)
            sync.dma_start(c.vectors[:], vectors).then_inc(loaded, 16)
            sync.dma_start(c.weights[:], weights).then_inc(loaded, 16)
            sync.wait_ge(loaded, 48)

        @block.gpsimd
        def _(pool):
            pool.memset(c.mean_w[:], 1.0 / D)
            pool.memset(c.eps[:], LN_EPS)
            pool.memset(c.ident[:], 0.0).then_inc(made)
            pool.wait_ge(made, 1)
            pool.affine_select(out=c.ident[:], in_=c.ident[:], compare_op=ALU.not_equal, fill=1.0, base=0,
                               pattern=[[-1, P]], channel_multiplier=1).then_inc(made)


def store_result(nc, ctx, c, out):
    stored = ctx.enter_context(nc.semaphore("stored"))
    with nc.Block() as block:

        @block.sync
        def _(sync):
            sync.dma_start(out, c.xT[:]).then_inc(stored, 16)
            sync.wait_ge(stored, 16)


LAYERS = [linear_attention_layer, cross_attention_layer, gated_recurrence_layer, causal_attention_layer,
          context_attention_layer, expert_layer]


def build_program(nc, x_t, ctx_t, mask, weights, vectors, w0, w1, wo, out, layers=None):
    with ExitStack() as ctx:
        c = Chip(nc, ctx)
        c.ctx_t, c.mask, c.w0, c.w1, c.wo = ctx_t, mask, w0, w1, wo
        load_everything(nc, ctx, c, x_t, weights, vectors)
        for layer in LAYERS if layers is None else layers:
            layer(nc, c)
        store_result(nc, ctx, c, out)


def kernel(**inputs):
    import numpy as np
    import concourse.bacc as bacc
    from concourse import mybir as _mybir
    from concourse.bass_utils import run_bass_kernel_spmd

    a = {k: np.asarray(v) for k, v in inputs.items()}
    wqkv = a["L1_attn_Wqkv"]
    part = lambda i: wqkv[:, :, 16 * i:16 * (i + 1)].transpose(1, 0, 2).reshape(D, D)
    bias = lambda i: a["L1_attn_bqkv"][:, 16 * i:16 * (i + 1)].reshape(D)
    mats = {
        "a_wq": a["L0_attn_wq"], "a_wk": a["L0_attn_wk"], "a_wv": a["L0_attn_wv"], "a_wo": a["L0_attn_wo"],
        "a_w1": a["L0_attn_w_ff1"], "a_w2": a["L0_attn_w_ff2"], "a_wd": a["L0_attn_w_d"],
        "x_wq": a["L0_xattn_Wq"].T, "x_wkv": a["L0_xattn_Wkv"].T, "x_wlkv": a["L0_xattn_Wlkv"].T,
        "x_wo": a["L0_xattn_Wo"].T,
        "f_wf": a["L0_ffn_wf"].T, "f_uf": a["L0_ffn_uf"].T, "f_wi": a["L0_ffn_wi"].T, "f_ui": a["L0_ffn_ui"].T,
        "f_wc": a["L0_ffn_wc"].T, "f_uc": a["L0_ffn_uc"].T, "f_wo": a["L0_ffn_wo"].T, "f_uo": a["L0_ffn_uo"].T,
        "b_wq": part(0), "b_wk": part(1), "b_wv": part(2), "b_wo": a["L1_attn_Wout"],
        "y_wq": a["L1_xattn_wq"], "y_wk": a["L1_xattn_wk"], "y_wv": a["L1_xattn_wv"], "y_wo": a["L1_xattn_wo"],
        "router": a["L1_ffn_router_w"],
    }
    vecs = {
        "a_g1": a["L0_attn_ln1_g"], "a_b1": a["L0_attn_ln1_b"], "a_bo": a["L0_attn_bo"], "a_g2": a["L0_attn_ln2_g"],
        "a_b2": a["L0_attn_ln2_b"], "a_bf1": a["L0_attn_b_ff1"], "a_bf2": a["L0_attn_b_ff2"], "a_bd": a["L0_attn_b_d"],
        "x_gx": a["L0_xattn_ln_x_g"], "x_bx": a["L0_xattn_ln_x_b"], "x_gl": a["L0_xattn_ln_l_g"],
        "x_bl": a["L0_xattn_ln_l_b"], "x_gq": np.tile(a["L0_xattn_qn_g"], 2), "x_gk": np.tile(a["L0_xattn_kn_g"], 2),
        "x_bo": a["L0_xattn_bo"],
        "f_bf": a["L0_ffn_bf"], "f_bi": a["L0_ffn_bi"], "f_bc": a["L0_ffn_bc"], "f_bo": a["L0_ffn_bo"],
        "f_c0": a["L0_ffn_in_c"],
        "b_bq": bias(0), "b_bk": bias(1), "b_bv": bias(2), "b_bo": a["L1_attn_bout"],
        "y_bq": a["L1_xattn_bq"], "y_bk": a["L1_xattn_bk"], "y_bv": a["L1_xattn_bv"], "y_bo": a["L1_xattn_bo"],
    }

    def tiles(m):
        n = -(-m.shape[0] // P)
        full = np.zeros((n * P, m.shape[1]), m.dtype)
        full[:m.shape[0]] = m
        return full.reshape(n, P, -1).transpose(1, 0, 2).reshape(P, -1)

    ins = {
        "x_t": a["x"].reshape(T, FT, P).transpose(2, 1, 0),
        "ctx_t": tiles(a["ctx_768"].reshape(B * KEYS, CF).T),
        "mask": a["mask_BxS2_bk0"].reshape(1, B * KEYS),
        "weights": np.concatenate([tiles(mats[n]) for n in MATS], 1),
        "vectors": np.concatenate([tiles(vecs[n].reshape(-1, 1)) for n in VECS], 1),
        "w0": a["L1_ffn_w0_kernel"].reshape(EXP, FT, P, HID).transpose(0, 2, 1, 3),
        "w1": a["L1_ffn_w1_kernel"].reshape(EXP, FT, P, HID).transpose(0, 2, 1, 3),
        "wo": a["L1_ffn_wo_kernel"],
    }
    ins = {n: np.ascontiguousarray(v) for n, v in ins.items()}
    nc = bacc.Bacc("TRN2", target_bir_lowering=False, num_devices=1)
    args = [nc.dram_tensor(n, v.shape, _mybir.dt.from_np(v.dtype), kind="ExternalInput").ap() for n, v in ins.items()]
    out = nc.dram_tensor("out", (P, FT, T), F32, kind="ExternalOutput").ap()
    build_program(nc, *args, out)
    got = run_bass_kernel_spmd(nc, [ins], core_ids=[0]).results[0]["out"]
    return got.transpose(2, 1, 0).reshape(B, S, D)
```

```python
from contextlib import ExitStack

import concourse.bass as bass
from concourse import mybir

F32 = mybir.dt.float32
BF16 = mybir.dt.bfloat16
U8 = mybir.dt.uint8
ALU = mybir.AluOpType
ACT = mybir.ActivationFunctionType
AX = mybir.AxisListType.X

P = 128
B, S, D = 2, 1024, 256
T = B * S
FT = D // P
CH = 512
NCH = S // CH
TT = S // P
LN_EPS = 1e-5
NEG = -1e30

MATS = {
    "a_wq": (256, 256), "a_wk": (256, 256), "a_wv": (256, 256), "a_wo": (256, 256),
    "a_w1": (256, 1024), "a_w2": (1024, 256), "a_wd": (256, 256),
    "x_wq": (256, 256), "x_wkv": (192, 512), "x_wlkv": (256, 512), "x_wo": (256, 256),
    "f_wf": (256, 256), "f_uf": (256, 256), "f_wi": (256, 256), "f_ui": (256, 256),
    "f_wc": (256, 256), "f_uc": (256, 256), "f_wo": (256, 256), "f_uo": (256, 256),
    "b_wq": (256, 256), "b_wk": (256, 256), "b_wv": (256, 256), "b_wo": (256, 256),
    "y_wq": (256, 256), "y_wk": (192, 256), "y_wv": (192, 256), "y_wo": (256, 256),
    "router": (256, 8),
}
VECS = {
    "a_g1": 2, "a_b1": 2, "a_bo": 2, "a_g2": 2, "a_b2": 2, "a_bf1": 8, "a_bf2": 2, "a_bd": 2,
    "x_gx": 2, "x_bx": 2, "x_gl": 2, "x_bl": 2, "x_gq": 1, "x_gk": 1, "x_bo": 2,
    "f_bf": 2, "f_bi": 2, "f_bc": 2, "f_bo": 2, "f_c0": 2,
    "b_bq": 2, "b_bk": 2, "b_bv": 2, "b_bo": 2,
    "y_bq": 2, "y_bk": 2, "y_bv": 2, "y_bo": 2,
}
KEYS = 64
CF = 192
EXP, HID, CAP, GR = 8, 1368, 64, 8
HT = -(-HID // P)
HLAST = HID - (HT - 1) * P


def mat_offsets():
    off, at = {}, 0
    for name, (rows, cols) in MATS.items():
        tiles = -(-rows // P)
        off[name] = (at, tiles, cols)
        at += tiles * cols
    return off, at


def vec_offsets():
    off, at = {}, 0
    for name, n in VECS.items():
        off[name] = (at, n)
        at += n
    return off, at


class Sig:

    def __init__(self, sem, per_round):
        self.sem, self.per_round, self.round = sem, per_round, 0

    def __call__(self, n):
        return self.sem, self.round * self.per_round + n


class Chip:

    def __init__(self, nc, ctx):
        sb = lambda name, shape, dt=F32: ctx.enter_context(nc.sbuf_tensor(name, shape, dt))
        self.mats, n_mat = mat_offsets()
        self.vecs, n_vec = vec_offsets()
        self.xT = sb("xT", [P, FT, T])
        self.weights = sb("weights_sb", [P, n_mat])
        self.vectors = sb("vectors_sb", [P, n_vec])
        self.ident = sb("ident", [P, P])
        self.mean_w = sb("mean_w", [P, P])
        self.eps = sb("eps", [P, 1])
        self.eps_eps = sb("eps_eps", [P, 1])
        self.arena = sb("arena", [P, 6 * FT * S])
        self.ln = sb("ln", [P, 3 * NCH, CH])
        self.ln_s, self.ln_d, self.ln_r = (self.ln[:, i * NCH:(i + 1) * NCH, :] for i in range(3))
        self.psum = [ctx.enter_context(nc.psum_tensor(f"psum{i}", [P, 2 * CH], F32)) for i in range(4)]

    def slot(self, i):
        n = FT * S
        return self.arena[:, i * n:(i + 1) * n].rearrange("p (m t) -> p m t", m=FT)

    def two_slots(self, i):
        n = FT * T
        return self.arena[:, i * n // 2:i * n // 2 + n].rearrange("p (m t) -> p m t", m=FT)

    def spent_weights(self):
        assert FT * T <= self.mats["x_wq"][0]
        return self.weights[:, 0:FT * T].rearrange("p (m t) -> p m t", m=FT)

    def bank(self, i):
        return self.psum[i // 2][:, (i % 2) * CH:(i % 2 + 1) * CH]

    def w(self, name, k, first, n, rows=P):
        at, _, cols = self.mats[name]
        return self.weights[0:rows, at + k * cols + first:at + k * cols + first + n]

    def v(self, name, k):
        return self.vectors[:, self.vecs[name][0] + k:self.vecs[name][0] + k + 1]


def layer_norm_pe(pe, c, s):
    for j in range(NCH):
        pe.wait_ge(*s["ln_sum"](j + 1))
        pe.matmul(c.bank(j), c.mean_w[:], c.ln_s[:, j, :], start=True, stop=True).then_inc(s["ln_mean"].sem)
    for j in range(NCH):
        pe.wait_ge(*s["ln_sq"](j + 1))
        for k in range(FT):
            mm = pe.matmul(c.bank(2 + j), c.mean_w[:], c.slot(3)[:, k, j * CH:(j + 1) * CH],
                           start=(k == 0), stop=(k == FT - 1))
        mm.then_inc(s["ln_var"].sem)


def layer_norm_act(act, c, s, twice=False, once=True):
    for j in range(NCH):
        act.wait_ge(*s["ln_cent"](j + 1))
        act.activation(c.slot(3)[:, :, j * CH:(j + 1) * CH], c.slot(2)[:, :, j * CH:(j + 1) * CH],
                       ACT.Square).then_inc(s["ln_sq"].sem)
    for j in range(NCH):
        act.wait_ge(*s["ln_var"](j + 1))
        if once:
            ins = act.activation(c.ln_d[:, j, :], c.bank(2 + j), ACT.Ln, bias=c.eps[:, 0:1])
        if twice:
            ins = act.activation(c.ln_s[:, j, :], c.bank(2 + j), ACT.Ln, bias=c.eps_eps[:, 0:1], scale=1.0 + LN_EPS)
        ins.then_inc(s["ln_log"].sem)
    for j in range(NCH):
        act.wait_ge(*s["ln_log"](j + 1))
        if once:
            ins = act.activation(c.ln_r[:, j, :], c.ln_d[:, j, :], ACT.Exp, scale=-0.5)
        if twice:
            ins = act.activation(c.ln_s[:, j, :], c.ln_s[:, j, :], ACT.Exp, scale=-0.5)
        ins.then_inc(s["ln_rstd"].sem)


def layer_norm_dve(dve, c, s, x, out, gain=None, bias=None, twice=False, once_out=None):
    for j in range(NCH):
        dve.tensor_tensor(c.ln_s[:, j, :], x(0, j), x(1, j), ALU.add).then_inc(s["ln_sum"].sem)
    for j in range(NCH):
        dve.wait_ge(*s["ln_mean"](j + 1))
        for k in range(FT):
            ins = dve.tensor_tensor(c.slot(2)[:, k, j * CH:(j + 1) * CH], x(k, j), c.bank(j), ALU.subtract)
        ins.then_inc(s["ln_cent"].sem)
    factor = c.ln_s if twice else c.ln_r
    for j in range(NCH):
        dve.wait_ge(*s["ln_rstd"](j + 1))
        centred = lambda k: c.slot(2)[:, k, j * CH:(j + 1) * CH]
        for k in range(FT):
            if gain is None:
                ins = dve.tensor_tensor(out(k, j), centred(k), factor[:, j, :], ALU.mult)
            else:
                ins = dve.scalar_tensor_tensor(out=out(k, j), in0=centred(k), scalar=gain(k), in1=factor[:, j, :],
                                               op0=ALU.mult, op1=ALU.mult)
                ins.then_inc(s["ln_scaled"].sem)
        if gain is not None:
            for k in range(FT):
                dve.wait_ge(*s["ln_scaled"](FT * j + k + 1))
                ins = dve.tensor_scalar(out(k, j), out(k, j), bias(k), None, ALU.add)
        if once_out is None or j < NCH - 1:
            ins.then_inc(s["ln_out"].sem)
        if once_out is not None:
            for k in range(FT):
                ins = dve.tensor_tensor(once_out(k, j), centred(k), c.ln_r[:, j, :], ALU.mult)
            if j == NCH - 1:
                ins.then_inc(s["ln_out"].sem)


LN_SIGNALS = {"ln_sum": NCH, "ln_mean": NCH, "ln_cent": NCH, "ln_sq": NCH, "ln_var": NCH, "ln_log": NCH, "ln_rstd": NCH,
              "ln_scaled": FT * NCH, "ln_out": NCH}


def norm_signals():
    n = B * NCH
    return {"sum": n, "mean": n, "cent": n, "sq": n, "var": n, "log": n, "rstd": n, "scaled": FT * n}


def norm_both(nc, c, s, out, gain=None, bias=None, twice=False):
    N = B * NCH
    at = lambda t, j: t[:, :, j * CH:(j + 1) * CH]
    centred, squares = c.two_slots(4), c.two_slots(2)
    with nc.Block() as block:

        @block.tensor
        def _(pe):
            for j in range(N):
                pe.wait_ge(*s["sum"](j + 1))
                pe.matmul(c.bank(j), c.mean_w[:], c.ln[:, j, :], start=True, stop=True).then_inc(s["mean"].sem)
            for j in range(N):
                pe.wait_ge(*s["sq"](j + 1))
                for k in range(FT):
                    mm = pe.matmul(c.bank(N + j), c.mean_w[:], at(squares, j)[:, k, :], start=(k == 0), stop=(k == FT - 1))
                mm.then_inc(s["var"].sem)

        @block.scalar
        def _(act):
            for j in range(N):
                act.wait_ge(*s["cent"](j + 1))
                act.activation(at(squares, j), at(centred, j), ACT.Square).then_inc(s["sq"].sem)
            for j in range(N):
                act.wait_ge(*s["var"](j + 1))
                if twice:
                    ins = act.activation(c.ln[:, j, :], c.bank(N + j), ACT.Ln, bias=c.eps_eps[:, 0:1], scale=1.0 + LN_EPS)
                else:
                    ins = act.activation(c.ln[:, j, :], c.bank(N + j), ACT.Ln, bias=c.eps[:, 0:1])
                ins.then_inc(s["log"].sem)
            for j in range(N):
                act.wait_ge(*s["log"](j + 1))
                act.activation(c.ln[:, j, :], c.ln[:, j, :], ACT.Exp, scale=-0.5).then_inc(s["rstd"].sem)

        @block.vector
        def _(dve):
            for j in range(N):
                dve.tensor_tensor(c.ln[:, j, :], at(c.xT, j)[:, 0, :], at(c.xT, j)[:, 1, :], ALU.add).then_inc(s["sum"].sem)
            for j in range(N):
                dve.wait_ge(*s["mean"](j + 1))
                for k in range(FT):
                    ins = dve.tensor_tensor(at(centred, j)[:, k, :], at(c.xT, j)[:, k, :], c.bank(j), ALU.subtract)
                ins.then_inc(s["cent"].sem)
            for j in range(N):
                dve.wait_ge(*s["rstd"](j + 1))
                for k in range(FT):
                    to, of = at(out, j)[:, k, :], at(centred, j)[:, k, :]
                    if gain is None:
                        dve.tensor_tensor(to, of, c.ln[:, j, :], ALU.mult)
                    else:
                        dve.scalar_tensor_tensor(out=to, in0=of, scalar=gain(k), in1=c.ln[:, j, :],
                                                 op0=ALU.mult, op1=ALU.mult).then_inc(s["scaled"].sem)
                if gain is not None:
                    for k in range(FT):
                        dve.wait_ge(*s["scaled"](FT * j + k + 1))
                        dve.tensor_scalar(at(out, j)[:, k, :], at(out, j)[:, k, :], bias(k), None, ALU.add)


def clear_signals(nc, *groups, also=()):
    with nc.Block() as block:

        @block.gpsimd
        def _(pool):
            for sem in [sig.sem for group in groups for sig in group.values()] + list(also):
                pool.sem_clear(sem)


def signals(nc, ctx, layer, counts):
    return {name: Sig(ctx.enter_context(nc.semaphore(f"{layer}_{name}")), n) for name, n in counts.items()}


def set_round(b, *groups):
    for group in groups:
        for sig in group.values():
            sig.round = b


def linear_attention_layer(nc, c):
    H, DH = 4, 64
    SCALE = float(DH) ** -0.25
    with ExitStack() as ctx:
        ln_n = LN_SIGNALS
        s = signals(nc, ctx, "a", dict(
            ln_n, k_proj=4, k_max=4, k_shift=1, k_max_all=1, k_added=1, k_inv=1, zeroed=1, k_exp=4, k_turned=4, k_copied=4, v_proj=4, v_copied=4,
            q_proj=4, q_max=4, q_shift=4, q_exp=4, q_sum=4, q_inv=4, q_norm=4, q_turned=4, q_copied=4,
            ctx_done=1, ctx_copied=1, at_done=4, at_copied=4, o_done=4, y_done=4,
            ff_done=16, ff_gelu=16, f2_done=4, y2_done=4, d_done=4, x_done=4))
        s2 = signals(nc, ctx, "a2", ln_n)
        sb = lambda name, shape: ctx.enter_context(nc.sbuf_tensor(name, shape, F32))
        k_mx = sb("a_k_mx", [P, FT, NCH])
        k_m = sb("a_k_m", [P, FT])
        k_s = sb("a_k_s", [P, FT, NCH])
        k_r = sb("a_k_r", [P, FT])
        q_m = sb("a_q_m", [P, 4, 8])
        q_s = sb("a_q_s", [P, 4, 8])
        context = sb("a_context", [P, FT, P])
        h1, h2, ek, v, ekt, qn = (c.slot(i) for i in range(6))
        v_t = v.rearrange("p a n -> p (a n)").rearrange("p (t n) -> p t n", t=TT)
        ekt_t = ekt.rearrange("p a n -> p (a n)").rearrange("p (t n) -> p t n", t=TT)
        q_t = qn.rearrange("p a n -> p (a n)").rearrange("p (u n) -> p u n", u=4)
        qt, at = c.slot(2), c.slot(5)
        y = h1
        hid = [c.arena[:, (2 + 2 * j) * 2048:(4 + 2 * j) * 2048].rearrange("p (f n) -> p f n", f=8) for j in range(NCH)]
        with nc.Fori(0, B) as b:
            set_round(b, s, s2)
            x = lambda k, j: c.xT[:, k, bass.ds(b * S + j * CH, CH)]
            col = lambda t: (lambda k, j: t[:, k, j * CH:(j + 1) * CH])
            with nc.Block() as block:

                @block.gpsimd
                def _(pool):
                    pool.memset(context[:], 0.0).then_inc(s["zeroed"].sem)

                @block.tensor
                def _(pe):
                    layer_norm_pe(pe, c, s)
                    pe.wait_ge(*s["ln_out"](NCH))
                    for m in range(FT):
                        for j in range(NCH):
                            for k in range(FT):
                                mm = pe.matmul(c.bank(2 * m + j), c.w("a_wk", k, m * P, P), h2[:, k, j * CH:(j + 1) * CH],
                                               start=(k == 0), stop=(k == 1))
                            mm.then_inc(s["k_proj"].sem)
                    for u in range(4):
                        for t in (0, 1):
                            for k in range(FT):
                                mm = pe.matmul(c.bank(4 + u)[:, t * D:(t + 1) * D], h2[:, k, (2 * u + t) * P:(2 * u + t + 1) * P],
                                               c.w("a_wv", k, 0, D), start=(k == 0), stop=(k == 1))
                        mm.then_inc(s["v_proj"].sem)
                    for u in range(4):
                        pe.wait_ge(*s["v_copied"](u + 1))
                        for t in (0, 1):
                            for k in range(FT):
                                mm = pe.matmul(c.bank(4 + u)[:, t * D:(t + 1) * D], h2[:, k, (2 * u + t) * P:(2 * u + t + 1) * P],
                                               c.w("a_wq", k, 0, D), start=(k == 0), stop=(k == 1))
                        mm.then_inc(s["q_proj"].sem)
                    pe.wait_ge(*s["k_exp"](4))
                    for u in range(4):
                        for t in (0, 1):
                            for m in range(FT):
                                mm = pe.transpose(c.bank(u)[:, t * D + m * P:t * D + (m + 1) * P],
                                                  ek[:, m, (2 * u + t) * P:(2 * u + t + 1) * P], c.ident[:])
                        mm.then_inc(s["k_turned"].sem)
                    pe.wait_ge(*s["k_copied"](4))
                    for m in range(FT):
                        for t in range(TT):
                            mm = pe.matmul(c.bank(0)[:, m * P:(m + 1) * P], ekt_t[:, t, m * P:(m + 1) * P],
                                           v_t[:, t, m * P:(m + 1) * P], start=(t == 0), stop=(t == TT - 1))
                    mm.then_inc(s["ctx_done"].sem)
                    for u in range(4):
                        pe.wait_ge(*s["q_norm"](u + 1))
                        for m in range(FT):
                            for t in (0, 1):
                                mm = pe.transpose(c.bank(4 + u)[:, m * D + t * P:m * D + (t + 1) * P],
                                                  q_t[:, u, t * D + m * P:t * D + (m + 1) * P], c.ident[:])
                        mm.then_inc(s["q_turned"].sem)
                    pe.wait_ge(*s["ctx_copied"](1))
                    pe.wait_ge(*s["q_copied"](4))
                    for m in range(FT):
                        for j in range(NCH):
                            pe.matmul(c.bank(2 * m + j), context[:, m, :], qt[:, m, j * CH:(j + 1) * CH],
                                      start=True, stop=True).then_inc(s["at_done"].sem)
                    pe.wait_ge(*s["at_copied"](4))
                    for m in range(FT):
                        for j in range(NCH):
                            for k in range(FT):
                                mm = pe.matmul(c.bank(4 + 2 * m + j), c.w("a_wo", k, m * P, P), at[:, k, j * CH:(j + 1) * CH],
                                               start=(k == 0), stop=(k == 1))
                            mm.then_inc(s["o_done"].sem)
                    layer_norm_pe(pe, c, s2)
                    n = 0
                    for j in range(NCH):
                        pe.wait_ge(*s2["ln_out"](NCH))
                        for f in range(8):
                            if n >= 4:
                                pe.wait_ge(*s["ff_gelu"](n - 3))
                            for k in range(FT):
                                mm = pe.matmul(c.bank(4 + n % 4), c.w("a_w1", k, f * P, P), h2[:, k, j * CH:(j + 1) * CH],
                                               start=(k == 0), stop=(k == 1))
                            mm.then_inc(s["ff_done"].sem)
                            n += 1
                    for j in range(NCH):
                        pe.wait_ge(*s["ff_gelu"](8 * (j + 1)))
                        for m in range(FT):
                            for f in range(8):
                                mm = pe.matmul(c.bank(2 * m + j), c.w("a_w2", f, m * P, P), hid[j][:, f, :],
                                               start=(f == 0), stop=(f == 7))
                            mm.then_inc(s["f2_done"].sem)
                    pe.wait_ge(*s["ff_gelu"](16))
                    for j in range(NCH):
                        pe.wait_ge(*s["y2_done"](2 * (j + 1)))
                        for m in range(FT):
                            for k in range(FT):
                                mm = pe.matmul(c.bank(4 + 2 * m + j), c.w("a_wd", k, m * P, P), y[:, k, j * CH:(j + 1) * CH],
                                               start=(k == 0), stop=(k == 1))
                            mm.then_inc(s["d_done"].sem)

                @block.scalar
                def _(act):
                    layer_norm_act(act, c, s, twice=True)
                    act.wait_ge(*s["k_shift"](1))
                    for m in range(FT):
                        for j in range(NCH):
                            act.activation(ek[:, m, j * CH:(j + 1) * CH], c.bank(2 * m + j), ACT.Exp, bias=k_m[:, m:m + 1],
                                           scale=SCALE, accum_out=k_s[:, m, j:j + 1]).then_inc(s["k_exp"].sem)
                    for u in range(4):
                        act.wait_ge(*s["q_shift"](u + 1))
                        act.activation(q_t[:, u, :], q_t[:, u, :], ACT.Exp, scale=SCALE).then_inc(s["q_exp"].sem)
                    for u in range(4):
                        act.wait_ge(*s["k_turned"](u + 1))
                        act.activation(ekt_t[:, 2 * u:2 * u + 2, :].rearrange("p t n -> p (t n)"), c.bank(u), ACT.Copy)\
                           .then_inc(s["k_copied"].sem)
                    for u in range(4):
                        act.wait_ge(*s["q_turned"](u + 1))
                        act.activation(qt[:, :, u * D:(u + 1) * D], c.bank(4 + u).rearrange("p (m n) -> p m n", m=FT),
                                       ACT.Copy).then_inc(s["q_copied"].sem)
                    for m in range(FT):
                        for j in range(NCH):
                            act.wait_ge(*s["at_done"](2 * m + j + 1))
                            act.activation(at[:, m, j * CH:(j + 1) * CH], c.bank(2 * m + j), ACT.Copy)\
                               .then_inc(s["at_copied"].sem)
                    layer_norm_act(act, c, s2)
                    n = 0
                    act.wait_ge(*s2["ln_out"](NCH))
                    for j in range(NCH):
                        for f in range(8):
                            act.wait_ge(*s["ff_done"](n + 1))
                            act.activation(hid[j][:, f, :], c.bank(4 + n % 4), ACT.Gelu_apprx_tanh,
                                           bias=c.v("a_bf1", f)).then_inc(s["ff_gelu"].sem)
                            n += 1

                @block.vector
                def _(dve):
                    layer_norm_dve(dve, c, s, x, col(h2), lambda k: c.v("a_g1", k), lambda k: c.v("a_b1", k), twice=True, once_out=col(h1))
                    for m in range(FT):
                        for j in range(NCH):
                            dve.wait_ge(*s["k_proj"](2 * m + j + 1))
                            dve.tensor_reduce(k_mx[:, m, j:j + 1], c.bank(2 * m + j), AX, ALU.max).then_inc(s["k_max"].sem)
                    dve.wait_ge(*s["k_max"](4))
                    dve.tensor_reduce(k_m[:], k_mx[:], AX, ALU.max).then_inc(s["k_max_all"].sem)
                    dve.wait_ge(*s["k_max_all"](1))
                    dve.tensor_scalar(k_m[:], k_m[:], -SCALE, None, ALU.mult).then_inc(s["k_shift"].sem)
                    for u in range(4):
                        dve.wait_ge(*s["v_proj"](u + 1))
                        dve.tensor_copy(v_t[:, 2 * u:2 * u + 2, :].rearrange("p t n -> p (t n)"), c.bank(4 + u))\
                           .then_inc(s["v_copied"].sem)
                    heads = lambda ap: ap.rearrange("p (h d) -> p h d", d=DH)
                    wide = lambda ap: ap.unsqueeze(2).to_broadcast([P, 8, DH])
                    for u in range(4):
                        dve.wait_ge(*s["q_proj"](u + 1))
                        dve.tensor_reduce(q_m[:, u, :], heads(c.bank(4 + u)), AX, ALU.max).then_inc(s["q_max"].sem)
                        dve.wait_ge(*s["q_max"](u + 1))
                        dve.tensor_tensor(heads(q_t[:, u, :]), heads(c.bank(4 + u)), wide(q_m[:, u, :]), ALU.subtract)\
                           .then_inc(s["q_shift"].sem)
                    for u in range(4):
                        dve.wait_ge(*s["q_exp"](u + 1))
                        dve.tensor_reduce(q_s[:, u, :], heads(q_t[:, u, :]), AX, ALU.add).then_inc(s["q_sum"].sem)
                        dve.wait_ge(*s["q_sum"](u + 1))
                        dve.reciprocal(q_s[:, u, :], q_s[:, u, :]).then_inc(s["q_inv"].sem)
                        dve.wait_ge(*s["q_inv"](u + 1))
                        dve.tensor_tensor(heads(q_t[:, u, :]), heads(q_t[:, u, :]), wide(q_s[:, u, :]), ALU.mult)\
                           .then_inc(s["q_norm"].sem)
                    dve.wait_ge(*s["k_exp"](4))
                    dve.tensor_tensor(k_r[:], k_s[:, :, 0], k_s[:, :, 1], ALU.add).then_inc(s["k_added"].sem)
                    dve.wait_ge(*s["k_added"](1))
                    dve.reciprocal(k_r[:], k_r[:]).then_inc(s["k_inv"].sem)
                    dve.wait_ge(*s["k_inv"](1))
                    dve.wait_ge(*s["zeroed"](1))
                    dve.wait_ge(*s["ctx_done"](1))
                    for m in range(FT):
                        for h in (0, DH):
                            ins = dve.tensor_scalar(context[h:h + DH, m, h:h + DH], c.bank(0)[h:h + DH, m * P + h:m * P + h + DH],
                                                    k_r[h:h + DH, m:m + 1], None, ALU.mult)
                    ins.then_inc(s["ctx_copied"].sem)
                    for m in range(FT):
                        for j in range(NCH):
                            dve.wait_ge(*s["o_done"](2 * m + j + 1))
                            dve.scalar_tensor_tensor(out=y[:, m, j * CH:(j + 1) * CH], in0=c.bank(4 + 2 * m + j),
                                                     scalar=c.v("a_bo", m), in1=h1[:, m, j * CH:(j + 1) * CH],
                                                     op0=ALU.add, op1=ALU.add).then_inc(s["y_done"].sem)
                    dve.wait_ge(*s["y_done"](4))
                    layer_norm_dve(dve, c, s2, col(y), col(h2), lambda k: c.v("a_g2", k), lambda k: c.v("a_b2", k))
                    for j in range(NCH):
                        for m in range(FT):
                            dve.wait_ge(*s["f2_done"](2 * j + m + 1))
                            dve.scalar_tensor_tensor(out=y[:, m, j * CH:(j + 1) * CH], in0=c.bank(2 * m + j),
                                                     scalar=c.v("a_bf2", m), in1=y[:, m, j * CH:(j + 1) * CH],
                                                     op0=ALU.add, op1=ALU.add).then_inc(s["y2_done"].sem)
                    for j in range(NCH):
                        for m in range(FT):
                            dve.wait_ge(*s["d_done"](2 * j + m + 1))
                            dve.scalar_tensor_tensor(out=x(m, j), in0=c.bank(4 + 2 * m + j), scalar=c.v("a_bd", m),
                                                     in1=x(m, j), op0=ALU.add, op1=ALU.add).then_inc(s["x_done"].sem)
        clear_signals(nc, s, s2)


def cross_attention_layer(nc, c):
    H, DH = 4, 64
    SCALE = DH ** -0.5
    HP = H // FT
    NB = TT + 1
    UNITS = TT * H
    TILES = 3 * UNITS + 2 * TT
    KC = [P, CF - P]
    with ExitStack() as ctx:
        norm_s = signals(nc, ctx, "xn", norm_signals())
        s = signals(nc, ctx, "x", dict(
            ln_in=1, q_proj=4, k_proj=4, v_proj=4, raw=8, square=8, ms=8, ms_max=8, ms_log=8, inv=8, scaled=8, v_copied=4,
            ctx_v=1, scores=UNITS, shift=UNITS, ctx_max=TT, row_max=UNITS, expd=UNITS,
            padded=1, turned=TILES, copied=TILES, av=UNITS, den=TT, den_inv=TT, normed=TT, o_done=4, x_done=4))
        g = signals(nc, ctx, "xc", dict(load=1, made=4, sum_s=1, mean=1, cent=1, sq=1, var=1, log=1, rstd=1, scaled=1,
                                        out=1, k=1, v=1, raw=1, square=1, ms=1, ms_max=1, ms_log=1, inv=1, kn=1, vc=1,
                                        mask=1, mask2=1))
        set_round(0, g)
        sb = lambda name, shape, dt=F32: ctx.enter_context(nc.sbuf_tensor(name, shape, dt))
        same_head = sb("x_same_head", [P, P])
        ctx_mean = sb("x_ctx_mean", [P, P])
        mask_u8 = sb("x_mask_u8", [P, B * KEYS], U8)
        mask_add = sb("x_mask_add", [P, B * KEYS])
        cx = sb("x_cx", [P, 2, B * KEYS])
        cs = sb("x_cs", [P, 2, B * KEYS])
        cr = sb("x_cr", [P, 2, B * KEYS])
        k_ctx = sb("x_k_ctx", [P, FT, B * KEYS])
        v_ctx_all = sb("x_v_ctx_all", [KEYS, B, D])
        k_ctx_now = sb("x_k_ctx_now", [P, FT, P])
        mask_sel = sb("x_mask_sel", [P, H * KEYS])
        v_ctx = sb("x_v_ctx", [KEYS, D])
        turned = [sb(f"x_turned{i}", [P, NB, P]) for i in range(2)]
        o = sb("x_o", [P, 2, D])
        ctx_s = sb("x_ctx_s", [P, 2, H * KEYS])
        mxc = sb("x_mxc", [P, 2, H])
        mx = sb("x_mx", [P, 2])
        nm = sb("x_nm", [P, 2])
        rs = sb("x_rs", [P, 2, H, 2])
        rr = sb("x_rr", [P, 2, H])
        ln, qt, scr, inv, kt, v = c.slot(0), c.slot(1), c.slot(2), c.slot(3), c.slot(4), c.slot(5)
        ot = c.slot(0)
        v_t = v.rearrange("p a n -> p (a n)").rearrange("p (t n) -> p t n", t=TT)
        probs = [c.arena[:, (2 + i) * 2048:(2 + i) * 2048 + NB * P] for i in range(2)]

        with nc.Block() as block:

            @block.sync
            def _(sync):
                sync.dma_start(cx[:], c.ctx_t).then_inc(g["load"].sem, 16)
                sync.dma_start(mask_u8[:], c.mask[0, :].partition_broadcast(P)).then_inc(g["load"].sem, 16)

            @block.gpsimd
            def _(pool):
                pool.memset(ctx_mean[:], 1.0 / CF)
                pool.memset(k_ctx_now[:], 0.0)
                pool.memset(same_head[:], 0.0).then_inc(g["made"].sem)
                pool.wait_ge(*g["made"](1))
                pool.memset(same_head[0:DH, 0:DH], 1.0 / DH)
                pool.memset(same_head[DH:P, DH:P], 1.0 / DH).then_inc(g["made"].sem)

            @block.tensor
            def _(pe):
                pe.wait_ge(*g["made"](2))
                pe.wait_ge(g["load"].sem, 32)
                for k in range(2):
                    mm = pe.matmul(c.bank(0)[:, 0:P], ctx_mean[0:KC[k], :], cx[0:KC[k], k, :], start=(k == 0), stop=(k == 1))
                mm.then_inc(g["mean"].sem)
                pe.wait_ge(*g["sq"](1))
                for k in range(2):
                    mm = pe.matmul(c.bank(1)[:, 0:P], ctx_mean[0:KC[k], :], cs[0:KC[k], k, :], start=(k == 0), stop=(k == 1))
                mm.then_inc(g["var"].sem)
                pe.wait_ge(*g["out"](1))
                for m in range(FT):
                    for k in range(2):
                        mm = pe.matmul(c.bank(2)[:, m * P:(m + 1) * P], c.w("x_wkv", k, m * P, P, KC[k]), cx[0:KC[k], k, :],
                                       start=(k == 0), stop=(k == 1))
                mm.then_inc(g["k"].sem)
                for b in range(B):
                    for k in range(2):
                        mm = pe.matmul(c.bank(3)[0:KEYS, b * D:(b + 1) * D], cx[0:KC[k], k, b * KEYS:(b + 1) * KEYS],
                                       c.w("x_wkv", k, D, D, KC[k]), start=(k == 0), stop=(k == 1))
                mm.then_inc(g["v"].sem)
                pe.wait_ge(*g["square"](1))
                pe.matmul(c.bank(4)[:, 0:D], same_head[:], cs[:].rearrange("p m n -> p (m n)"), start=True, stop=True)\
                  .then_inc(g["ms"].sem)

            @block.scalar
            def _(act):
                act.wait_ge(*g["cent"](1))
                for k in range(2):
                    ins = act.activation(cs[0:KC[k], k, :], cx[0:KC[k], k, :], ACT.Square)
                ins.then_inc(g["sq"].sem)
                act.wait_ge(*g["var"](1))
                act.activation(cr[:, 0, :], c.bank(1)[:, 0:P], ACT.Ln, bias=c.eps[:, 0:1]).then_inc(g["log"].sem)
                act.wait_ge(*g["log"](1))
                act.activation(cr[:, 1, :], cr[:, 0, :], ACT.Exp, scale=-0.5).then_inc(g["rstd"].sem)
                act.wait_ge(*g["k"](1))
                act.activation(k_ctx[:].rearrange("p m n -> p (m n)"), c.bank(2)[:, 0:D], ACT.Copy).then_inc(g["raw"].sem)
                act.activation(cs[:].rearrange("p m n -> p (m n)"), c.bank(2)[:, 0:D], ACT.Square).then_inc(g["square"].sem)
                act.wait_ge(*g["ms_max"](1))
                act.activation(cr[:], cr[:], ACT.Ln).then_inc(g["ms_log"].sem)
                act.wait_ge(*g["ms_log"](1))
                act.activation(cr[:], cr[:], ACT.Exp, scale=-0.5).then_inc(g["inv"].sem)

            @block.vector
            def _(dve):
                dve.wait_ge(*g["mean"](1))
                for k in range(2):
                    ins = dve.tensor_tensor(cx[0:KC[k], k, :], cx[0:KC[k], k, :], c.bank(0)[0:KC[k], 0:P], ALU.subtract)
                ins.then_inc(g["cent"].sem)
                dve.wait_ge(*g["rstd"](1))
                for k in range(2):
                    ins = dve.scalar_tensor_tensor(out=cx[0:KC[k], k, :], in0=cx[0:KC[k], k, :], scalar=c.v("x_gx", k)[0:KC[k], :],
                                                   in1=cr[0:KC[k], 1, :], op0=ALU.mult, op1=ALU.mult)
                ins.then_inc(g["scaled"].sem)
                dve.wait_ge(*g["scaled"](1))
                for k in range(2):
                    ins = dve.tensor_scalar(cx[0:KC[k], k, :], cx[0:KC[k], k, :], c.v("x_bx", k)[0:KC[k], :], None, ALU.add)
                ins.then_inc(g["out"].sem)
                dve.tensor_copy(mask_add[:], mask_u8[:]).then_inc(g["mask"].sem)
                dve.wait_ge(*g["mask"](1))
                dve.tensor_scalar(mask_add[:], mask_add[:], -1.0, -NEG, ALU.add, ALU.mult).then_inc(g["mask2"].sem)
                dve.wait_ge(*g["v"](1))
                dve.tensor_copy(v_ctx_all[:].rearrange("p b n -> p (b n)"), c.bank(3)[0:KEYS, :]).then_inc(g["vc"].sem)
                dve.wait_ge(*g["ms"](1))
                dve.tensor_scalar(cr[:].rearrange("p m n -> p (m n)"), c.bank(4)[:, 0:D], 1e-16, None, ALU.max)\
                   .then_inc(g["ms_max"].sem)
                dve.wait_ge(*g["inv"](1))
                dve.scalar_tensor_tensor(out=k_ctx[:], in0=k_ctx[:], scalar=c.v("x_gk", 0), in1=cr[:],
                                         op0=ALU.mult, op1=ALU.mult).then_inc(g["kn"].sem)

        xn_all = c.spent_weights()
        norm_both(nc, c, norm_s, xn_all, lambda k: c.v("x_gl", k), lambda k: c.v("x_bl", k), twice=True)
        with nc.Fori(0, B) as b:
            set_round(b, s)
            x = lambda k, j: c.xT[:, k, bass.ds(b * S + j * CH, CH)]
            order = [("c", 0, 0)]
            for u in range(UNITS + 2):
                if u < UNITS:
                    order += [("p", u, 0), ("p", u, 1)]
                if (u + 2) % H == 0 and u + 2 < UNITS:
                    order.append(("c", (u + 2) // H, 0))
                if u >= 2 and (u - 2) % H == H - 1:
                    order.append(("o", (u - 2) // H, 0))
                if u < UNITS:
                    order.append(("p", u, 2))
            nth = {what: n for n, what in enumerate(order)}
            assert len(order) == TILES
            turn_bank = lambda what: c.bank(5 + nth[what] % 2)
            score = lambda u: c.psum[u % 2]
            out_bank = lambda qi: c.bank(4 if qi % 2 else 7)
            with nc.Block() as block:

                @block.gpsimd
                def _(pool):
                    pool.tensor_copy(ln, xn_all[:, :, bass.ds(b * S, S)]).then_inc(s["ln_in"].sem)

                @block.tensor
                def _(pe):
                    for name, base, first, done in (("x_wq", 0, 0, s["q_proj"]), ("x_wlkv", 4, 0, s["k_proj"])):
                        for m in range(FT):
                            for j in range(NCH):
                                for k in range(FT):
                                    mm = pe.matmul(c.bank(base + 2 * m + j), c.w(name, k, m * P, P),
                                                   xn_all[:, k, bass.ds(b * S + j * CH, CH)], start=(k == 0), stop=(k == 1))
                                mm.then_inc(done.sem)
                    for n in range(8):
                        pe.wait_ge(*s["square"](n + 1))
                        pe.wait_ge(*s["raw"](n + 1))
                        m, j = (n % 4) // 2, n % 2
                        pe.matmul(c.bank(n), same_head[:], scr[:, m, j * CH:(j + 1) * CH] if n < 4 else
                                  v[:, m, j * CH:(j + 1) * CH], start=True, stop=True).then_inc(s["ms"].sem)
                    for t2 in range(4):
                        if t2 == 0:
                            pe.wait_ge(*s["ms_max"](8))
                            pe.wait_ge(*s["ln_in"](1))
                        for t in (0, 1):
                            for k in range(FT):
                                mm = pe.matmul(c.bank(t2)[:, t * D:(t + 1) * D], ln[:, k, (2 * t2 + t) * P:(2 * t2 + t + 1) * P],
                                               c.w("x_wlkv", k, D, D), start=(k == 0), stop=(k == 1))
                        mm.then_inc(s["v_proj"].sem)

                    def scores(u):
                        qi, h = divmod(u, H)
                        m, at = h // HP, (h % HP) * DH
                        if u == 0:
                            pe.wait_ge(*s["scaled"](8))
                            pe.wait_ge(*s["v_copied"](4))
                        if h == 0:
                            n = nth["c", qi, 0]
                            half = turn_bank(("c", qi, 0))[:, 0:D]
                            if n >= 2:
                                pe.wait_ge(*s["copied"](n - 1))
                            pe.matmul(half, c.ident[:], mask_sel[:], start=True, stop=False)
                            for i in range(FT):
                                mm = pe.matmul(half[:, i * P:(i + 1) * P], qt[:, i, qi * P:(qi + 1) * P],
                                               k_ctx_now[:, i, :], start=False, stop=(i == 1))
                            mm.then_inc(s["turned"].sem)
                        if u >= 2:
                            pe.wait_ge(*s["expd"](u - 1))
                        for j in range(NCH):
                            mm = pe.matmul(score(u)[:, j * CH:(j + 1) * CH], qt[at:at + DH, m, qi * P:(qi + 1) * P],
                                           kt[at:at + DH, m, j * CH:(j + 1) * CH], start=True, stop=True)
                        mm.then_inc(s["scores"].sem)

                    def turn(u, i):
                        n = nth["p", u, i]
                        pe.wait_ge(*s["expd"](u + 1))
                        if u == 0:
                            pe.wait_ge(*s["padded"](1))
                        if n >= 2:
                            pe.wait_ge(*s["copied"](n - 1))
                        blocks = range(4 * i, min(4 * i + 4, NB))
                        for kb in blocks:
                            mm = pe.transpose(turn_bank(("p", u, i))[:, (kb % 4) * P:(kb % 4 + 1) * P],
                                              probs[u % 2][:, kb * P:(kb + 1) * P], c.ident[:])
                        mm.then_inc(s["turned"].sem)

                    def turn_outputs(qi):
                        n = nth["o", qi, 0]
                        pe.wait_ge(*s["normed"](qi + 1))
                        pe.wait_ge(*s["copied"](n - 1))
                        for m in range(FT):
                            mm = pe.transpose(turn_bank(("o", qi, 0))[:, m * P:(m + 1) * P], o[:, qi % 2, m * P:(m + 1) * P], c.ident[:])
                        mm.then_inc(s["turned"].sem)

                    def values(u):
                        qi, h = divmod(u, H)
                        pe.wait_ge(*s["copied"](nth["p", u, 2] + 1))
                        if h == 0 and qi >= 2:
                            pe.wait_ge(*s["normed"](qi - 1))
                        out = out_bank(qi)[:, h * DH:(h + 1) * DH]
                        for kb in range(TT):
                            pe.matmul(out, turned[u % 2][:, kb, :], v_t[:, kb, h * DH:(h + 1) * DH], start=(kb == 0), stop=False)
                        pe.matmul(out, turned[u % 2][0:KEYS, TT, :], v_ctx[:, h * DH:(h + 1) * DH], start=False, stop=True)\
                          .then_inc(s["av"].sem)

                    pe.wait_ge(*s["ctx_v"](1))
                    scores(0)
                    scores(1)
                    for u in range(UNITS + 2):
                        if u < UNITS:
                            turn(u, 0)
                            turn(u, 1)
                        if u + 2 < UNITS:
                            scores(u + 2)
                        if u >= 2 and (u - 2) % H == H - 1:
                            turn_outputs((u - 2) // H)
                        if 1 <= u <= UNITS:
                            values(u - 1)
                        if u < UNITS:
                            turn(u, 2)
                    pe.wait_ge(*s["copied"](TILES))
                    for m in range(FT):
                        for j in range(NCH):
                            for k in range(FT):
                                mm = pe.matmul(c.bank(2 * m + j), c.w("x_wo", k, m * P, P), ot[:, k, j * CH:(j + 1) * CH],
                                               start=(k == 0), stop=(k == 1))
                            mm.then_inc(s["o_done"].sem)

                @block.scalar
                def _(act):
                    for n in range(8):
                        m, j = (n % 4) // 2, n % 2
                        done = s["q_proj"] if n < 4 else s["k_proj"]
                        act.wait_ge(*done(n % 4 + 1))
                        act.activation((qt if n < 4 else kt)[:, m, j * CH:(j + 1) * CH], c.bank(n), ACT.Copy).then_inc(s["raw"].sem)
                        act.activation((scr if n < 4 else v)[:, m, j * CH:(j + 1) * CH], c.bank(n), ACT.Square)\
                           .then_inc(s["square"].sem)
                    for f, ready, done in ((ACT.Ln, s["ms_max"], s["ms_log"]), (ACT.Exp, s["ms_log"], s["inv"])):
                        for n in range(8):
                            m, j = (n % 4) // 2, n % 2
                            act.wait_ge(*ready(n + 1))
                            half = (inv if n < 4 else scr)[:, m, j * CH:(j + 1) * CH]
                            act.activation(half, half, f, scale=1.0 if f == ACT.Ln else -0.5).then_inc(done.sem)

                    def exps(u):
                        qi, h = divmod(u, H)
                        act.wait_ge(*s["shift"](u + 1))
                        if u == 0:
                            act.wait_ge(*s["scaled"](8))
                        if u >= 2:
                            act.wait_ge(*s["turned"](nth["p", u - 2, 2] + 1))
                        act.activation(probs[u % 2][:, 0:S], score(u)[:], ACT.Exp, bias=nm[:, u % 2:u % 2 + 1], scale=SCALE,
                                       accum_out=rs[:, qi % 2, h, 0:1])
                        act.activation(probs[u % 2][:, S:S + KEYS], ctx_s[:, qi % 2, h * KEYS:(h + 1) * KEYS],
                                       ACT.Exp, bias=nm[:, u % 2:u % 2 + 1], scale=SCALE,
                                       accum_out=rs[:, qi % 2, h, 1:2]).then_inc(s["expd"].sem)

                    for u in range(UNITS):
                        exps(u)

                @block.vector
                def _(dve):
                    for h in range(HP):
                        dve.tensor_copy(k_ctx_now[h * DH:(h + 1) * DH, :, h * KEYS:(h + 1) * KEYS],
                                        k_ctx[h * DH:(h + 1) * DH, :, bass.ds(b * KEYS, KEYS)])
                    for h in range(H):
                        dve.tensor_copy(mask_sel[:, h * KEYS:(h + 1) * KEYS], mask_add[:, bass.ds(b * KEYS, KEYS)])
                    dve.tensor_copy(v_ctx[:], v_ctx_all[:].rearrange("p b n -> p (b n)")[:, bass.ds(b * D, D)]).then_inc(s["ctx_v"].sem)
                    for n in range(8):
                        m, j = (n % 4) // 2, n % 2
                        dve.wait_ge(*s["ms"](n + 1))
                        if n == 4:
                            dve.wait_ge(*s["ms"](8))
                        dve.tensor_scalar((inv if n < 4 else scr)[:, m, j * CH:(j + 1) * CH], c.bank(n), 1e-16, None, ALU.max)\
                           .then_inc(s["ms_max"].sem)
                    for t2 in range(4):
                        dve.wait_ge(*s["v_proj"](t2 + 1))
                        dve.tensor_copy(v_t[:, 2 * t2:2 * t2 + 2, :].rearrange("p t n -> p (t n)"), c.bank(t2)).then_inc(s["v_copied"].sem)
                    for n in range(8):
                        m, j = (n % 4) // 2, n % 2
                        dve.wait_ge(*s["inv"](n + 1))
                        t = (qt if n < 4 else kt)[:, m, j * CH:(j + 1) * CH]
                        dve.scalar_tensor_tensor(out=t, in0=t, scalar=c.v("x_gq" if n < 4 else "x_gk", 0),
                                                 in1=(inv if n < 4 else scr)[:, m, j * CH:(j + 1) * CH],
                                                 op0=ALU.mult, op1=ALU.mult).then_inc(s["scaled"].sem)

                    def shift(u):
                        qi, h = divmod(u, H)
                        if h == 0:
                            dve.wait_ge(*s["turned"](nth["c", qi, 0] + 1))
                            if qi >= 2:
                                dve.wait_ge(*s["expd"](H * (qi - 1)))
                            bank = turn_bank(("c", qi, 0))[:, 0:D]
                            dve.tensor_reduce(mxc[:, qi % 2, :], bank.rearrange("p (h n) -> p h n", h=H), AX, ALU.max)\
                               .then_inc(s["ctx_max"].sem)
                            dve.tensor_copy(ctx_s[:, qi % 2, :], bank).then_inc(s["copied"].sem)
                            dve.wait_ge(*s["ctx_max"](qi + 1))
                        dve.wait_ge(*s["scores"](u + 1))
                        dve.tensor_reduce(mx[:, u % 2:u % 2 + 1], score(u)[:], AX, ALU.max).then_inc(s["row_max"].sem)
                        dve.wait_ge(*s["row_max"](u + 1))
                        dve.tensor_scalar(nm[:, u % 2:u % 2 + 1], mx[:, u % 2:u % 2 + 1], mxc[:, qi % 2, h:h + 1], -SCALE,
                                          ALU.max, ALU.mult).then_inc(s["shift"].sem)

                    def copy_turned(u, i):
                        n = nth["p", u, i]
                        dve.wait_ge(*s["turned"](n + 1))
                        if u >= 2 and i == 0:
                            dve.wait_ge(*s["av"](u - 1))
                        blocks = range(4 * i, min(4 * i + 4, NB))
                        rows = P if i < 2 else KEYS
                        dve.tensor_copy(turned[u % 2][0:rows, blocks[0]:blocks[-1] + 1, :].rearrange("p k n -> p (k n)"),
                                        turn_bank(("p", u, i))[0:rows, 0:len(blocks) * P]).then_inc(s["copied"].sem)

                    def copy_outputs(qi):
                        n = nth["o", qi, 0]
                        dve.wait_ge(*s["turned"](n + 1))
                        dve.tensor_copy(ot[:, :, qi * P:(qi + 1) * P], turn_bank(("o", qi, 0))[:, 0:D].rearrange("p (m n) -> p m n", m=FT))\
                           .then_inc(s["copied"].sem)

                    def norm(qi):
                        dve.wait_ge(*s["av"](H * (qi + 1)))
                        dve.wait_ge(*s["expd"](H * (qi + 1)))
                        dve.tensor_reduce(rr[:, qi % 2, :], rs[:, qi % 2, :, :], AX, ALU.add).then_inc(s["den"].sem)
                        dve.wait_ge(*s["den"](qi + 1))
                        dve.reciprocal(rr[:, qi % 2, :], rr[:, qi % 2, :]).then_inc(s["den_inv"].sem)
                        dve.wait_ge(*s["den_inv"](qi + 1))
                        dve.tensor_tensor(o[:, qi % 2, :].rearrange("p (h d) -> p h d", h=H),
                                          out_bank(qi)[:, 0:D].rearrange("p (h d) -> p h d", h=H),
                                          rr[:, qi % 2, :].unsqueeze(2).to_broadcast([P, H, DH]), ALU.mult).then_inc(s["normed"].sem)

                    dve.wait_ge(*s["scaled"](8))
                    for i in range(2):
                        ins = dve.memset(probs[i][:, S + KEYS:], 0.0)
                    ins.then_inc(s["padded"].sem)
                    shift(0)
                    shift(1)
                    for u in range(UNITS + 2):
                        if u < UNITS:
                            copy_turned(u, 0)
                            copy_turned(u, 1)
                        if u + 2 < UNITS:
                            shift(u + 2)
                        if u >= 2 and (u - 2) % H == H - 1:
                            copy_outputs((u - 2) // H)
                        if 1 <= u <= UNITS and (u - 1) % H == H - 1:
                            norm((u - 1) // H)
                        if u < UNITS:
                            copy_turned(u, 2)
                    for m in range(FT):
                        for j in range(NCH):
                            dve.wait_ge(*s["o_done"](2 * m + j + 1))
                            dve.scalar_tensor_tensor(out=x(m, j), in0=c.bank(2 * m + j), scalar=c.v("x_bo", m),
                                                     in1=x(m, j), op0=ALU.add, op1=ALU.add).then_inc(s["x_done"].sem)
        clear_signals(nc, norm_s, s, g)


def gated_recurrence_layer(nc, c):
    GATES = (("f_wf", "f_uf", "f_bf"), ("f_wi", "f_ui", "f_bi"), ("f_wc", "f_uc", "f_bc"))
    NG = len(GATES)
    N = NG * FT * NCH
    with ExitStack() as ctx:
        ln = signals(nc, ctx, "fn", norm_signals())
        s = signals(nc, ctx, "f", dict(gate_in=N, gate=N, fed=4, kept=4, cell=4))
        s2 = signals(nc, ctx, "f2", dict(o_done=4, tanh=4, x_done=4))
        first = ctx.enter_context(nc.semaphore("f_first_cell"))
        xn_all = c.spent_weights()
        cell, fed = c.slot(1), c.slot(5)
        gates = [c.slot(i) for i in (2, 3, 4)]
        norm_both(nc, c, ln, xn_all)
        with nc.Block() as block:

            @block.vector
            def _(dve):
                dve.memset(cell, 0.0).then_inc(first)
                dve.wait_ge(first, 1)
                for k in range(FT):
                    dve.tensor_scalar(cell[:, k, :], cell[:, k, :], c.v("f_c0", k), None, ALU.add)

        with nc.Fori(0, B) as b:
            set_round(b, s)
            with nc.Block() as block:

                @block.tensor
                def _(pe):
                    n = 0
                    for j in range(NCH):
                        for m in range(FT):
                            for w, u, _ in GATES:
                                if n >= 8:
                                    pe.wait_ge(*s["gate"](n - 7))
                                for k in range(FT):
                                    pe.matmul(c.bank(n % 8), c.w(w, k, m * P, P), xn_all[:, k, bass.ds(b * S + j * CH, CH)],
                                              start=(k == 0), stop=False)
                                for k in range(FT):
                                    mm = pe.matmul(c.bank(n % 8), c.w(u, k, m * P, P), cell[:, k, j * CH:(j + 1) * CH],
                                                   start=False, stop=(k == 1))
                                mm.then_inc(s["gate_in"].sem)
                                n += 1

                @block.scalar
                def _(act):
                    n = 0
                    for j in range(NCH):
                        for m in range(FT):
                            for i, (_, _, bias) in enumerate(GATES):
                                act.wait_ge(*s["gate_in"](n + 1))
                                act.activation(gates[i][:, m, j * CH:(j + 1) * CH], c.bank(n % 8),
                                               ACT.Tanh if i == 2 else ACT.Sigmoid, bias=c.v(bias, m)).then_inc(s["gate"].sem)
                                n += 1

                @block.vector
                def _(dve):
                    f, i, g = gates
                    for j in range(NCH):
                        dve.wait_ge(*s["gate"](NG * FT * (j + 1)))
                        for m in range(FT):
                            at = lambda t: t[:, m, j * CH:(j + 1) * CH]
                            n = FT * j + m + 1
                            dve.tensor_tensor(at(fed), at(i), at(g), ALU.mult).then_inc(s["fed"].sem)
                            dve.tensor_tensor(at(cell), at(f), at(cell), ALU.mult).then_inc(s["kept"].sem)
                            dve.wait_ge(*s["fed"](n))
                            dve.wait_ge(*s["kept"](n))
                            dve.tensor_tensor(at(cell), at(cell), at(fed), ALU.add).then_inc(s["cell"].sem)

        with nc.Fori(0, B) as b:
            set_round(b, s2)
            with nc.Block() as block:

                @block.tensor
                def _(pe):
                    for m in range(FT):
                        for j in range(NCH):
                            for k in range(FT):
                                pe.matmul(c.bank(2 * m + j), c.w("f_wo", k, m * P, P), xn_all[:, k, bass.ds(b * S + j * CH, CH)],
                                          start=(k == 0), stop=False)
                            for k in range(FT):
                                mm = pe.matmul(c.bank(2 * m + j), c.w("f_uo", k, m * P, P), cell[:, k, j * CH:(j + 1) * CH],
                                               start=False, stop=(k == 1))
                            mm.then_inc(s2["o_done"].sem)

                @block.scalar
                def _(act):
                    for n in range(FT * NCH):
                        act.wait_ge(*s2["o_done"](n + 1))
                        m, j = divmod(n, NCH)
                        act.activation(fed[:, m, j * CH:(j + 1) * CH], c.bank(n), ACT.Tanh, bias=c.v("f_bo", m)).then_inc(s2["tanh"].sem)

                @block.vector
                def _(dve):
                    for n in range(FT * NCH):
                        dve.wait_ge(*s2["tanh"](n + 1))
                        m, j = divmod(n, NCH)
                        xs = c.xT[:, m, bass.ds(b * S + j * CH, CH)]
                        dve.tensor_tensor(xs, xs, fed[:, m, j * CH:(j + 1) * CH], ALU.add).then_inc(s2["x_done"].sem)
        clear_signals(nc, ln, s, s2, also=[first])


class Unit:

    def __init__(self, heads, qi):
        self.heads, self.qi, self.keys = heads, qi, (qi + 1) * P
        self.pitch = CH if len(heads) == 2 else self.keys
        self.blocks = [(i, kb) for i in range(len(heads)) for kb in range(qi + 1)]

    def spread(self, ap):
        return ap[:, 0:self.pitch * len(self.heads)].rearrange("p (h n) -> p h n", n=self.pitch)[:, :, 0:self.keys]


def causal_attention_layer(nc, c):
    H, DH = 16, 16
    SCALE = DH ** -0.5
    QPART = (0, 0, 0, 1, 1, 1, 2, 2)
    KPART = (0, 1, 2, 0, 1, 2, 0, 1)
    QUAD = 4
    QUADS = H // QUAD
    WIDE = QUAD * DH
    LOADS = 16
    units, last_of_quad = [], []
    for first in range(0, H, QUAD):
        heads = list(range(first, first + QUAD))
        units += [Unit(heads, 0), Unit(heads, 1)]
        units += [Unit(heads[i:i + 2], qi) for qi in (2, 3) for i in (0, 2)]
        units += [Unit([h], qi) for h in heads for qi in range(4, TT)]
        last_of_quad.append(len(units))
    U = len(units)
    more = [u for u in range(U) if len(units[u].blocks) > 4]
    nth2 = {u: n for n, u in enumerate(more)}
    with ExitStack() as ctx:
        norm_s = signals(nc, ctx, "bn", norm_signals())
        pr = signals(nc, ctx, "bp", dict(q_proj=4, k_proj=4, v_proj=4, q_raw=4, k_raw=4, v_copied=4, part=6, rest=4,
                                         stored=6 * 16))
        s = signals(nc, ctx, "b", dict(
            loaded0=LOADS * 16 * QUADS // 2, loaded1=LOADS * 16 * QUADS // 2,
            scores=U, row_max=U, shift=U, expd=U, turned1=U + TT // 2, copied1=U + TT // 2,
            turned2=len(more) + TT // 2, copied2=len(more) + TT // 2,
            av=U, den_inv=U, normed=U, o_done=4, x_done=4))
        loaded = [s["loaded0"], s["loaded1"]]
        made = ctx.enter_context(nc.semaphore("b_made"))
        sb = lambda name, shape, dt=F32: ctx.enter_context(nc.sbuf_tensor(name, shape, dt))
        ident16 = sb("b_ident16", [P, P], BF16)
        future = sb("b_future", [P, P], BF16)
        q_parts = sb("b_q_parts", [P, 3, FT, S], BF16)
        k_parts = sb("b_k_parts", [P, 3, FT, S], BF16)
        q_stack = sb("b_q_stack", [P, 2, QUAD, S], BF16)
        k_stack = sb("b_k_stack", [P, 2, QUAD, S], BF16)
        rs = sb("b_rs", [P, 4, QUAD])
        mx = sb("b_mx", [P, 4, QUAD])
        nm = sb("b_nm", [P, 4, QUAD])
        q_dram = nc.dram_tensor("b_q_dram", (B, 3, D, S), BF16, kind="Internal").ap()
        k_dram = nc.dram_tensor("b_k_dram", (B, 3, D, S), BF16, kind="Internal").ap()
        xn_all = c.spent_weights()
        ot, o = c.slot(0), c.slot(1)
        v_all = c.arena[:, 4 * FT * S:]
        o_t = o.rearrange("p a n -> p (a n)").rearrange("p (t n) -> p t n", t=TT)
        half = lambda i: c.arena[:, 2 * 2048 + i * S:2 * 2048 + (i + 1) * S]
        probs = [half(0), half(1)]
        turned = [half(i).rearrange("p (k n) -> p k n", k=TT) for i in (2, 3)]
        stack_at = lambda h: ((h // QUAD) % 2, h % QUAD)
        with nc.Block() as block:

            @block.gpsimd
            def _(pool):
                pool.tensor_copy(ident16[:], c.ident[:])
                pool.memset(future[:], 0.0).then_inc(made)
                pool.wait_ge(made, 1)
                pool.affine_select(out=future[:], in_=future[:], compare_op=ALU.is_ge, fill=NEG, base=0,
                                   pattern=[[-1, P]], channel_multiplier=1)

        norm_both(nc, c, norm_s, xn_all)

        v_tiles = v_all.rearrange("p (t n) -> p t n", t=B * TT)
        spare = lambda t: t[:].rearrange("p a r n -> p (a r n)")[:, 0:3 * FT * S]\
            .rearrange("p (a m n) -> p a m n", a=3, m=FT)
        parts_of = ((q_parts[:], k_parts[:]), (spare(q_stack), spare(k_stack)))
        raw_of = ((c.slot(0), c.slot(1)), (c.slot(2), c.slot(3)))
        with nc.Block() as block:

            @block.sync
            def _(sync):
                for b in range(B):
                    set_round(b, pr)
                    for i in range(3):
                        for n, dram in enumerate((q_dram, k_dram)):
                            sync.wait_ge(*pr["part"](2 * i + n + 1))
                            sync.dma_start(dram[b, i].rearrange("(m p) n -> p m n", p=P), parts_of[b][n][:, i, :, :])\
                                .then_inc(pr["stored"].sem, 16)
                sync.wait_ge(pr["stored"].sem, B * 6 * 16)

            @block.tensor
            def _(pe):
                for b in range(B):
                    set_round(b, pr)
                    xn = lambda k, first, n: xn_all[:, k, b * S + first:b * S + first + n]
                    for name, base, done in (("b_wq", 0, pr["q_proj"]), ("b_wk", 4, pr["k_proj"])):
                        for n in range(4):
                            m, j = divmod(n, NCH)
                            if b:
                                pe.wait_ge(*pr["k_raw" if base else "v_copied"](n + 1 - 4))
                            for k in range(FT):
                                mm = pe.matmul(c.bank(base + n), c.w(name, k, m * P, P), xn(k, j * CH, CH),
                                               start=(k == 0), stop=(k == 1))
                            mm.then_inc(done.sem)
                    for t2 in range(4):
                        pe.wait_ge(*pr["q_raw"](t2 + 1))
                        for t in (0, 1):
                            for k in range(FT):
                                mm = pe.matmul(c.bank(t2)[:, t * D:(t + 1) * D], xn(k, (2 * t2 + t) * P, P),
                                               c.w("b_wv", k, 0, D), start=(k == 0), stop=(k == 1))
                        mm.then_inc(pr["v_proj"].sem)

            @block.scalar
            def _(act):
                for b in range(B):
                    set_round(b, pr)
                    for t, bias, ready, done, base in ((raw_of[b][0], "b_bq", pr["q_proj"], pr["q_raw"], 0),
                                                       (raw_of[b][1], "b_bk", pr["k_proj"], pr["k_raw"], 4)):
                        for n in range(4):
                            m, j = divmod(n, NCH)
                            act.wait_ge(*ready(n + 1))
                            act.activation(t[:, m, j * CH:(j + 1) * CH], c.bank(base + n), ACT.Identity, bias=c.v(bias, m))\
                               .then_inc(done.sem)
                    for i in range(3):
                        for n in range(2):
                            if i == 0:
                                act.wait_ge(*pr["k_raw" if n else "q_raw"](4))
                            else:
                                act.wait_ge(*pr["rest"](2 * (i - 1) + n + 1))
                            act.activation(parts_of[b][n][:, i, :, :], raw_of[b][n], ACT.Copy).then_inc(pr["part"].sem)

            @block.vector
            def _(dve):
                for b in range(B):
                    set_round(b, pr)
                    for t2 in range(4):
                        dve.wait_ge(*pr["v_proj"](t2 + 1))
                        dve.tensor_copy(v_tiles[:, b * TT + 2 * t2:b * TT + 2 * t2 + 2, :].rearrange("p t n -> p (t n)"),
                                        c.bank(t2)).then_inc(pr["v_copied"].sem)
                    for i in range(2):
                        for n in range(2):
                            dve.wait_ge(*pr["part"](2 * i + n + 1))
                            dve.tensor_tensor(raw_of[b][n], raw_of[b][n], parts_of[b][n][:, i, :, :], ALU.subtract)\
                               .then_inc(pr["rest"].sem)

        with nc.Fori(0, B) as b:
            set_round(b, s)
            x = lambda k, j: c.xT[:, k, bass.ds(b * S + j * CH, CH)]
            turn_bank = lambda i: c.bank(5 + i)
            score = lambda u: c.psum[u % 2]
            out_bank = lambda u: c.bank(4 if u % 2 else 7)
            with nc.Block() as block:

                @block.sync
                def _(sync):
                    q_now, k_now = (t[bass.ds(b, 1)].rearrange("b a f n -> (b a) f n") for t in (q_dram, k_dram))
                    for quad in range(QUADS):
                        if quad >= 2:
                            sync.wait_ge(*s["scores"](last_of_quad[quad - 2]))
                        at = quad % 2
                        by_head = lambda ap: ap.rearrange("a (h d) n -> a d h n", d=DH)
                        rows = slice(quad * QUAD * DH, (quad + 1) * QUAD * DH)
                        for i in range(3):
                            first, n = QPART.index(i) * DH, QPART.count(i)
                            for r in range(n):
                                sync.dma_start(q_stack[first + r * DH:first + (r + 1) * DH, at, :, :],
                                               by_head(q_now[i:i + 1, rows, :])[0]).then_inc(loaded[at].sem, 16)
                        for r, i in enumerate(KPART):
                            sync.dma_start(k_stack[r * DH:(r + 1) * DH, at, :, :],
                                           by_head(k_now[i:i + 1, rows, :])[0]).then_inc(loaded[at].sem, 16)

                @block.tensor
                def _(pe):
                    def scores(u):
                        unit = units[u]
                        if u == 0 or u in last_of_quad:
                            quad = unit.heads[0] // QUAD
                            pe.wait_ge(*loaded[quad % 2](LOADS * 16 * (quad // 2 + 1)))
                        if u >= 2:
                            pe.wait_ge(*s["expd"](u - 1))
                        for i, h in enumerate(unit.heads):
                            a, r = stack_at(h)
                            for first in range(0, unit.keys, CH):
                                n = min(CH, unit.keys - first)
                                last = first + n == unit.keys
                                at = i * unit.pitch + first
                                pe.matmul(score(u)[:, at:at + n], q_stack[:, a, r, unit.qi * P:(unit.qi + 1) * P],
                                          k_stack[:, a, r, first:first + n], start=True, stop=not last)
                            at = i * unit.pitch + unit.qi * P
                            mm = pe.matmul(score(u)[:, at:at + P], ident16[:], future[:], start=False, stop=True)
                        mm.then_inc(s["scores"].sem)

                    def turn(u):
                        unit = units[u]
                        pe.wait_ge(*s["expd"](u + 1))
                        for n, (i, kb) in enumerate(unit.blocks):
                            tile = n // 4
                            if n == 0 and u >= 1:
                                pe.wait_ge(*s["copied1"](u))
                            if n == 4 and nth2[u] >= 1:
                                pe.wait_ge(*s["copied2"](nth2[u]))
                            mm = pe.transpose(turn_bank(tile)[:, (n % 4) * P:(n % 4 + 1) * P],
                                              probs[u % 2][:, i * unit.pitch + kb * P:i * unit.pitch + (kb + 1) * P], c.ident[:])
                            if n == 3:
                                mm.then_inc(s["turned1"].sem)
                        if u in nth2:
                            mm.then_inc(s["turned2"].sem)

                    def values(u):
                        unit = units[u]
                        pe.wait_ge(*s["copied1"](u + 1))
                        if u in nth2:
                            pe.wait_ge(*s["copied2"](nth2[u] + 1))
                        if u >= 2:
                            pe.wait_ge(*s["normed"](u - 1))
                        for n, (i, kb) in enumerate(unit.blocks):
                            h = unit.heads[i]
                            first = h // QUAD * WIDE
                            mm = pe.matmul(out_bank(u)[:, i * WIDE:(i + 1) * WIDE], turned[u % 2][:, n, :],
                                           v_all[:, bass.ds(b * (TT * D) + kb * D + first, WIDE)], start=(kb == 0), stop=(kb == unit.qi))
                        mm.then_inc(s["av"].sem)

                    scores(0)
                    scores(1)
                    for u in range(U + 1):
                        if u < U:
                            turn(u)
                        if u + 2 < U:
                            scores(u + 2)
                        if u >= 1:
                            values(u - 1)
                    pe.wait_ge(*s["normed"](U))
                    for qi in range(TT):
                        i, n = qi % 2, qi // 2
                        pe.wait_ge(*(s["copied2"](len(more) + n) if i else s["copied1"](U + n)))
                        for m in range(FT):
                            mm = pe.transpose(turn_bank(i)[:, m * P:(m + 1) * P], o_t[:, qi, m * P:(m + 1) * P], c.ident[:])
                        mm.then_inc((s["turned2"] if i else s["turned1"]).sem)
                    pe.wait_ge(*s["copied1"](U + TT // 2))
                    pe.wait_ge(*s["copied2"](len(more) + TT // 2))
                    for m in range(FT):
                        for j in range(NCH):
                            for k in range(FT):
                                mm = pe.matmul(c.bank(2 * m + j), c.w("b_wo", k, m * P, P), ot[:, k, j * CH:(j + 1) * CH],
                                               start=(k == 0), stop=(k == 1))
                            mm.then_inc(s["o_done"].sem)

                @block.scalar
                def _(act):
                    def exps(u):
                        unit = units[u]
                        act.wait_ge(*s["shift"](u + 1))
                        if u >= 2:
                            act.wait_ge(*(s["turned2"](nth2[u - 2] + 1) if u - 2 in nth2 else s["turned1"](u - 1)))
                        if u >= 4:
                            act.wait_ge(*s["normed"](u - 3))
                        for i in range(len(unit.heads)):
                            at = slice(i * unit.pitch, i * unit.pitch + unit.keys)
                            ins = act.activation(probs[u % 2][:, at], score(u)[:, at], ACT.Exp, bias=nm[:, u % 4, i:i + 1],
                                                 scale=SCALE, accum_out=rs[:, u % 4, i:i + 1])
                        ins.then_inc(s["expd"].sem)

                    exps(0)
                    exps(1)
                    for u in range(U):
                        if u in nth2:
                            act.wait_ge(*s["turned2"](nth2[u] + 1))
                            if u >= 2:
                                act.wait_ge(*s["av"](u - 1))
                            n = len(units[u].blocks)
                            act.activation(turned[u % 2][:, 4:n, :].rearrange("p k n -> p (k n)"), turn_bank(1)[:, 0:(n - 4) * P],
                                           ACT.Copy).then_inc(s["copied2"].sem)
                        if u + 2 < U:
                            exps(u + 2)
                    for n in range(TT // 2):
                        act.wait_ge(*s["turned2"](len(more) + n + 1))
                        for m in range(FT):
                            ins = act.activation(ot[:, m, (2 * n + 1) * P:(2 * n + 2) * P], turn_bank(1)[:, m * P:(m + 1) * P],
                                                 ACT.Identity, bias=c.v("b_bv", m))
                        ins.then_inc(s["copied2"].sem)

                @block.vector
                def _(dve):
                    def shift(u):
                        unit = units[u]
                        nh = len(unit.heads)
                        dve.wait_ge(*s["scores"](u + 1))
                        if u >= 4:
                            dve.wait_ge(*s["expd"](u - 3))
                        dve.tensor_reduce(mx[:, u % 4, 0:nh], unit.spread(score(u)), AX, ALU.max).then_inc(s["row_max"].sem)
                        dve.wait_ge(*s["row_max"](u + 1))
                        dve.tensor_scalar(nm[:, u % 4, 0:nh], mx[:, u % 4, 0:nh], -SCALE, None, ALU.mult).then_inc(s["shift"].sem)

                    def copy_turned(u):
                        dve.wait_ge(*s["turned1"](u + 1))
                        if u >= 2:
                            dve.wait_ge(*s["av"](u - 1))
                        dve.tensor_copy(turned[u % 2][:, 0:4, :].rearrange("p k n -> p (k n)"), turn_bank(0)).then_inc(s["copied1"].sem)

                    def norm(u):
                        unit = units[u]
                        nh, h0 = len(unit.heads), unit.heads[0]
                        dve.wait_ge(*s["expd"](u + 1))
                        dve.reciprocal(rs[:, u % 4, 0:nh], rs[:, u % 4, 0:nh]).then_inc(s["den_inv"].sem)
                        dve.wait_ge(*s["den_inv"](u + 1))
                        dve.wait_ge(*s["av"](u + 1))
                        first, step = h0 % QUAD * DH, WIDE + DH
                        own = out_bank(u)[:, first:first + nh * step].rearrange("p (h d) -> p h d", h=nh)[:, :, 0:DH]
                        dve.tensor_tensor(o_t[:, unit.qi, h0 * DH:(h0 + nh) * DH].rearrange("p (h d) -> p h d", h=nh), own,
                                          rs[:, u % 4, 0:nh].unsqueeze(2).to_broadcast([P, nh, DH]), ALU.mult).then_inc(s["normed"].sem)

                    shift(0)
                    shift(1)
                    for u in range(U + 2):
                        if u < U:
                            copy_turned(u)
                        if u + 2 < U:
                            shift(u + 2)
                        if u >= 2:
                            norm(u - 2)
                    for n in range(TT // 2):
                        dve.wait_ge(*s["turned1"](U + n + 1))
                        for m in range(FT):
                            ins = dve.tensor_scalar(ot[:, m, 2 * n * P:(2 * n + 1) * P], turn_bank(0)[:, m * P:(m + 1) * P],
                                                    c.v("b_bv", m), None, ALU.add)
                        ins.then_inc(s["copied1"].sem)
                    for m in range(FT):
                        for j in range(NCH):
                            dve.wait_ge(*s["o_done"](2 * m + j + 1))
                            dve.scalar_tensor_tensor(out=x(m, j), in0=c.bank(2 * m + j), scalar=c.v("b_bo", m),
                                                     in1=x(m, j), op0=ALU.add, op1=ALU.add).then_inc(s["x_done"].sem)
        clear_signals(nc, norm_s, pr, s, also=[made])


def context_attention_layer(nc, c):
    H, DH = 16, 16
    SCALE = DH ** -0.5
    HT8 = H // FT
    PAIRS = H // 2
    KC = [P, CF - P]
    with ExitStack() as ctx:
        norm_s = signals(nc, ctx, "yn", norm_signals())
        s = signals(nc, ctx, "y", dict(
            q_proj=4, q_raw=4, scores=TT, row_max=TT, shifted=TT, expd=TT,
            den=TT, den_inv=TT, turned=3 * TT, copied=3 * TT, av=TT, normed=TT, o_done=4, x_done=4))
        g = signals(nc, ctx, "yc", dict(load=1, made=3, k=1, v=1, kb=1, out=1))
        set_round(0, g)
        sb = lambda name, shape, dt=F32: ctx.enter_context(nc.sbuf_tensor(name, shape, dt))
        of_head = sb("y_of_head", [P, HT8])
        cx = sb("y_cx", [P, 2, B * KEYS])
        kc = sb("y_kc", [P, FT, B * KEYS])
        k_diag = sb("y_k_diag", [P, B, FT, CH])
        v_diag = sb("y_v_diag", [P, B, PAIRS, 2 * DH])
        mx = sb("y_mx", [P, 2, H])
        rs = sb("y_rs", [P, 2, H])
        o = sb("y_o", [P, 2, D])
        xn_all, q, ot = c.spent_weights(), c.slot(1), c.slot(4)
        quarter = lambda first, i: c.arena[:, first * 2048 + i * S:first * 2048 + (i + 1) * S]
        probs = [quarter(2, 0), quarter(2, 1)]
        turned = [quarter(3, i).rearrange("p (k n) -> p k n", k=PAIRS) for i in range(2)]
        with nc.Block() as block:

            @block.sync
            def _(sync):
                sync.dma_start(cx[:], c.ctx_t).then_inc(g["load"].sem, 16)

            @block.gpsimd
            def _(pool):
                pool.memset(v_diag[:], 0.0).then_inc(g["made"].sem)
                pool.memset(of_head[:], 1.0).then_inc(g["made"].sem)
                pool.wait_ge(*g["made"](2))
                pool.affine_select(out=of_head[:], in_=of_head[:], compare_op=ALU.is_ge, fill=0.0, base=0,
                                   pattern=[[-DH, HT8]], channel_multiplier=1).then_inc(g["made"].sem)
                pool.wait_ge(*g["made"](3))
                pool.affine_select(out=of_head[:], in_=of_head[:], compare_op=ALU.is_ge, fill=0.0, base=DH - 1,
                                   pattern=[[DH, HT8]], channel_multiplier=-1).then_inc(g["made"].sem)

            @block.tensor
            def _(pe):
                pe.wait_ge(g["load"].sem, 16)
                for m in range(FT):
                    for k in range(2):
                        mm = pe.matmul(c.bank(0)[:, m * P:(m + 1) * P], c.w("y_wk", k, m * P, P, KC[k]), cx[0:KC[k], k, :],
                                       start=(k == 0), stop=(k == 1))
                mm.then_inc(g["k"].sem)
                for b in range(B):
                    for k in range(2):
                        mm = pe.matmul(c.bank(1)[0:KEYS, b * D:(b + 1) * D], cx[0:KC[k], k, b * KEYS:(b + 1) * KEYS],
                                       c.w("y_wv", k, 0, D, KC[k]), start=(k == 0), stop=(k == 1))
                mm.then_inc(g["v"].sem)

            @block.vector
            def _(dve):
                dve.wait_ge(*g["k"](1))
                for m in range(FT):
                    ins = dve.tensor_scalar(kc[:, m, :], c.bank(0)[:, m * P:(m + 1) * P], c.v("y_bk", m), None, ALU.add)
                ins.then_inc(g["kb"].sem)
                dve.wait_ge(*g["kb"](1))
                dve.wait_ge(*g["made"](4))
                for b in range(B):
                    for m in range(FT):
                        dve.tensor_tensor(k_diag[:, b, m, :].rearrange("p (h n) -> p h n", h=HT8),
                                          kc[:, m, b * KEYS:(b + 1) * KEYS].unsqueeze(1).to_broadcast([P, HT8, KEYS]),
                                          of_head[:].unsqueeze(2).to_broadcast([P, HT8, KEYS]), ALU.mult)
                dve.wait_ge(*g["v"](1))
                for b in range(B):
                    pairs = c.bank(1)[0:KEYS, b * D:(b + 1) * D].rearrange("p (r d) -> p r d", r=PAIRS)
                    for i in (0, 1):
                        dve.tensor_copy(v_diag[i * KEYS:(i + 1) * KEYS, b, :, i * DH:(i + 1) * DH], pairs[:, :, i * DH:(i + 1) * DH])

        norm_both(nc, c, norm_s, xn_all)
        with nc.Fori(0, B) as b:
            set_round(b, s)
            x = lambda k, j: c.xT[:, k, bass.ds(b * S + j * CH, CH)]
            kd = k_diag[:].rearrange("p b m n -> p (b m n)")
            vd = v_diag[:].rearrange("p b r d -> p (b r d)")
            score = lambda u: c.psum[u % 2]
            turn_bank = lambda n: c.bank(5 + n % 2)
            out_bank = lambda u: c.bank(4 if u % 2 else 7)
            order = []
            for u in range(TT + 2):
                if u < TT:
                    order += [(u, 0), (u, 1)]
                if u >= 2:
                    order.append((u - 2, "o"))
            nth = {what: n for n, what in enumerate(order)}
            with nc.Block() as block:

                @block.tensor
                def _(pe):
                    for m in range(FT):
                        for j in range(NCH):
                            for k in range(FT):
                                mm = pe.matmul(c.bank(4 + 2 * m + j), c.w("y_wq", k, m * P, P),
                                               xn_all[:, k, bass.ds(b * S + j * CH, CH)], start=(k == 0), stop=(k == 1))
                            mm.then_inc(s["q_proj"].sem)

                    def scores(u):
                        if u == 0:
                            pe.wait_ge(*s["q_raw"](4))
                        if u >= 2:
                            pe.wait_ge(*s["shifted"](u - 1))
                        for m in range(FT):
                            mm = pe.matmul(score(u)[:, m * CH:(m + 1) * CH], q[:, m, u * P:(u + 1) * P],
                                           kd[:, bass.ds(b * (FT * CH) + m * CH, CH)], start=True, stop=True)
                        mm.then_inc(s["scores"].sem)

                    def turn(u, i):
                        n = nth[u, i]
                        pe.wait_ge(*s["expd"](u + 1))
                        if n >= 2:
                            pe.wait_ge(*s["copied"](n - 1))
                        for r in range(4):
                            mm = pe.transpose(turn_bank(n)[:, r * P:(r + 1) * P], probs[u % 2][:, (4 * i + r) * P:(4 * i + r + 1) * P],
                                              c.ident[:])
                        mm.then_inc(s["turned"].sem)

                    def values(u):
                        pe.wait_ge(*s["copied"](nth[u, 1] + 1))
                        if u >= 2:
                            pe.wait_ge(*s["normed"](u - 1))
                        for r in range(PAIRS):
                            mm = pe.matmul(out_bank(u)[:, r * 2 * DH:(r + 1) * 2 * DH], turned[u % 2][:, r, :],
                                           vd[:, bass.ds(b * D + r * 2 * DH, 2 * DH)], start=True, stop=True)
                        mm.then_inc(s["av"].sem)

                    def turn_outputs(u):
                        n = nth[u, "o"]
                        pe.wait_ge(*s["normed"](u + 1))
                        pe.wait_ge(*s["copied"](n - 1))
                        for m in range(FT):
                            mm = pe.transpose(turn_bank(n)[:, m * P:(m + 1) * P], o[:, u % 2, m * P:(m + 1) * P], c.ident[:])
                        mm.then_inc(s["turned"].sem)

                    scores(0)
                    for u in range(TT + 2):
                        if u + 1 < TT:
                            scores(u + 1)
                        if u < TT:
                            turn(u, 0)
                            turn(u, 1)
                        if u >= 2:
                            turn_outputs(u - 2)
                        if 1 <= u <= TT:
                            values(u - 1)
                    pe.wait_ge(*s["copied"](len(order)))
                    for m in range(FT):
                        for j in range(NCH):
                            for k in range(FT):
                                mm = pe.matmul(c.bank(2 * m + j), c.w("y_wo", k, m * P, P), ot[:, k, j * CH:(j + 1) * CH],
                                               start=(k == 0), stop=(k == 1))
                            mm.then_inc(s["o_done"].sem)

                @block.scalar
                def _(act):
                    for n in range(4):
                        m, j = divmod(n, NCH)
                        act.wait_ge(*s["q_proj"](n + 1))
                        act.activation(q[:, m, j * CH:(j + 1) * CH], c.bank(4 + n), ACT.Identity, bias=c.v("y_bq", m)).then_inc(s["q_raw"].sem)
                    for u in range(TT):
                        act.wait_ge(*s["shifted"](u + 1))
                        act.activation(probs[u % 2], probs[u % 2], ACT.Exp, scale=SCALE).then_inc(s["expd"].sem)

                @block.vector
                def _(dve):
                    heads = lambda ap: ap.rearrange("p (h n) -> p h n", h=H)
                    wide = lambda ap, n: ap.unsqueeze(2).to_broadcast([P, H, n])

                    def shift(u):
                        dve.wait_ge(*s["scores"](u + 1))
                        dve.tensor_reduce(mx[:, u % 2, :], heads(score(u)[:]), AX, ALU.max).then_inc(s["row_max"].sem)
                        dve.wait_ge(*s["row_max"](u + 1))
                        if u >= 2:
                            dve.wait_ge(*s["turned"](nth[u - 2, 1] + 1))
                        dve.tensor_tensor(heads(probs[u % 2]), heads(score(u)[:]), wide(mx[:, u % 2, :], KEYS), ALU.subtract)\
                           .then_inc(s["shifted"].sem)

                    def copy_turned(u, i):
                        n = nth[u, i]
                        dve.wait_ge(*s["turned"](n + 1))
                        if u >= 2 and i == 0:
                            dve.wait_ge(*s["av"](u - 1))
                        dve.tensor_copy(turned[u % 2][:, 4 * i:4 * i + 4, :].rearrange("p k n -> p (k n)"), turn_bank(n))\
                           .then_inc(s["copied"].sem)

                    def den(u):
                        dve.wait_ge(*s["expd"](u + 1))
                        if u >= 2:
                            dve.wait_ge(*s["normed"](u - 1))
                        dve.tensor_reduce(rs[:, u % 2, :], heads(probs[u % 2]), AX, ALU.add).then_inc(s["den"].sem)
                        dve.wait_ge(*s["den"](u + 1))
                        dve.reciprocal(rs[:, u % 2, :], rs[:, u % 2, :]).then_inc(s["den_inv"].sem)

                    def norm(u):
                        dve.wait_ge(*s["av"](u + 1))
                        dve.wait_ge(*s["den_inv"](u + 1))
                        dve.tensor_tensor(heads(o[:, u % 2, :]), heads(out_bank(u)[:, 0:D]), wide(rs[:, u % 2, :], DH), ALU.mult)\
                           .then_inc(s["normed"].sem)

                    def copy_outputs(u):
                        n = nth[u, "o"]
                        dve.wait_ge(*s["turned"](n + 1))
                        for m in range(FT):
                            ins = dve.tensor_scalar(ot[:, m, u * P:(u + 1) * P], turn_bank(n)[:, m * P:(m + 1) * P],
                                                    c.v("y_bv", m), None, ALU.add)
                        ins.then_inc(s["copied"].sem)

                    shift(0)
                    for u in range(TT + 2):
                        if u < TT:
                            den(u)
                        if u + 1 < TT:
                            shift(u + 1)
                        if u < TT:
                            copy_turned(u, 0)
                            copy_turned(u, 1)
                        if u >= 2:
                            copy_outputs(u - 2)
                        if 1 <= u <= TT:
                            norm(u - 1)
                    for m in range(FT):
                        for j in range(NCH):
                            dve.wait_ge(*s["o_done"](2 * m + j + 1))
                            dve.scalar_tensor_tensor(out=x(m, j), in0=c.bank(2 * m + j), scalar=c.v("y_bo", m),
                                                     in1=x(m, j), op0=ALU.add, op1=ALU.add).then_inc(s["x_done"].sem)
        clear_signals(nc, norm_s, s, g)


def expert_layer(nc, c):
    TIL = T // P
    GP = GR // 2
    NP_ = TIL * EXP
    RN = FT + GP + 2 + FT * GP
    NEXT = EXP + 2
    with ExitStack() as ctx:
        sb = lambda name, shape, dt=F32: ctx.enter_context(nc.sbuf_tensor(name, shape, dt))
        norm_s = signals(nc, ctx, "mn", norm_signals())
        s = signals(nc, ctx, "m", dict(turned=2 * B * 2, copied=2 * B * 2, logits=1, logits_read=1))
        set_round(0, s)
        r = signals(nc, ctx, "r", dict(made=4, step=40, prep=5, cum1=1, cnt=2, cum2=1))
        set_round(0, r)
        e = signals(nc, ctx, "e", dict(
            made=2 * RN, read=2 * RN, w0_done=2 * HT, w1_done=2 * HT, gelu=2 * HT, hidden=2 * HT, prep=10, prepared=2))
        w_sig = [ctx.enter_context(nc.semaphore(f"e_weights{i}")) for i in range(2)]
        xn_tok = c.arena[:, 4 * FT * S:].rearrange("p (t n) -> p t n", t=TIL)
        logits = sb("m_logits", [P, TIL, EXP])
        tab = {n: sb(f"m_{n}", [P, TIL, EXP]) for n in ("raw", "rest", "m1", "m2", "p1", "p2", "t")}
        order8 = sb("m_order", [P, EXP])
        col16 = {n: sb(f"m_{n}", [P, TIL]) for n in ("mx", "sm", "g1", "g2", "pick")}
        pos = [sb(f"m_pos{i}", [P, NEXT * TIL]) for i in (1, 2)]
        before = sb("m_before", [P, P])
        ones = sb("m_ones", [P, P])
        iota_i = sb("m_iota_i", [P, CAP], mybir.dt.int32)
        iota = sb("m_iota", [P, CAP])
        disp = [sb(f"m_disp{i}", [P, TIL, CAP]) for i in range(2)]
        comb = [sb(f"m_comb{i}", [P, TIL, P]) for i in range(2)]
        one = sb("m_one", [P, TIL, CAP])
        two = sb("m_two", [P, TIL, CAP])
        back = sb("m_back", [P, TIL, P])
        x_in = sb("m_x_in", [P, FT, CH])
        gelu = c.arena[:, (HT + 2) * CH:(HT + 4) * CH].rearrange("p (i n) -> p i n", i=2)
        hidden = c.arena[:, 0:HT * CH].rearrange("p (h n) -> p h n", h=HT)
        e_out = c.arena[:, HT * CH:(HT + 2) * CH].rearrange("p (g n) -> p g n", g=GP)
        xn = c.two_slots(0)
        n_w = FT * HID
        per = 2 * n_w + HT * D
        assert 2 * per <= c.mats["router"][0]
        wbuf = [c.weights[:, i * per:(i + 1) * per] for i in range(2)]
        w0 = [w[:, 0:n_w].rearrange("p (k h) -> p k h", k=FT) for w in wbuf]
        w1 = [w[:, n_w:2 * n_w].rearrange("p (k h) -> p k h", k=FT) for w in wbuf]
        wo = [w[:, 2 * n_w:].rearrange("p (h n) -> p h n", h=HT) for w in wbuf]
        FULL = (HT - 1) * P
        col = lambda t: (lambda k, j: t[:, k, j * CH:(j + 1) * CH])

        def load_expert(sync, i, ex):
            pick = lambda m: m[bass.ds(ex, 1)].rearrange("e a b c -> (e a) b c") if len(m.shape) == 4 else \
                m[bass.ds(ex, 1)].rearrange("e a b -> (e a) b")
            sync.dma_start(w0[i], pick(c.w0)).then_inc(w_sig[i], 16)
            sync.dma_start(w1[i], pick(c.w1)).then_inc(w_sig[i], 16)
            rows = pick(c.wo)
            sync.dma_start(wo[i][:, 0:HT - 1, :], rows[0:FULL, :].rearrange("(h p) n -> p h n", p=P)).then_inc(w_sig[i], 16)
            sync.dma_start(wo[i][0:HLAST, HT - 1, :], rows[FULL:HID, :]).then_inc(w_sig[i], 16)

        W_LOAD = 4 * 16
        with nc.Block() as block:

            @block.sync
            def _(sync):
                for i in range(2):
                    load_expert(sync, i, i)

            @block.gpsimd
            def _(pool):
                for i in range(2):
                    pool.memset(comb[i][:], 0.0)
                    pool.memset(pos[i][:], -1.0)
                pool.iota(iota_i[:], pattern=[[1, CAP]], base=0, channel_multiplier=0).then_inc(r["made"].sem)
                pool.memset(ones[:], 1.0).then_inc(r["made"].sem)
                pool.wait_ge(*r["made"](2))
                pool.affine_select(out=before[:], in_=ones[:], compare_op=ALU.is_gt, fill=0.0, base=0,
                                   pattern=[[1, P]], channel_multiplier=-1)
                for i in range(EXP):
                    pool.memset(order8[:, i:i + 1], float(EXP - i))
                pool.tensor_copy(iota[:], iota_i[:]).then_inc(r["made"].sem)

        norm_both(nc, c, norm_s, xn)
        with nc.Block() as block:

            @block.tensor
            def _(pe):
                for t in range(TIL):
                    for k in range(FT):
                        mm = pe.matmul(c.bank(7)[:, t * EXP:(t + 1) * EXP], xn[:, k, t * P:(t + 1) * P],
                                       c.w("router", k, 0, EXP), start=(k == 0), stop=(k == 1))
                mm.then_inc(s["logits"].sem)
                for t2 in range(TIL // 2):
                    if t2 >= 4:
                        pe.wait_ge(*s["copied"](t2 - 3))
                    for t in (0, 1):
                        for k in range(FT):
                            mm = pe.transpose(c.bank(t2 % 4)[:, t * D + k * P:t * D + (k + 1) * P],
                                              xn[:, k, (2 * t2 + t) * P:(2 * t2 + t + 1) * P], c.ident[:])
                    mm.then_inc(s["turned"].sem)

            @block.scalar
            def _(act):
                for t2 in range(TIL // 2):
                    act.wait_ge(*s["turned"](t2 + 1))
                    act.activation(xn_tok[:, 2 * t2:2 * t2 + 2, :].rearrange("p t n -> p (t n)"), c.bank(t2 % 4), ACT.Copy)\
                       .then_inc(s["copied"].sem)

            @block.vector
            def _(dve):
                dve.wait_ge(*s["logits"](1))
                dve.tensor_copy(logits[:].rearrange("p t e -> p (t e)"), c.bank(7)[:, 0:NP_]).then_inc(s["logits_read"].sem)

        def prepare(dve, i, ex, done, sig):
            wide_pos = lambda p: p[:, bass.ds(ex * TIL, TIL)].unsqueeze(2).to_broadcast([P, TIL, CAP])
            wide_iota = iota[:].unsqueeze(1).to_broadcast([P, TIL, CAP])
            wide16 = lambda t: t[:].unsqueeze(2).to_broadcast([P, TIL, CAP])
            n = [0]

            def step(f):
                def go():
                    n[0] += 1
                    f().then_inc(sig.sem)
                    dve.wait_ge(*sig(5 * done + n[0]))
                return go
            return [
                step(lambda: dve.tensor_tensor(one[:], wide_pos(pos[0]), wide_iota, ALU.is_equal)),
                step(lambda: dve.tensor_tensor(two[:], wide_pos(pos[1]), wide_iota, ALU.is_equal)),
                step(lambda: dve.tensor_tensor(disp[i][:], one[:], two[:], ALU.add)),
                step(lambda: dve.tensor_tensor(one[:], one[:], wide16(col16["g1"]), ALU.mult)),
                step(lambda: dve.tensor_tensor(two[:], two[:], wide16(col16["g2"]), ALU.mult)),
            ], lambda: combine_halves(dve, i)

        def combine_halves(dve, i):
            for g in range(2):
                for q in range(GP):
                    tiles = slice(4 * q + 2 * g, 4 * q + 2 * g + 2)
                    ins = dve.tensor_tensor(comb[i][:, tiles, g * CAP:(g + 1) * CAP], one[:, tiles, :], two[:, tiles, :], ALU.add)
            return ins

        with nc.Block() as block:

            @block.tensor
            def _(pe):
                even = lambda t: t.rearrange("p (g t) e -> p g t e", t=2)[:, :, 0, :]
                odd = lambda t: t.rearrange("p (g t) e -> p g t e", t=2)[:, :, 1, :]
                table = lambda i: c.bank(i)[:, 0:NP_].rearrange("p (t e) -> p t e", t=TIL)
                pe.wait_ge(*r["made"](3))
                pe.wait_ge(*r["cum1"](1))
                pe.matmul(table(0), before[:], tab["m1"][:], start=True, stop=False)
                pe.matmul(odd(table(0)), ones[:], even(tab["m1"][:]), start=False, stop=True).then_inc(r["cnt"].sem)
                pe.wait_ge(*r["cum2"](1))
                pe.matmul(table(1), before[:], tab["m2"][:], start=True, stop=False)
                pe.matmul(odd(table(1)), ones[:], even(tab["m2"][:]), start=False, stop=False)
                for to in (even, odd):
                    for of in (even, odd):
                        mm = pe.matmul(to(table(1)), ones[:], of(tab["m1"][:]), start=False, stop=(to is odd and of is odd))
                mm.then_inc(r["cnt"].sem)

            @block.scalar
            def _(act):
                act.wait_ge(*r["step"](2))
                act.activation(tab["raw"][:], tab["raw"][:], ACT.Exp).then_inc(r["step"].sem)

            @block.vector
            def _(dve):
                n = [0]

                def do(ins):
                    n[0] += 1
                    ins.then_inc(r["step"].sem)
                    dve.wait_ge(*r["step"](n[0]))

                wide = lambda t: t[:].unsqueeze(2).to_broadcast([P, TIL, EXP])
                order_w = order8[:].unsqueeze(1).to_broadcast([P, TIL, EXP])
                raw, rest, t = tab["raw"], tab["rest"], tab["t"]
                dve.wait_ge(*r["made"](3))
                do(dve.tensor_reduce(col16["mx"][:], logits[:], AX, ALU.max))
                do(dve.tensor_tensor(raw[:], logits[:], wide(col16["mx"]), ALU.subtract))
                n[0] += 1
                dve.wait_ge(*r["step"](n[0]))
                do(dve.tensor_reduce(col16["sm"][:], raw[:], AX, ALU.add))
                do(dve.reciprocal(col16["sm"][:], col16["sm"][:]))
                do(dve.tensor_tensor(raw[:], raw[:], wide(col16["sm"]), ALU.mult))

                def first_max(values, gate, chosen):
                    do(dve.tensor_reduce(gate[:], values[:], AX, ALU.max))
                    do(dve.tensor_tensor(t[:], values[:], wide(gate), ALU.is_equal))
                    do(dve.tensor_tensor(t[:], t[:], order_w, ALU.mult))
                    do(dve.tensor_reduce(col16["pick"][:], t[:], AX, ALU.max))
                    do(dve.tensor_tensor(chosen[:], t[:], wide(col16["pick"]), ALU.is_equal))

                first_max(raw, col16["g1"], tab["m1"])
                do(dve.tensor_tensor(t[:], raw[:], tab["m1"][:], ALU.mult))
                do(dve.tensor_tensor(rest[:], raw[:], t[:], ALU.subtract))
                first_max(rest, col16["g2"], tab["m2"])
                dve.tensor_copy(t[:], t[:]).then_inc(r["cum1"].sem)

                def keep(i, m, p, bank):
                    do(dve.tensor_copy(p[:].rearrange("p t e -> p (t e)"), c.bank(bank)[:, 0:NP_]))
                    do(dve.tensor_scalar(t[:], p[:], float(CAP), None, ALU.is_lt))
                    do(dve.tensor_tensor(m[:], m[:], t[:], ALU.mult))
                    do(dve.tensor_scalar(p[:], p[:], 1.0, None, ALU.add))
                    do(dve.tensor_tensor(p[:], p[:], m[:], ALU.mult))
                    do(dve.tensor_scalar(pos[i][:, 0:NP_].rearrange("p (e t) -> p t e", t=TIL), p[:], -1.0, None, ALU.add))

                dve.wait_ge(*r["cnt"](1))
                keep(0, tab["m1"], tab["p1"], 0)
                dve.tensor_copy(t[:], t[:]).then_inc(r["cum2"].sem)
                dve.wait_ge(r["cnt"].sem, 2)
                keep(1, tab["m2"], tab["p2"], 1)
                steps, last = prepare(dve, 0, 0, 0, r["prep"])
                for go in steps:
                    go()
                last()

        def expert_round(rd, load):
            with nc.Block() as block:
                H_N = lambda h: P if h < HT - 1 else HLAST

                @block.sync
                def _(sync):
                    if load:
                        for i in range(2):
                            sync.wait_ge(*e["made"](RN * i + 8))
                            load_expert(sync, i, 2 * rd + 2 + i)

                @block.tensor
                def _(pe):
                    ring = [0]

                    def reuse():
                        n = ring[0]
                        ring[0] += 1
                        if n >= 4:
                            pe.wait_ge(*e["read"](n - 3))
                        return c.bank(4 + n % 4)

                    for i in range(2):
                        if i == 1:
                            pe.wait_ge(*e["prepared"](1))
                        for m in range(FT):
                            bank = reuse()
                            for g in range(GR):
                                for t in range(2):
                                    mm = pe.matmul(bank[:, g * CAP:(g + 1) * CAP], xn_tok[:, 2 * g + t, m * P:(m + 1) * P],
                                                   disp[i][:, 2 * g + t, :], start=(t == 0), stop=(t == 1))
                            mm.then_inc(e["made"].sem)
                        for q in range(GP):
                            bank = reuse()
                            for t in range(4):
                                mm = pe.transpose(bank[:, t * P:(t + 1) * P], comb[i][:, 4 * q + t, :], c.ident[:])
                            mm.then_inc(e["made"].sem)
                        pe.wait_ge(w_sig[i], w_value(rd))
                        pe.wait_ge(*e["read"](RN * i + 2))
                        for h in range(HT):
                            n = HT * i + h
                            for w, base, free, done in ((w0, 0, e["gelu"], e["w0_done"]), (w1, 2, e["hidden"], e["w1_done"])):
                                if n >= 2:
                                    pe.wait_ge(*free(n - 1))
                                for k in range(FT):
                                    mm = pe.matmul(c.bank(base + n % 2)[0:H_N(h), :], w[i][:, k, h * P:h * P + H_N(h)],
                                                   x_in[:, k, :], start=(k == 0), stop=(k == 1))
                                mm.then_inc(done.sem)
                        pe.wait_ge(*e["hidden"](HT * (i + 1)))
                        for q2 in range(2):
                            bank = reuse()
                            for q in (0, 1):
                                for h in range(HT):
                                    mm = pe.matmul(bank[:, q * D:(q + 1) * D],
                                                   hidden[0:H_N(h), h, (2 * q2 + q) * P:(2 * q2 + q + 1) * P],
                                                   wo[i][0:H_N(h), h, :], start=(h == 0), stop=(h == HT - 1))
                            mm.then_inc(e["made"].sem)
                        pe.wait_ge(*e["read"](RN * i + 8))
                        for m in range(FT):
                            for q in range(GP):
                                bank = reuse()
                                pe.matmul(bank, e_out[:, q, m * P:(m + 1) * P],
                                          back[:, 4 * q:4 * q + 4, :].rearrange("p t n -> p (t n)"), start=True, stop=True)\
                                  .then_inc(e["made"].sem)

                @block.scalar
                def _(act):
                    for n in range(2 * HT):
                        h = n % HT
                        act.wait_ge(*e["w0_done"](n + 1))
                        if n >= 2:
                            act.wait_ge(*e["hidden"](n - 1))
                        act.activation(gelu[0:H_N(h), n % 2, :], c.bank(n % 2)[0:H_N(h), :], ACT.Gelu_apprx_tanh).then_inc(e["gelu"].sem)

                @block.vector
                def _(dve):
                    n = [0]

                    def take(f):
                        n[0] += 1
                        dve.wait_ge(*e["made"](n[0]))
                        f(c.bank(4 + (n[0] - 1) % 4)).then_inc(e["read"].sem)

                    for i in range(2):
                        for m in range(FT):
                            take(lambda bank: dve.tensor_copy(x_in[:, m, :], bank))
                        for q in range(GP):
                            take(lambda bank: dve.tensor_copy(back[:, 4 * q:4 * q + 4, :].rearrange("p t n -> p (t n)"), bank))
                        steps, last = prepare(dve, 1 - i, 2 * rd + 1 + i, i, e["prep"])
                        for h in range(HT):
                            k = HT * i + h
                            dve.wait_ge(*e["gelu"](k + 1))
                            dve.wait_ge(*e["w1_done"](k + 1))
                            dve.tensor_tensor(hidden[0:H_N(h), h, :], gelu[0:H_N(h), k % 2, :], c.bank(2 + k % 2)[0:H_N(h), :],
                                              ALU.mult).then_inc(e["hidden"].sem)
                            if h < len(steps):
                                steps[h]()
                            if h == len(steps):
                                last().then_inc(e["prepared"].sem)
                        for q2 in range(2):
                            take(lambda bank: dve.tensor_copy(e_out[:, 2 * q2:2 * q2 + 2, :].rearrange("p q n -> p (q n)"), bank))
                        for m in range(FT):
                            for q in range(GP):
                                xs = c.xT[:, m, q * CH:(q + 1) * CH]
                                take(lambda bank: dve.tensor_tensor(xs, bank, xs, ALU.add))

        w_value = lambda rd: W_LOAD * (rd + 1)
        ROUNDS = EXP // 2
        with nc.Fori(0, ROUNDS - 1) as rd:
            set_round(rd, e)
            expert_round(rd, True)
        set_round(ROUNDS - 1, e)
        expert_round(ROUNDS - 1, False)
        clear_signals(nc, norm_s, s, r, e, also=w_sig)


def load_everything(nc, ctx, c, x_t, weights, vectors):
    n_first = c.mats["x_wq"][0]
    loaded = ctx.enter_context(nc.semaphore("loaded"))
    c.others_loaded = ctx.enter_context(nc.semaphore("others_loaded"))
    made = ctx.enter_context(nc.semaphore("made"))
    with nc.Block() as block:

        @block.sync
        def _(sync):
            sync.dma_start(c.xT[:], x_t).then_inc(loaded, 16)
            sync.dma_start(c.vectors[:], vectors).then_inc(loaded, 16)
            sync.dma_start(c.weights[:, 0:n_first], weights[:, 0:n_first]).then_inc(loaded, 16)
            sync.dma_start(c.weights[:, n_first:], weights[:, n_first:]).then_inc(c.others_loaded, 16)
            sync.wait_ge(loaded, 48)

        @block.gpsimd
        def _(pool):
            pool.memset(c.mean_w[:], 1.0 / D)
            pool.memset(c.eps[:], LN_EPS)
            pool.memset(c.eps_eps[:], LN_EPS * LN_EPS)
            pool.memset(c.ident[:], 0.0).then_inc(made)
            pool.wait_ge(made, 1)
            pool.affine_select(out=c.ident[:], in_=c.ident[:], compare_op=ALU.not_equal, fill=1.0, base=0,
                               pattern=[[-1, P]], channel_multiplier=1).then_inc(made)


def wait_for_weights(nc, c):
    with nc.Block() as block:

        @block.sync
        def _(sync):
            sync.wait_ge(c.others_loaded, 16)


def store_result(nc, ctx, c, out):
    stored = ctx.enter_context(nc.semaphore("stored"))
    with nc.Block() as block:

        @block.sync
        def _(sync):
            sync.dma_start(out, c.xT[:]).then_inc(stored, 16)
            sync.wait_ge(stored, 16)


LAYERS = [linear_attention_layer, cross_attention_layer, gated_recurrence_layer, causal_attention_layer,
          context_attention_layer, expert_layer]


def build_program(nc, x_t, ctx_t, mask, weights, vectors, w0, w1, wo, out):
    with ExitStack() as ctx:
        c = Chip(nc, ctx)
        c.ctx_t, c.mask, c.w0, c.w1, c.wo = ctx_t, mask, w0, w1, wo
        load_everything(nc, ctx, c, x_t, weights, vectors)
        for n, layer in enumerate(LAYERS):
            if n == 1 or len(LAYERS) == 1:
                wait_for_weights(nc, c)
            layer(nc, c)
        store_result(nc, ctx, c, out)


def kernel(**inputs):
    import numpy as np
    import concourse.bacc as bacc
    from concourse import mybir as _mybir
    from concourse.bass_utils import run_bass_kernel_spmd

    a = {k: np.asarray(v) for k, v in inputs.items()}
    wqkv = a["L1_attn_Wqkv"]
    part = lambda i: wqkv[:, :, 16 * i:16 * (i + 1)].transpose(1, 0, 2).reshape(D, D)
    bias = lambda i: a["L1_attn_bqkv"][:, 16 * i:16 * (i + 1)].reshape(D)
    mats = {
        "a_wq": a["L0_attn_wq"], "a_wk": a["L0_attn_wk"], "a_wv": a["L0_attn_wv"], "a_wo": a["L0_attn_wo"],
        "a_w1": a["L0_attn_w_ff1"], "a_w2": a["L0_attn_w_ff2"], "a_wd": a["L0_attn_w_d"],
        "x_wq": a["L0_xattn_Wq"].T, "x_wkv": a["L0_xattn_Wkv"].T, "x_wlkv": a["L0_xattn_Wlkv"].T,
        "x_wo": a["L0_xattn_Wo"].T,
        "f_wf": a["L0_ffn_wf"].T, "f_uf": a["L0_ffn_uf"].T, "f_wi": a["L0_ffn_wi"].T, "f_ui": a["L0_ffn_ui"].T,
        "f_wc": a["L0_ffn_wc"].T, "f_uc": a["L0_ffn_uc"].T, "f_wo": a["L0_ffn_wo"].T, "f_uo": a["L0_ffn_uo"].T,
        "b_wq": part(0), "b_wk": part(1), "b_wv": part(2), "b_wo": a["L1_attn_Wout"],
        "y_wq": a["L1_xattn_wq"], "y_wk": a["L1_xattn_wk"], "y_wv": a["L1_xattn_wv"], "y_wo": a["L1_xattn_wo"],
        "router": a["L1_ffn_router_w"],
    }
    vecs = {
        "a_g1": a["L0_attn_ln1_g"], "a_b1": a["L0_attn_ln1_b"], "a_bo": a["L0_attn_bo"], "a_g2": a["L0_attn_ln2_g"],
        "a_b2": a["L0_attn_ln2_b"], "a_bf1": a["L0_attn_b_ff1"], "a_bf2": a["L0_attn_b_ff2"], "a_bd": a["L0_attn_b_d"],
        "x_gx": a["L0_xattn_ln_x_g"], "x_bx": a["L0_xattn_ln_x_b"], "x_gl": a["L0_xattn_ln_l_g"],
        "x_bl": a["L0_xattn_ln_l_b"], "x_gq": np.tile(a["L0_xattn_qn_g"], 2), "x_gk": np.tile(a["L0_xattn_kn_g"], 2),
        "x_bo": a["L0_xattn_bo"],
        "f_bf": a["L0_ffn_bf"], "f_bi": a["L0_ffn_bi"], "f_bc": a["L0_ffn_bc"], "f_bo": a["L0_ffn_bo"],
        "f_c0": a["L0_ffn_in_c"],
        "b_bq": bias(0), "b_bk": bias(1), "b_bv": bias(2), "b_bo": a["L1_attn_bout"],
        "y_bq": a["L1_xattn_bq"], "y_bk": a["L1_xattn_bk"], "y_bv": a["L1_xattn_bv"], "y_bo": a["L1_xattn_bo"],
    }

    def tiles(m):
        n = -(-m.shape[0] // P)
        full = np.zeros((n * P, m.shape[1]), m.dtype)
        full[:m.shape[0]] = m
        return full.reshape(n, P, -1).transpose(1, 0, 2).reshape(P, -1)

    ins = {
        "x_t": a["x"].reshape(T, FT, P).transpose(2, 1, 0),
        "ctx_t": tiles(a["ctx_768"].reshape(B * KEYS, CF).T),
        "mask": a["mask_BxS2_bk0"].reshape(1, B * KEYS),
        "weights": np.concatenate([tiles(mats[n]) for n in MATS], 1),
        "vectors": np.concatenate([tiles(vecs[n].reshape(-1, 1)) for n in VECS], 1),
        "w0": a["L1_ffn_w0_kernel"].reshape(EXP, FT, P, HID).transpose(0, 2, 1, 3),
        "w1": a["L1_ffn_w1_kernel"].reshape(EXP, FT, P, HID).transpose(0, 2, 1, 3),
        "wo": a["L1_ffn_wo_kernel"],
    }
    ins = {n: np.ascontiguousarray(v) for n, v in ins.items()}
    nc = bacc.Bacc("TRN2", target_bir_lowering=False, num_devices=1)
    args = [nc.dram_tensor(n, v.shape, _mybir.dt.from_np(v.dtype), kind="ExternalInput").ap() for n, v in ins.items()]
    out = nc.dram_tensor("out", (P, FT, T), F32, kind="ExternalOutput").ap()
    build_program(nc, *args, out)
    got = run_bass_kernel_spmd(nc, [ins], core_ids=[0]).results[0]["out"]
    return got.transpose(2, 1, 0).reshape(B, S, D)
```

```python
from contextlib import ExitStack

import concourse.bass as bass
from concourse import mybir

F32 = mybir.dt.float32
BF16 = mybir.dt.bfloat16
F32R = mybir.dt.float32r
U8 = mybir.dt.uint8
ALU = mybir.AluOpType
ACT = mybir.ActivationFunctionType
AX = mybir.AxisListType.X

P = 128
B, S, D = 2, 1024, 256
T = B * S
FT = D // P
CH = 512
NCH = S // CH
TT = S // P
LN_EPS = 1e-5
NEG = -1e30

MATS = {
    "a_wq": (256, 256), "a_wk": (256, 256), "a_wv": (256, 256), "a_wo": (256, 256),
    "a_w1": (256, 1024), "a_w2": (1024, 256), "a_wd": (256, 256),
    "x_wq": (256, 256), "x_wkv": (192, 512), "x_wlkv": (256, 512), "x_wo": (256, 256),
    "f_wf": (256, 256), "f_uf": (256, 256), "f_wi": (256, 256), "f_ui": (256, 256),
    "f_wc": (256, 256), "f_uc": (256, 256), "f_wo": (256, 256), "f_uo": (256, 256),
    "b_wq": (256, 256), "b_wk": (256, 256), "b_wv": (256, 256), "b_wo": (256, 256),
    "y_wq": (256, 256), "y_wk": (192, 256), "y_wv": (192, 256), "y_wo": (256, 256),
    "router": (256, 8),
}
VECS = {
    "a_g1": 2, "a_b1": 2, "a_bo": 2, "a_g2": 2, "a_b2": 2, "a_bf1": 8, "a_bf2": 2, "a_bd": 2,
    "x_gx": 2, "x_bx": 2, "x_gl": 2, "x_bl": 2, "x_gq": 1, "x_gk": 1, "x_bo": 2,
    "f_bf": 2, "f_bi": 2, "f_bc": 2, "f_bo": 2, "f_c0": 2,
    "b_bq": 2, "b_bk": 2, "b_bv": 2, "b_bo": 2,
    "y_bq": 2, "y_bk": 2, "y_bv": 2, "y_bo": 2,
}
KEYS = 64
CF = 192
EXP, HID, CAP, GR = 8, 1368, 64, 8
HT = -(-HID // P)
HLAST = HID - (HT - 1) * P


def mat_offsets():
    off, at = {}, 0
    for name, (rows, cols) in MATS.items():
        tiles = -(-rows // P)
        off[name] = (at, tiles, cols)
        at += tiles * cols
    return off, at


def vec_offsets():
    off, at = {}, 0
    for name, n in VECS.items():
        off[name] = (at, n)
        at += n
    return off, at


class Sig:

    def __init__(self, sem, per_round):
        self.sem, self.per_round, self.round = sem, per_round, 0

    def __call__(self, n):
        return self.sem, self.round * self.per_round + n


class Chip:

    def __init__(self, nc, ctx):
        sb = lambda name, shape, dt=F32: ctx.enter_context(nc.sbuf_tensor(name, shape, dt))
        self.mats, n_mat = mat_offsets()
        self.vecs, n_vec = vec_offsets()
        self.xT = sb("xT", [P, FT, T])
        self.n_mat = n_mat
        self.vectors = sb("vectors_sb", [P, n_vec])
        self.ident = sb("ident", [P, P])
        self.mean_w = sb("mean_w", [P, P])
        self.eps = sb("eps", [P, 1])
        self.eps_eps = sb("eps_eps", [P, 1])
        self.arena = sb("arena", [P, 6 * FT * S])
        self.psum = [ctx.enter_context(nc.psum_tensor(f"psum{i}", [P, 2 * CH], F32)) for i in range(4)]

    def take_room(self, nc, ctx):
        self.weights = ctx.enter_context(nc.sbuf_tensor("weights_sb", [P, self.n_mat], F32))
        self.ln = ctx.enter_context(nc.sbuf_tensor("ln", [P, 3 * NCH, CH], F32))
        self.ln_s, self.ln_d, self.ln_r = (self.ln[:, i * NCH:(i + 1) * NCH, :] for i in range(3))

    def slot(self, i):
        n = FT * S
        return self.arena[:, i * n:(i + 1) * n].rearrange("p (m t) -> p m t", m=FT)

    def two_slots(self, i):
        n = FT * T
        return self.arena[:, i * n // 2:i * n // 2 + n].rearrange("p (m t) -> p m t", m=FT)

    def spent_weights(self):
        assert FT * T <= self.mats["x_wq"][0]
        return self.weights[:, 0:FT * T].rearrange("p (m t) -> p m t", m=FT)

    def bank(self, i):
        return self.psum[i // 2][:, (i % 2) * CH:(i % 2 + 1) * CH]

    def w(self, name, k, first, n, rows=P):
        at, _, cols = self.mats[name]
        return self.weights[0:rows, at + k * cols + first:at + k * cols + first + n]

    def v(self, name, k):
        return self.vectors[:, self.vecs[name][0] + k:self.vecs[name][0] + k + 1]


def layer_norm_pe(pe, c, s):
    for j in range(NCH):
        pe.wait_ge(*s["ln_sum"](j + 1))
        pe.matmul(c.bank(j), c.mean_w[:], c.ln_s[:, j, :], start=True, stop=True).then_inc(s["ln_mean"].sem)
    for j in range(NCH):
        pe.wait_ge(*s["ln_sq"](j + 1))
        for k in range(FT):
            mm = pe.matmul(c.bank(2 + j), c.mean_w[:], c.slot(3)[:, k, j * CH:(j + 1) * CH],
                           start=(k == 0), stop=(k == FT - 1))
        mm.then_inc(s["ln_var"].sem)


def layer_norm_act(act, c, s, twice=False):
    for j in range(NCH):
        act.wait_ge(*s["ln_cent"](j + 1))
        act.activation(c.slot(3)[:, :, j * CH:(j + 1) * CH], c.slot(2)[:, :, j * CH:(j + 1) * CH],
                       ACT.Square).then_inc(s["ln_sq"].sem)
    for j in range(NCH):
        act.wait_ge(*s["ln_var"](j + 1))
        ins = act.activation(c.ln_d[:, j, :], c.bank(2 + j), ACT.Ln, bias=c.eps[:, 0:1])
        if twice:
            ins = act.activation(c.ln_s[:, j, :], c.bank(2 + j), ACT.Ln, bias=c.eps_eps[:, 0:1], scale=1.0 + LN_EPS)
        ins.then_inc(s["ln_log"].sem)
    for j in range(NCH):
        act.wait_ge(*s["ln_log"](j + 1))
        ins = act.activation(c.ln_r[:, j, :], c.ln_d[:, j, :], ACT.Exp, scale=-0.5)
        if twice:
            ins = act.activation(c.ln_s[:, j, :], c.ln_s[:, j, :], ACT.Exp, scale=-0.5)
        ins.then_inc(s["ln_rstd"].sem)


def layer_norm_dve(dve, c, s, x, out, gain=None, bias=None, twice=False, once_out=None):
    for j in range(NCH):
        dve.tensor_tensor(c.ln_s[:, j, :], x(0, j), x(1, j), ALU.add).then_inc(s["ln_sum"].sem)
    for j in range(NCH):
        dve.wait_ge(*s["ln_mean"](j + 1))
        for k in range(FT):
            ins = dve.tensor_tensor(c.slot(2)[:, k, j * CH:(j + 1) * CH], x(k, j), c.bank(j), ALU.subtract)
        ins.then_inc(s["ln_cent"].sem)
    factor = c.ln_s if twice else c.ln_r
    for j in range(NCH):
        dve.wait_ge(*s["ln_rstd"](j + 1))
        centred = lambda k: c.slot(2)[:, k, j * CH:(j + 1) * CH]
        for k in range(FT):
            if gain is None:
                ins = dve.tensor_tensor(out(k, j), centred(k), factor[:, j, :], ALU.mult)
            else:
                ins = dve.scalar_tensor_tensor(out=out(k, j), in0=centred(k), scalar=gain(k), in1=factor[:, j, :],
                                               op0=ALU.mult, op1=ALU.mult)
                ins.then_inc(s["ln_scaled"].sem)
        if gain is not None:
            for k in range(FT):
                dve.wait_ge(*s["ln_scaled"](FT * j + k + 1))
                ins = dve.tensor_scalar(out(k, j), out(k, j), bias(k), None, ALU.add)
        if once_out is None or j < NCH - 1:
            ins.then_inc(s["ln_out"].sem)
        if once_out is not None:
            for k in range(FT):
                ins = dve.tensor_tensor(once_out(k, j), centred(k), c.ln_r[:, j, :], ALU.mult)
            if j == NCH - 1:
                ins.then_inc(s["ln_out"].sem)


LN_SIGNALS = {"ln_sum": NCH, "ln_mean": NCH, "ln_cent": NCH, "ln_sq": NCH, "ln_var": NCH, "ln_log": NCH, "ln_rstd": NCH,
              "ln_scaled": FT * NCH, "ln_out": NCH}


def norm_signals():
    n = B * NCH
    return {"sum": n, "mean": n, "cent": n, "sq": n, "var": n, "log": n, "rstd": n, "scaled": FT * n}


def norm_both(nc, c, s, out, gain=None, bias=None, twice=False):
    N = B * NCH
    at = lambda t, j: t[:, :, j * CH:(j + 1) * CH]
    centred, squares = c.two_slots(4), c.two_slots(2)
    with nc.Block() as block:

        @block.tensor
        def _(pe):
            for j in range(N):
                pe.wait_ge(*s["sum"](j + 1))
                pe.matmul(c.bank(j), c.mean_w[:], c.ln[:, j, :], start=True, stop=True).then_inc(s["mean"].sem)
            for j in range(N):
                pe.wait_ge(*s["sq"](j + 1))
                for k in range(FT):
                    mm = pe.matmul(c.bank(N + j), c.mean_w[:], at(squares, j)[:, k, :], start=(k == 0), stop=(k == FT - 1))
                mm.then_inc(s["var"].sem)

        @block.scalar
        def _(act):
            for j in range(N):
                act.wait_ge(*s["cent"](j + 1))
                act.activation(at(squares, j), at(centred, j), ACT.Square).then_inc(s["sq"].sem)
            for j in range(N):
                act.wait_ge(*s["var"](j + 1))
                if twice:
                    ins = act.activation(c.ln[:, j, :], c.bank(N + j), ACT.Ln, bias=c.eps_eps[:, 0:1], scale=1.0 + LN_EPS)
                else:
                    ins = act.activation(c.ln[:, j, :], c.bank(N + j), ACT.Ln, bias=c.eps[:, 0:1])
                ins.then_inc(s["log"].sem)
            for j in range(N):
                act.wait_ge(*s["log"](j + 1))
                act.activation(c.ln[:, j, :], c.ln[:, j, :], ACT.Exp, scale=-0.5).then_inc(s["rstd"].sem)

        @block.vector
        def _(dve):
            for j in range(N):
                dve.tensor_tensor(c.ln[:, j, :], at(c.xT, j)[:, 0, :], at(c.xT, j)[:, 1, :], ALU.add).then_inc(s["sum"].sem)
            for j in range(N):
                dve.wait_ge(*s["mean"](j + 1))
                for k in range(FT):
                    ins = dve.tensor_tensor(at(centred, j)[:, k, :], at(c.xT, j)[:, k, :], c.bank(j), ALU.subtract)
                ins.then_inc(s["cent"].sem)
            for j in range(N):
                dve.wait_ge(*s["rstd"](j + 1))
                for k in range(FT):
                    to, of = at(out, j)[:, k, :], at(centred, j)[:, k, :]
                    if gain is None:
                        dve.tensor_tensor(to, of, c.ln[:, j, :], ALU.mult)
                    else:
                        dve.scalar_tensor_tensor(out=to, in0=of, scalar=gain(k), in1=c.ln[:, j, :],
                                                 op0=ALU.mult, op1=ALU.mult).then_inc(s["scaled"].sem)
                if gain is not None:
                    for k in range(FT):
                        dve.wait_ge(*s["scaled"](FT * j + k + 1))
                        dve.tensor_scalar(at(out, j)[:, k, :], at(out, j)[:, k, :], bias(k), None, ALU.add)


def clear_signals(nc, *groups, also=()):
    with nc.Block() as block:

        @block.gpsimd
        def _(pool):
            for sem in [sig.sem for group in groups for sig in group.values()] + list(also):
                pool.sem_clear(sem)


def signals(nc, ctx, layer, counts):
    return {name: Sig(ctx.enter_context(nc.semaphore(f"{layer}_{name}")), n) for name, n in counts.items()}


def set_round(b, *groups):
    for group in groups:
        for sig in group.values():
            sig.round = b


def linear_attention_layer(nc, c):
    DH = 64
    SCALE = float(DH) ** -0.25
    with ExitStack() as ctx:
        s = signals(nc, ctx, "a", dict(
            LN_SIGNALS, k_proj=4, k_max=4, k_shift=1, k_max_all=1, k_added=1, k_inv=1, zeroed=1, k_exp=4, k_turned=4, k_copied=4, v_proj=4, v_copied=4,
            q_proj=4, q_max=4, q_shift=4, q_exp=4, q_sum=4, q_inv=4, q_norm=4, q_turned=4, q_copied=4,
            ctx_done=1, ctx_copied=1, at_done=4, at_copied=4, o_done=4, y_done=4,
            ff_done=16, ff_gelu=16, f2_done=4, y2_done=4, d_done=4, x_done=4))
        s2 = signals(nc, ctx, "a2", LN_SIGNALS)
        sb = lambda name, shape: ctx.enter_context(nc.sbuf_tensor(name, shape, F32))
        k_mx = sb("a_k_mx", [P, FT, NCH])
        k_m = sb("a_k_m", [P, FT])
        k_s = sb("a_k_s", [P, FT, NCH])
        k_r = sb("a_k_r", [P, FT])
        q_m = sb("a_q_m", [P, 4, 8])
        q_s = sb("a_q_s", [P, 4, 8])
        context = sb("a_context", [P, FT, P])
        h1, h2, ek, v, ekt, qn = (c.slot(i) for i in range(6))
        v_t = v.rearrange("p a n -> p (a n)").rearrange("p (t n) -> p t n", t=TT)
        ekt_t = ekt.rearrange("p a n -> p (a n)").rearrange("p (t n) -> p t n", t=TT)
        q_t = qn.rearrange("p a n -> p (a n)").rearrange("p (u n) -> p u n", u=4)
        qt, at = c.slot(2), c.slot(5)
        y = h1
        hid = [c.arena[:, (2 + 2 * j) * 2048:(4 + 2 * j) * 2048].rearrange("p (f n) -> p f n", f=8) for j in range(NCH)]
        n_first = c.mats["x_wq"][0]
        part = (c.weights.shape[1] - n_first) // B
        assert n_first + B * part == c.weights.shape[1]
        with nc.Fori(0, B) as b:
            set_round(b, s, s2)
            x = lambda k, j: c.xT[:, k, bass.ds(b * S + j * CH, CH)]
            col = lambda t: (lambda k, j: t[:, k, j * CH:(j + 1) * CH])
            with nc.Block() as block:

                @block.sync
                def _(sync):
                    sync.wait_ge(c.first_loaded, 32)
                    sync.dma_start(c.weights[:, bass.ds(b * part + n_first, part)],
                                   c.weights_dram[:, bass.ds(b * part + n_first, part)]).then_inc(c.others_loaded, 16)

                @block.gpsimd
                def _(pool):
                    pool.memset(context[:], 0.0).then_inc(s["zeroed"].sem)

                @block.tensor
                def _(pe):
                    layer_norm_pe(pe, c, s)
                    pe.wait_ge(c.first_loaded, 32)
                    pe.wait_ge(*s["ln_out"](NCH))
                    for m in range(FT):
                        for j in range(NCH):
                            for k in range(FT):
                                mm = pe.matmul(c.bank(2 * m + j), c.w("a_wk", k, m * P, P), h2[:, k, j * CH:(j + 1) * CH],
                                               start=(k == 0), stop=(k == 1))
                            mm.then_inc(s["k_proj"].sem)
                    for u in range(4):
                        for t in (0, 1):
                            for k in range(FT):
                                mm = pe.matmul(c.bank(4 + u)[:, t * D:(t + 1) * D], h2[:, k, (2 * u + t) * P:(2 * u + t + 1) * P],
                                               c.w("a_wv", k, 0, D), start=(k == 0), stop=(k == 1))
                        mm.then_inc(s["v_proj"].sem)
                    for u in range(4):
                        pe.wait_ge(*s["v_copied"](u + 1))
                        for t in (0, 1):
                            for k in range(FT):
                                mm = pe.matmul(c.bank(4 + u)[:, t * D:(t + 1) * D], h2[:, k, (2 * u + t) * P:(2 * u + t + 1) * P],
                                               c.w("a_wq", k, 0, D), start=(k == 0), stop=(k == 1))
                        mm.then_inc(s["q_proj"].sem)
                    pe.wait_ge(*s["k_exp"](4))
                    for u in range(4):
                        for t in (0, 1):
                            for m in range(FT):
                                mm = pe.transpose(c.bank(u)[:, t * D + m * P:t * D + (m + 1) * P],
                                                  ek[:, m, (2 * u + t) * P:(2 * u + t + 1) * P], c.ident[:])
                        mm.then_inc(s["k_turned"].sem)
                    pe.wait_ge(*s["k_copied"](4))
                    for m in range(FT):
                        for t in range(TT):
                            mm = pe.matmul(c.bank(0)[:, m * P:(m + 1) * P], ekt_t[:, t, m * P:(m + 1) * P],
                                           v_t[:, t, m * P:(m + 1) * P], start=(t == 0), stop=(t == TT - 1))
                    mm.then_inc(s["ctx_done"].sem)
                    for u in range(4):
                        pe.wait_ge(*s["q_norm"](u + 1))
                        for m in range(FT):
                            for t in (0, 1):
                                mm = pe.transpose(c.bank(4 + u)[:, m * D + t * P:m * D + (t + 1) * P],
                                                  q_t[:, u, t * D + m * P:t * D + (m + 1) * P], c.ident[:])
                        mm.then_inc(s["q_turned"].sem)
                    pe.wait_ge(*s["ctx_copied"](1))
                    pe.wait_ge(*s["q_copied"](4))
                    for m in range(FT):
                        for j in range(NCH):
                            pe.matmul(c.bank(2 * m + j), context[:, m, :], qt[:, m, j * CH:(j + 1) * CH],
                                      start=True, stop=True).then_inc(s["at_done"].sem)
                    pe.wait_ge(*s["at_copied"](4))
                    for m in range(FT):
                        for j in range(NCH):
                            for k in range(FT):
                                mm = pe.matmul(c.bank(4 + 2 * m + j), c.w("a_wo", k, m * P, P), at[:, k, j * CH:(j + 1) * CH],
                                               start=(k == 0), stop=(k == 1))
                            mm.then_inc(s["o_done"].sem)
                    layer_norm_pe(pe, c, s2)
                    n = 0
                    for j in range(NCH):
                        pe.wait_ge(*s2["ln_out"](NCH))
                        for f in range(8):
                            if n >= 4:
                                pe.wait_ge(*s["ff_gelu"](n - 3))
                            for k in range(FT):
                                mm = pe.matmul(c.bank(4 + n % 4), c.w("a_w1", k, f * P, P), h2[:, k, j * CH:(j + 1) * CH],
                                               start=(k == 0), stop=(k == 1))
                            mm.then_inc(s["ff_done"].sem)
                            n += 1
                    for j in range(NCH):
                        pe.wait_ge(*s["ff_gelu"](8 * (j + 1)))
                        for m in range(FT):
                            for f in range(8):
                                mm = pe.matmul(c.bank(2 * m + j), c.w("a_w2", f, m * P, P), hid[j][:, f, :],
                                               start=(f == 0), stop=(f == 7))
                            mm.then_inc(s["f2_done"].sem)
                    pe.wait_ge(*s["ff_gelu"](16))
                    for j in range(NCH):
                        pe.wait_ge(*s["y2_done"](2 * (j + 1)))
                        for m in range(FT):
                            for k in range(FT):
                                mm = pe.matmul(c.bank(4 + 2 * m + j), c.w("a_wd", k, m * P, P), y[:, k, j * CH:(j + 1) * CH],
                                               start=(k == 0), stop=(k == 1))
                            mm.then_inc(s["d_done"].sem)

                @block.scalar
                def _(act):
                    layer_norm_act(act, c, s, twice=True)
                    act.wait_ge(*s["k_shift"](1))
                    for m in range(FT):
                        for j in range(NCH):
                            act.activation(ek[:, m, j * CH:(j + 1) * CH], c.bank(2 * m + j), ACT.Exp, bias=k_m[:, m:m + 1],
                                           scale=SCALE, accum_out=k_s[:, m, j:j + 1]).then_inc(s["k_exp"].sem)
                    for u in range(4):
                        act.wait_ge(*s["q_shift"](u + 1))
                        act.activation(q_t[:, u, :], q_t[:, u, :], ACT.Exp, scale=SCALE).then_inc(s["q_exp"].sem)
                    for u in range(4):
                        act.wait_ge(*s["k_turned"](u + 1))
                        act.activation(ekt_t[:, 2 * u:2 * u + 2, :].rearrange("p t n -> p (t n)"), c.bank(u), ACT.Copy)\
                           .then_inc(s["k_copied"].sem)
                    for u in range(4):
                        act.wait_ge(*s["q_turned"](u + 1))
                        act.activation(qt[:, :, u * D:(u + 1) * D], c.bank(4 + u).rearrange("p (m n) -> p m n", m=FT),
                                       ACT.Copy).then_inc(s["q_copied"].sem)
                    for m in range(FT):
                        for j in range(NCH):
                            act.wait_ge(*s["at_done"](2 * m + j + 1))
                            act.activation(at[:, m, j * CH:(j + 1) * CH], c.bank(2 * m + j), ACT.Copy)\
                               .then_inc(s["at_copied"].sem)
                    layer_norm_act(act, c, s2)
                    n = 0
                    act.wait_ge(*s2["ln_out"](NCH))
                    for j in range(NCH):
                        for f in range(8):
                            act.wait_ge(*s["ff_done"](n + 1))
                            act.activation(hid[j][:, f, :], c.bank(4 + n % 4), ACT.Gelu_apprx_tanh,
                                           bias=c.v("a_bf1", f)).then_inc(s["ff_gelu"].sem)
                            n += 1

                @block.vector
                def _(dve):
                    layer_norm_dve(dve, c, s, x, col(h2), lambda k: c.v("a_g1", k), lambda k: c.v("a_b1", k), twice=True, once_out=col(h1))
                    for m in range(FT):
                        for j in range(NCH):
                            dve.wait_ge(*s["k_proj"](2 * m + j + 1))
                            dve.tensor_reduce(k_mx[:, m, j:j + 1], c.bank(2 * m + j), AX, ALU.max).then_inc(s["k_max"].sem)
                    dve.wait_ge(*s["k_max"](4))
                    dve.tensor_reduce(k_m[:], k_mx[:], AX, ALU.max).then_inc(s["k_max_all"].sem)
                    dve.wait_ge(*s["k_max_all"](1))
                    dve.tensor_scalar(k_m[:], k_m[:], -SCALE, None, ALU.mult).then_inc(s["k_shift"].sem)
                    for u in range(4):
                        dve.wait_ge(*s["v_proj"](u + 1))
                        dve.tensor_copy(v_t[:, 2 * u:2 * u + 2, :].rearrange("p t n -> p (t n)"), c.bank(4 + u))\
                           .then_inc(s["v_copied"].sem)
                    heads = lambda ap: ap.rearrange("p (h d) -> p h d", d=DH)
                    wide = lambda ap: ap.unsqueeze(2).to_broadcast([P, 8, DH])
                    for u in range(4):
                        dve.wait_ge(*s["q_proj"](u + 1))
                        dve.tensor_reduce(q_m[:, u, :], heads(c.bank(4 + u)), AX, ALU.max).then_inc(s["q_max"].sem)
                        dve.wait_ge(*s["q_max"](u + 1))
                        dve.tensor_tensor(heads(q_t[:, u, :]), heads(c.bank(4 + u)), wide(q_m[:, u, :]), ALU.subtract)\
                           .then_inc(s["q_shift"].sem)
                    for u in range(4):
                        dve.wait_ge(*s["q_exp"](u + 1))
                        dve.tensor_reduce(q_s[:, u, :], heads(q_t[:, u, :]), AX, ALU.add).then_inc(s["q_sum"].sem)
                        dve.wait_ge(*s["q_sum"](u + 1))
                        dve.reciprocal(q_s[:, u, :], q_s[:, u, :]).then_inc(s["q_inv"].sem)
                        dve.wait_ge(*s["q_inv"](u + 1))
                        dve.tensor_tensor(heads(q_t[:, u, :]), heads(q_t[:, u, :]), wide(q_s[:, u, :]), ALU.mult)\
                           .then_inc(s["q_norm"].sem)
                    dve.wait_ge(*s["k_exp"](4))
                    dve.tensor_tensor(k_r[:], k_s[:, :, 0], k_s[:, :, 1], ALU.add).then_inc(s["k_added"].sem)
                    dve.wait_ge(*s["k_added"](1))
                    dve.reciprocal(k_r[:], k_r[:]).then_inc(s["k_inv"].sem)
                    dve.wait_ge(*s["k_inv"](1))
                    dve.wait_ge(*s["zeroed"](1))
                    dve.wait_ge(*s["ctx_done"](1))
                    for m in range(FT):
                        for h in (0, DH):
                            ins = dve.tensor_scalar(context[h:h + DH, m, h:h + DH], c.bank(0)[h:h + DH, m * P + h:m * P + h + DH],
                                                    k_r[h:h + DH, m:m + 1], None, ALU.mult)
                    ins.then_inc(s["ctx_copied"].sem)
                    for m in range(FT):
                        for j in range(NCH):
                            dve.wait_ge(*s["o_done"](2 * m + j + 1))
                            dve.scalar_tensor_tensor(out=y[:, m, j * CH:(j + 1) * CH], in0=c.bank(4 + 2 * m + j),
                                                     scalar=c.v("a_bo", m), in1=h1[:, m, j * CH:(j + 1) * CH],
                                                     op0=ALU.add, op1=ALU.add).then_inc(s["y_done"].sem)
                    dve.wait_ge(*s["y_done"](4))
                    layer_norm_dve(dve, c, s2, col(y), col(h2), lambda k: c.v("a_g2", k), lambda k: c.v("a_b2", k))
                    for j in range(NCH):
                        for m in range(FT):
                            dve.wait_ge(*s["f2_done"](2 * j + m + 1))
                            dve.scalar_tensor_tensor(out=y[:, m, j * CH:(j + 1) * CH], in0=c.bank(2 * m + j),
                                                     scalar=c.v("a_bf2", m), in1=y[:, m, j * CH:(j + 1) * CH],
                                                     op0=ALU.add, op1=ALU.add).then_inc(s["y2_done"].sem)
                    for j in range(NCH):
                        for m in range(FT):
                            dve.wait_ge(*s["d_done"](2 * j + m + 1))
                            dve.scalar_tensor_tensor(out=x(m, j), in0=c.bank(4 + 2 * m + j), scalar=c.v("a_bd", m),
                                                     in1=x(m, j), op0=ALU.add, op1=ALU.add).then_inc(s["x_done"].sem)
        clear_signals(nc, s, s2)


def cross_attention_layer(nc, c):
    H, DH = 4, 64
    SCALE = DH ** -0.5
    HP = H // FT
    NB = TT + 1
    UNITS = TT * H
    TILES = 3 * UNITS + 2 * TT
    KC = [P, CF - P]
    with ExitStack() as ctx:
        norm_s = signals(nc, ctx, "xn", norm_signals())
        s = signals(nc, ctx, "x", dict(
            ln_in=1, q_proj=4, k_proj=4, v_proj=4, raw=8, square=8, ms=8, ms_max=8, ms_log=8, inv=8, scaled=8, high=8, q_rest=4, k_rest=4, v_copied=4,
            ctx_v=1, scores=UNITS, shift=UNITS, ctx_max=TT, row_max=UNITS, expd=UNITS,
            padded=1, turned=TILES, copied=TILES, av=UNITS, den=TT, den_inv=TT, normed=TT, o_done=4, x_done=4))
        g = signals(nc, ctx, "xc", dict(load=1, made=4, mean=1, cent=1, sq=1, var=1, log=1, rstd=1, scaled=1,
                                        out=1, k=1, v=1, raw=1, square=1, ms=1, ms_max=1, ms_log=1, inv=1, kn=1, vc=1,
                                        mask=1, mask2=1))
        set_round(0, g)
        sb = lambda name, shape, dt=F32: ctx.enter_context(nc.sbuf_tensor(name, shape, dt))
        same_head = sb("x_same_head", [P, P])
        ctx_mean = sb("x_ctx_mean", [P, P])
        mask_u8 = sb("x_mask_u8", [P, B * KEYS], U8)
        mask_add = sb("x_mask_add", [P, B * KEYS])
        cx = sb("x_cx", [P, 2, B * KEYS])
        cs = sb("x_cs", [P, 2, B * KEYS])
        cr = sb("x_cr", [P, 2, B * KEYS])
        k_ctx = sb("x_k_ctx", [P, FT, B * KEYS])
        v_ctx_all = sb("x_v_ctx_all", [KEYS, B, D])
        k_ctx_now = sb("x_k_ctx_now", [P, FT, P])
        mask_sel = sb("x_mask_sel", [P, H * KEYS])
        v_ctx = sb("x_v_ctx", [KEYS, D])
        turned = [sb(f"x_turned{i}", [P, NB, P]) for i in range(2)]
        q_high, q_rest, k_high, k_rest = (sb(f"x_{n}", [P, FT, S], F32R) for n in ("q_high", "q_rest", "k_high", "k_rest"))
        o = sb("x_o", [P, 2, D])
        ctx_s = sb("x_ctx_s", [P, 2, H * KEYS])
        mxc = sb("x_mxc", [P, 2, H])
        mx = sb("x_mx", [P, 2])
        nm = sb("x_nm", [P, 2])
        rs = sb("x_rs", [P, 2, H, 2])
        rr = sb("x_rr", [P, 2, H])
        qt, scr, inv, kt, v = (c.slot(i) for i in range(1, 6))
        ot = c.slot(0)
        k_sq = ot
        n_used = FT * T
        ln = c.weights[:, n_used:n_used + FT * S].rearrange("p (m t) -> p m t", m=FT)
        assert n_used + FT * S <= c.mats["x_wq"][0]
        v_t = v.rearrange("p a n -> p (a n)").rearrange("p (t n) -> p t n", t=TT)
        probs = [c.arena[:, (2 + i) * 2048:(2 + i) * 2048 + NB * P] for i in range(2)]

        with nc.Block() as block:

            @block.sync
            def _(sync):
                sync.dma_start(cx[:], c.ctx_t).then_inc(g["load"].sem, 16)
                sync.dma_start(mask_u8[:], c.mask[0, :].partition_broadcast(P)).then_inc(g["load"].sem, 16)

            @block.gpsimd
            def _(pool):
                pool.memset(ctx_mean[:], 1.0 / CF)
                pool.memset(k_ctx_now[:], 0.0)
                pool.memset(same_head[:], 0.0).then_inc(g["made"].sem)
                pool.wait_ge(*g["made"](1))
                pool.memset(same_head[0:DH, 0:DH], 1.0 / DH)
                pool.memset(same_head[DH:P, DH:P], 1.0 / DH).then_inc(g["made"].sem)

            @block.tensor
            def _(pe):
                pe.wait_ge(*g["made"](2))
                pe.wait_ge(g["load"].sem, 32)
                for k in range(2):
                    mm = pe.matmul(c.bank(0)[:, 0:P], ctx_mean[0:KC[k], :], cx[0:KC[k], k, :], start=(k == 0), stop=(k == 1))
                mm.then_inc(g["mean"].sem)
                pe.wait_ge(*g["sq"](1))
                for k in range(2):
                    mm = pe.matmul(c.bank(1)[:, 0:P], ctx_mean[0:KC[k], :], cs[0:KC[k], k, :], start=(k == 0), stop=(k == 1))
                mm.then_inc(g["var"].sem)
                pe.wait_ge(*g["out"](1))
                for m in range(FT):
                    for k in range(2):
                        mm = pe.matmul(c.bank(2)[:, m * P:(m + 1) * P], c.w("x_wkv", k, m * P, P, KC[k]), cx[0:KC[k], k, :],
                                       start=(k == 0), stop=(k == 1))
                mm.then_inc(g["k"].sem)
                for b in range(B):
                    for k in range(2):
                        mm = pe.matmul(c.bank(3)[0:KEYS, b * D:(b + 1) * D], cx[0:KC[k], k, b * KEYS:(b + 1) * KEYS],
                                       c.w("x_wkv", k, D, D, KC[k]), start=(k == 0), stop=(k == 1))
                mm.then_inc(g["v"].sem)
                pe.wait_ge(*g["square"](1))
                pe.matmul(c.bank(4)[:, 0:D], same_head[:], cs[:].rearrange("p m n -> p (m n)"), start=True, stop=True)\
                  .then_inc(g["ms"].sem)

            @block.scalar
            def _(act):
                act.wait_ge(*g["cent"](1))
                for k in range(2):
                    ins = act.activation(cs[0:KC[k], k, :], cx[0:KC[k], k, :], ACT.Square)
                ins.then_inc(g["sq"].sem)
                act.wait_ge(*g["var"](1))
                act.activation(cr[:, 0, :], c.bank(1)[:, 0:P], ACT.Ln, bias=c.eps[:, 0:1]).then_inc(g["log"].sem)
                act.wait_ge(*g["log"](1))
                act.activation(cr[:, 1, :], cr[:, 0, :], ACT.Exp, scale=-0.5).then_inc(g["rstd"].sem)
                act.wait_ge(*g["k"](1))
                act.activation(k_ctx[:].rearrange("p m n -> p (m n)"), c.bank(2)[:, 0:D], ACT.Copy).then_inc(g["raw"].sem)
                act.activation(cs[:].rearrange("p m n -> p (m n)"), c.bank(2)[:, 0:D], ACT.Square).then_inc(g["square"].sem)
                act.wait_ge(*g["ms_max"](1))
                act.activation(cr[:], cr[:], ACT.Ln).then_inc(g["ms_log"].sem)
                act.wait_ge(*g["ms_log"](1))
                act.activation(cr[:], cr[:], ACT.Exp, scale=-0.5).then_inc(g["inv"].sem)

            @block.vector
            def _(dve):
                dve.wait_ge(*g["mean"](1))
                for k in range(2):
                    ins = dve.tensor_tensor(cx[0:KC[k], k, :], cx[0:KC[k], k, :], c.bank(0)[0:KC[k], 0:P], ALU.subtract)
                ins.then_inc(g["cent"].sem)
                dve.wait_ge(*g["rstd"](1))
                for k in range(2):
                    ins = dve.scalar_tensor_tensor(out=cx[0:KC[k], k, :], in0=cx[0:KC[k], k, :], scalar=c.v("x_gx", k)[0:KC[k], :],
                                                   in1=cr[0:KC[k], 1, :], op0=ALU.mult, op1=ALU.mult)
                ins.then_inc(g["scaled"].sem)
                dve.wait_ge(*g["scaled"](1))
                for k in range(2):
                    ins = dve.tensor_scalar(cx[0:KC[k], k, :], cx[0:KC[k], k, :], c.v("x_bx", k)[0:KC[k], :], None, ALU.add)
                ins.then_inc(g["out"].sem)
                dve.tensor_copy(mask_add[:], mask_u8[:]).then_inc(g["mask"].sem)
                dve.wait_ge(*g["mask"](1))
                dve.tensor_scalar(mask_add[:], mask_add[:], -1.0, -NEG, ALU.add, ALU.mult).then_inc(g["mask2"].sem)
                dve.wait_ge(*g["v"](1))
                dve.tensor_copy(v_ctx_all[:].rearrange("p b n -> p (b n)"), c.bank(3)[0:KEYS, :]).then_inc(g["vc"].sem)
                dve.wait_ge(*g["ms"](1))
                dve.tensor_scalar(cr[:].rearrange("p m n -> p (m n)"), c.bank(4)[:, 0:D], 1e-16, None, ALU.max)\
                   .then_inc(g["ms_max"].sem)
                dve.wait_ge(*g["inv"](1))
                dve.scalar_tensor_tensor(out=k_ctx[:], in0=k_ctx[:], scalar=c.v("x_gk", 0), in1=cr[:],
                                         op0=ALU.mult, op1=ALU.mult).then_inc(g["kn"].sem)

        xn_all = c.spent_weights()
        norm_both(nc, c, norm_s, xn_all, lambda k: c.v("x_gl", k), lambda k: c.v("x_bl", k), twice=True)
        with nc.Fori(0, B) as b:
            set_round(b, s)
            x = lambda k, j: c.xT[:, k, bass.ds(b * S + j * CH, CH)]
            order = [("c", 0, 0)]
            for u in range(UNITS + 2):
                if u < UNITS:
                    order += [("p", u, 0), ("p", u, 1)]
                if (u + 2) % H == 0 and u + 2 < UNITS:
                    order.append(("c", (u + 2) // H, 0))
                if u >= 2 and (u - 2) % H == H - 1:
                    order.append(("o", (u - 2) // H, 0))
                if u < UNITS:
                    order.append(("p", u, 2))
            nth = {what: n for n, what in enumerate(order)}
            assert len(order) == TILES
            turn_bank = lambda what: c.bank(5 + nth[what] % 2)
            score = lambda u: c.psum[u % 2]
            out_bank = lambda qi: c.bank(4 if qi % 2 else 7)
            with nc.Block() as block:

                def rest_of(engine, t, high, rest, first, done):
                    for n in range(4):
                        m, j = divmod(n, NCH)
                        at = (slice(None), m, slice(j * CH, (j + 1) * CH))
                        engine.wait_ge(*s["high"](first + n + 1))
                        engine.tensor_tensor(rest[at], t[at], high[at].bitcast(F32), ALU.subtract).then_inc(done.sem)

                @block.gpsimd
                def _(pool):
                    pool.tensor_copy(ln, xn_all[:, :, bass.ds(b * S, S)]).then_inc(s["ln_in"].sem)
                    rest_of(pool, qt, q_high, q_rest, 0, s["q_rest"])

                @block.tensor
                def _(pe):
                    for name, base, first, done in (("x_wq", 0, 0, s["q_proj"]), ("x_wlkv", 4, 0, s["k_proj"])):
                        for m in range(FT):
                            for j in range(NCH):
                                for k in range(FT):
                                    mm = pe.matmul(c.bank(base + 2 * m + j), c.w(name, k, m * P, P),
                                                   xn_all[:, k, bass.ds(b * S + j * CH, CH)], start=(k == 0), stop=(k == 1))
                                mm.then_inc(done.sem)
                    for n in range(8):
                        pe.wait_ge(*s["square"](n + 1))
                        pe.wait_ge(*s["raw"](n + 1))
                        m, j = (n % 4) // 2, n % 2
                        pe.matmul(c.bank(n), same_head[:], scr[:, m, j * CH:(j + 1) * CH] if n < 4 else
                                  k_sq[:, m, j * CH:(j + 1) * CH], start=True, stop=True).then_inc(s["ms"].sem)
                    for t2 in range(4):
                        pe.wait_ge(*s["ms_max"](t2 + 1))
                        if t2 == 0:
                            pe.wait_ge(*s["ln_in"](1))
                        for t in (0, 1):
                            for k in range(FT):
                                mm = pe.matmul(c.bank(t2)[:, t * D:(t + 1) * D], ln[:, k, (2 * t2 + t) * P:(2 * t2 + t + 1) * P],
                                               c.w("x_wlkv", k, D, D), start=(k == 0), stop=(k == 1))
                        mm.then_inc(s["v_proj"].sem)

                    def scores(u):
                        qi, h = divmod(u, H)
                        m, at = h // HP, (h % HP) * DH
                        if u == 0:
                            pe.wait_ge(*s["scaled"](8))
                            pe.wait_ge(*s["q_rest"](4))
                            pe.wait_ge(*s["k_rest"](4))
                            pe.wait_ge(*s["v_copied"](4))
                        if h == 0:
                            n = nth["c", qi, 0]
                            half = turn_bank(("c", qi, 0))[:, 0:D]
                            if n >= 2:
                                pe.wait_ge(*s["copied"](n - 1))
                            for i in range(FT):
                                mm = pe.matmul(half[:, i * P:(i + 1) * P], qt[:, i, qi * P:(qi + 1) * P],
                                               k_ctx_now[:, i, :], start=True, stop=True)
                            mm.then_inc(s["turned"].sem)
                        if u >= 2:
                            pe.wait_ge(*s["expd"](u - 1))
                        passes = ((q_high, k_high), (q_high, k_rest), (q_rest, k_high))
                        for j in range(NCH):
                            for n, (q_part, k_part) in enumerate(passes):
                                mm = pe.matmul(score(u)[:, j * CH:(j + 1) * CH], q_part[at:at + DH, m, qi * P:(qi + 1) * P],
                                               k_part[at:at + DH, m, j * CH:(j + 1) * CH], start=(n == 0), stop=(n == 2))
                        mm.then_inc(s["scores"].sem)

                    def turn(u, i):
                        n = nth["p", u, i]
                        pe.wait_ge(*s["expd"](u + 1))
                        if u == 0:
                            pe.wait_ge(*s["padded"](1))
                        if n >= 2:
                            pe.wait_ge(*s["copied"](n - 1))
                        blocks = range(4 * i, min(4 * i + 4, NB))
                        for kb in blocks:
                            mm = pe.transpose(turn_bank(("p", u, i))[:, (kb % 4) * P:(kb % 4 + 1) * P],
                                              probs[u % 2][:, kb * P:(kb + 1) * P], c.ident[:])
                        mm.then_inc(s["turned"].sem)

                    def turn_outputs(qi):
                        n = nth["o", qi, 0]
                        pe.wait_ge(*s["normed"](qi + 1))
                        pe.wait_ge(*s["copied"](n - 1))
                        for m in range(FT):
                            mm = pe.transpose(turn_bank(("o", qi, 0))[:, m * P:(m + 1) * P], o[:, qi % 2, m * P:(m + 1) * P], c.ident[:])
                        mm.then_inc(s["turned"].sem)

                    def values(u):
                        qi, h = divmod(u, H)
                        pe.wait_ge(*s["copied"](nth["p", u, 2] + 1))
                        if h == 0 and qi >= 2:
                            pe.wait_ge(*s["normed"](qi - 1))
                        out = out_bank(qi)[:, h * DH:(h + 1) * DH]
                        for kb in range(TT):
                            pe.matmul(out, turned[u % 2][:, kb, :], v_t[:, kb, h * DH:(h + 1) * DH], start=(kb == 0), stop=False)
                        pe.matmul(out, turned[u % 2][0:KEYS, TT, :], v_ctx[:, h * DH:(h + 1) * DH], start=False, stop=True)\
                          .then_inc(s["av"].sem)

                    pe.wait_ge(*s["ctx_v"](1))
                    scores(0)
                    scores(1)
                    for u in range(UNITS + 2):
                        if u < UNITS:
                            turn(u, 0)
                            turn(u, 1)
                        if u + 2 < UNITS:
                            scores(u + 2)
                        if u >= 2 and (u - 2) % H == H - 1:
                            turn_outputs((u - 2) // H)
                        if 1 <= u <= UNITS:
                            values(u - 1)
                        if u < UNITS:
                            turn(u, 2)
                    pe.wait_ge(*s["copied"](TILES))
                    for m in range(FT):
                        for j in range(NCH):
                            for k in range(FT):
                                mm = pe.matmul(c.bank(2 * m + j), c.w("x_wo", k, m * P, P), ot[:, k, j * CH:(j + 1) * CH],
                                               start=(k == 0), stop=(k == 1))
                            mm.then_inc(s["o_done"].sem)

                @block.scalar
                def _(act):
                    for n in range(8):
                        m, j = (n % 4) // 2, n % 2
                        done = s["q_proj"] if n < 4 else s["k_proj"]
                        act.wait_ge(*done(n % 4 + 1))
                        act.activation((qt if n < 4 else kt)[:, m, j * CH:(j + 1) * CH], c.bank(n), ACT.Copy).then_inc(s["raw"].sem)
                        act.activation((scr if n < 4 else k_sq)[:, m, j * CH:(j + 1) * CH], c.bank(n), ACT.Square)\
                           .then_inc(s["square"].sem)
                    for f, ready, done in ((ACT.Ln, s["ms_max"], s["ms_log"]), (ACT.Exp, s["ms_log"], s["inv"])):
                        for n in range(8):
                            m, j = (n % 4) // 2, n % 2
                            act.wait_ge(*ready(n + 1))
                            half = (inv if n < 4 else scr)[:, m, j * CH:(j + 1) * CH]
                            act.activation(half, half, f, scale=1.0 if f == ACT.Ln else -0.5).then_inc(done.sem)

                    for n in range(8):
                        m, j = (n % 4) // 2, n % 2
                        act.wait_ge(*s["scaled"](n + 1))
                        act.activation((q_high if n < 4 else k_high)[:, m, j * CH:(j + 1) * CH],
                                       (qt if n < 4 else kt)[:, m, j * CH:(j + 1) * CH], ACT.Copy).then_inc(s["high"].sem)

                    def exps(u):
                        qi, h = divmod(u, H)
                        act.wait_ge(*s["shift"](u + 1))
                        if u == 0:
                            act.wait_ge(*s["scaled"](8))
                        if u >= 2:
                            act.wait_ge(*s["turned"](nth["p", u - 2, 2] + 1))
                        act.activation(probs[u % 2][:, 0:S], score(u)[:], ACT.Exp, bias=nm[:, u % 2:u % 2 + 1], scale=SCALE,
                                       accum_out=rs[:, qi % 2, h, 0:1])
                        act.activation(probs[u % 2][:, S:S + KEYS], ctx_s[:, qi % 2, h * KEYS:(h + 1) * KEYS],
                                       ACT.Exp, bias=nm[:, u % 2:u % 2 + 1], scale=SCALE,
                                       accum_out=rs[:, qi % 2, h, 1:2]).then_inc(s["expd"].sem)

                    for u in range(UNITS):
                        exps(u)

                @block.vector
                def _(dve):
                    for h in range(HP):
                        dve.tensor_copy(k_ctx_now[h * DH:(h + 1) * DH, :, h * KEYS:(h + 1) * KEYS],
                                        k_ctx[h * DH:(h + 1) * DH, :, bass.ds(b * KEYS, KEYS)])
                    for h in range(H):
                        dve.tensor_copy(mask_sel[:, h * KEYS:(h + 1) * KEYS], mask_add[:, bass.ds(b * KEYS, KEYS)])
                    dve.tensor_copy(v_ctx[:], v_ctx_all[:].rearrange("p b n -> p (b n)")[:, bass.ds(b * D, D)]).then_inc(s["ctx_v"].sem)
                    for n in range(8):
                        m, j = (n % 4) // 2, n % 2
                        dve.wait_ge(*s["ms"](n + 1))
                        dve.tensor_scalar((inv if n < 4 else scr)[:, m, j * CH:(j + 1) * CH], c.bank(n), 1e-16, None, ALU.max)\
                           .then_inc(s["ms_max"].sem)
                    for n in range(8):
                        m, j = (n % 4) // 2, n % 2
                        dve.wait_ge(*s["inv"](n + 1))
                        t = (qt if n < 4 else kt)[:, m, j * CH:(j + 1) * CH]
                        dve.scalar_tensor_tensor(out=t, in0=t, scalar=c.v("x_gq" if n < 4 else "x_gk", 0),
                                                 in1=(inv if n < 4 else scr)[:, m, j * CH:(j + 1) * CH],
                                                 op0=ALU.mult, op1=ALU.mult).then_inc(s["scaled"].sem)

                    for t2 in range(4):
                        dve.wait_ge(*s["v_proj"](t2 + 1))
                        dve.tensor_copy(v_t[:, 2 * t2:2 * t2 + 2, :].rearrange("p t n -> p (t n)"), c.bank(t2)).then_inc(s["v_copied"].sem)
                    rest_of(dve, kt, k_high, k_rest, 4, s["k_rest"])

                    def shift(u):
                        qi, h = divmod(u, H)
                        if h == 0:
                            dve.wait_ge(*s["turned"](nth["c", qi, 0] + 1))
                            if qi >= 2:
                                dve.wait_ge(*s["expd"](H * (qi - 1)))
                            bank = turn_bank(("c", qi, 0))[:, 0:D]
                            dve.tensor_tensor(ctx_s[:, qi % 2, :], bank, mask_sel[:], ALU.add).then_inc(s["copied"].sem)
                            dve.wait_ge(*s["copied"](nth["c", qi, 0] + 1))
                            dve.tensor_reduce(mxc[:, qi % 2, :], ctx_s[:, qi % 2, :].rearrange("p (h n) -> p h n", h=H), AX, ALU.max)\
                               .then_inc(s["ctx_max"].sem)
                            dve.wait_ge(*s["ctx_max"](qi + 1))
                        dve.wait_ge(*s["scores"](u + 1))
                        dve.tensor_reduce(mx[:, u % 2:u % 2 + 1], score(u)[:], AX, ALU.max).then_inc(s["row_max"].sem)
                        dve.wait_ge(*s["row_max"](u + 1))
                        dve.tensor_scalar(nm[:, u % 2:u % 2 + 1], mx[:, u % 2:u % 2 + 1], mxc[:, qi % 2, h:h + 1], -SCALE,
                                          ALU.max, ALU.mult).then_inc(s["shift"].sem)

                    def copy_turned(u, i):
                        n = nth["p", u, i]
                        dve.wait_ge(*s["turned"](n + 1))
                        if u >= 2 and i == 0:
                            dve.wait_ge(*s["av"](u - 1))
                        blocks = range(4 * i, min(4 * i + 4, NB))
                        rows = P if i < 2 else KEYS
                        dve.tensor_copy(turned[u % 2][0:rows, blocks[0]:blocks[-1] + 1, :].rearrange("p k n -> p (k n)"),
                                        turn_bank(("p", u, i))[0:rows, 0:len(blocks) * P]).then_inc(s["copied"].sem)

                    def copy_outputs(qi):
                        n = nth["o", qi, 0]
                        dve.wait_ge(*s["turned"](n + 1))
                        dve.tensor_copy(ot[:, :, qi * P:(qi + 1) * P], turn_bank(("o", qi, 0))[:, 0:D].rearrange("p (m n) -> p m n", m=FT))\
                           .then_inc(s["copied"].sem)

                    def norm(qi):
                        dve.wait_ge(*s["av"](H * (qi + 1)))
                        dve.wait_ge(*s["expd"](H * (qi + 1)))
                        dve.tensor_reduce(rr[:, qi % 2, :], rs[:, qi % 2, :, :], AX, ALU.add).then_inc(s["den"].sem)
                        dve.wait_ge(*s["den"](qi + 1))
                        dve.reciprocal(rr[:, qi % 2, :], rr[:, qi % 2, :]).then_inc(s["den_inv"].sem)
                        dve.wait_ge(*s["den_inv"](qi + 1))
                        dve.tensor_tensor(o[:, qi % 2, :].rearrange("p (h d) -> p h d", h=H),
                                          out_bank(qi)[:, 0:D].rearrange("p (h d) -> p h d", h=H),
                                          rr[:, qi % 2, :].unsqueeze(2).to_broadcast([P, H, DH]), ALU.mult).then_inc(s["normed"].sem)

                    dve.wait_ge(*s["scaled"](8))
                    for i in range(2):
                        ins = dve.memset(probs[i][:, S + KEYS:], 0.0)
                    ins.then_inc(s["padded"].sem)
                    shift(0)
                    shift(1)
                    for u in range(UNITS + 2):
                        if u < UNITS:
                            copy_turned(u, 0)
                            copy_turned(u, 1)
                        if u + 2 < UNITS:
                            shift(u + 2)
                        if u >= 2 and (u - 2) % H == H - 1:
                            copy_outputs((u - 2) // H)
                        if 1 <= u <= UNITS and (u - 1) % H == H - 1:
                            norm((u - 1) // H)
                        if u < UNITS:
                            copy_turned(u, 2)
                    for m in range(FT):
                        for j in range(NCH):
                            dve.wait_ge(*s["o_done"](2 * m + j + 1))
                            dve.scalar_tensor_tensor(out=x(m, j), in0=c.bank(2 * m + j), scalar=c.v("x_bo", m),
                                                     in1=x(m, j), op0=ALU.add, op1=ALU.add).then_inc(s["x_done"].sem)
        clear_signals(nc, norm_s, s, g)


def gated_recurrence_layer(nc, c):
    GATES = (("f_wf", "f_uf", "f_bf"), ("f_wi", "f_ui", "f_bi"), ("f_wc", "f_uc", "f_bc"))
    NG = len(GATES)
    N = NG * FT * NCH
    with ExitStack() as ctx:
        ln = signals(nc, ctx, "fn", norm_signals())
        s = signals(nc, ctx, "f", dict(gate_in=N, gate=N, fed=4, kept=4, cell=4))
        s2 = signals(nc, ctx, "f2", dict(o_done=4, tanh=4, x_done=4))
        first = ctx.enter_context(nc.semaphore("f_first_cell"))
        xn_all = c.spent_weights()
        cell, fed = c.slot(1), c.slot(5)
        gates = [c.slot(i) for i in (2, 3, 4)]
        norm_both(nc, c, ln, xn_all)
        with nc.Block() as block:

            @block.vector
            def _(dve):
                dve.memset(cell, 0.0).then_inc(first)
                dve.wait_ge(first, 1)
                for k in range(FT):
                    dve.tensor_scalar(cell[:, k, :], cell[:, k, :], c.v("f_c0", k), None, ALU.add)

        with nc.Fori(0, B) as b:
            set_round(b, s)
            with nc.Block() as block:

                @block.tensor
                def _(pe):
                    n = 0
                    for j in range(NCH):
                        for m in range(FT):
                            for w, u, _ in GATES:
                                if n >= 8:
                                    pe.wait_ge(*s["gate"](n - 7))
                                for k in range(FT):
                                    pe.matmul(c.bank(n % 8), c.w(w, k, m * P, P), xn_all[:, k, bass.ds(b * S + j * CH, CH)],
                                              start=(k == 0), stop=False)
                                for k in range(FT):
                                    mm = pe.matmul(c.bank(n % 8), c.w(u, k, m * P, P), cell[:, k, j * CH:(j + 1) * CH],
                                                   start=False, stop=(k == 1))
                                mm.then_inc(s["gate_in"].sem)
                                n += 1

                @block.scalar
                def _(act):
                    n = 0
                    for j in range(NCH):
                        for m in range(FT):
                            for i, (_, _, bias) in enumerate(GATES):
                                act.wait_ge(*s["gate_in"](n + 1))
                                act.activation(gates[i][:, m, j * CH:(j + 1) * CH], c.bank(n % 8),
                                               ACT.Tanh if i == 2 else ACT.Sigmoid, bias=c.v(bias, m)).then_inc(s["gate"].sem)
                                n += 1

                @block.vector
                def _(dve):
                    f, i, g = gates
                    for j in range(NCH):
                        dve.wait_ge(*s["gate"](NG * FT * (j + 1)))
                        for m in range(FT):
                            at = lambda t: t[:, m, j * CH:(j + 1) * CH]
                            n = FT * j + m + 1
                            dve.tensor_tensor(at(fed), at(i), at(g), ALU.mult).then_inc(s["fed"].sem)
                            dve.tensor_tensor(at(cell), at(f), at(cell), ALU.mult).then_inc(s["kept"].sem)
                            dve.wait_ge(*s["fed"](n))
                            dve.wait_ge(*s["kept"](n))
                            dve.tensor_tensor(at(cell), at(cell), at(fed), ALU.add).then_inc(s["cell"].sem)

        with nc.Fori(0, B) as b:
            set_round(b, s2)
            with nc.Block() as block:

                @block.tensor
                def _(pe):
                    for m in range(FT):
                        for j in range(NCH):
                            for k in range(FT):
                                pe.matmul(c.bank(2 * m + j), c.w("f_wo", k, m * P, P), xn_all[:, k, bass.ds(b * S + j * CH, CH)],
                                          start=(k == 0), stop=False)
                            for k in range(FT):
                                mm = pe.matmul(c.bank(2 * m + j), c.w("f_uo", k, m * P, P), cell[:, k, j * CH:(j + 1) * CH],
                                               start=False, stop=(k == 1))
                            mm.then_inc(s2["o_done"].sem)

                @block.scalar
                def _(act):
                    for n in range(FT * NCH):
                        act.wait_ge(*s2["o_done"](n + 1))
                        m, j = divmod(n, NCH)
                        act.activation(fed[:, m, j * CH:(j + 1) * CH], c.bank(n), ACT.Tanh, bias=c.v("f_bo", m)).then_inc(s2["tanh"].sem)

                @block.vector
                def _(dve):
                    for n in range(FT * NCH):
                        dve.wait_ge(*s2["tanh"](n + 1))
                        m, j = divmod(n, NCH)
                        xs = c.xT[:, m, bass.ds(b * S + j * CH, CH)]
                        dve.tensor_tensor(xs, xs, fed[:, m, j * CH:(j + 1) * CH], ALU.add).then_inc(s2["x_done"].sem)
        clear_signals(nc, ln, s, s2, also=[first])


class Unit:

    def __init__(self, heads, qi):
        self.heads, self.qi, self.keys = heads, qi, (qi + 1) * P
        self.pitch = CH if len(heads) == 2 else self.keys
        self.blocks = [(i, kb) for i in range(len(heads)) for kb in range(qi + 1)]

    def spread(self, ap):
        return ap[:, 0:self.pitch * len(self.heads)].rearrange("p (h n) -> p h n", n=self.pitch)[:, :, 0:self.keys]


def causal_attention_layer(nc, c):
    H, DH = 16, 16
    SCALE = DH ** -0.5
    QPART = (0, 0, 0, 1, 1, 1, 2, 2)
    KPART = (0, 1, 2, 0, 1, 2, 0, 1)
    QUAD = 4
    QUADS = H // QUAD
    WIDE = QUAD * DH
    LOADS = 16
    units, last_of_quad = [], []
    for first in range(0, H, QUAD):
        heads = list(range(first, first + QUAD))
        units += [Unit(heads, 0), Unit(heads, 1)]
        units += [Unit(heads[i:i + 2], qi) for qi in (2, 3) for i in (0, 2)]
        units += [Unit([h], qi) for h in heads for qi in range(4, TT)]
        last_of_quad.append(len(units))
    U = len(units)
    more = [u for u in range(U) if len(units[u].blocks) > 4]
    nth2 = {u: n for n, u in enumerate(more)}
    with ExitStack() as ctx:
        norm_s = signals(nc, ctx, "bn", norm_signals())
        pr = signals(nc, ctx, "bp", dict(q_proj=4, k_proj=4, v_proj=4, q_raw=4, k_raw=4, v_copied=4, part=4, rest=2, last_part=2,
                                         stored=6 * 16))
        s = signals(nc, ctx, "b", dict(
            loaded0=LOADS * 16 * QUADS // 2, loaded1=LOADS * 16 * QUADS // 2,
            scores=U, row_max=U, shift=U, expd=U, turned1=U + TT // 2, copied1=U + TT // 2,
            turned2=len(more) + TT // 2, copied2=len(more) + TT // 2,
            av=U, den_inv=U, normed=U, o_done=4, x_done=4))
        loaded = [s["loaded0"], s["loaded1"]]
        made = ctx.enter_context(nc.semaphore("b_made"))
        sb = lambda name, shape, dt=F32: ctx.enter_context(nc.sbuf_tensor(name, shape, dt))
        ident16 = sb("b_ident16", [P, P], BF16)
        future = sb("b_future", [P, P], BF16)
        q_parts = sb("b_q_parts", [P, 3, FT, S], BF16)
        k_parts = sb("b_k_parts", [P, 3, FT, S], BF16)
        q_stack = sb("b_q_stack", [P, 2, QUAD, S], BF16)
        k_stack = sb("b_k_stack", [P, 2, QUAD, S], BF16)
        rs = sb("b_rs", [P, 4, QUAD])
        mx = sb("b_mx", [P, 4, QUAD])
        nm = sb("b_nm", [P, 4, QUAD])
        q_dram = nc.dram_tensor("b_q_dram", (B, 3, D, S), BF16, kind="Internal").ap()
        k_dram = nc.dram_tensor("b_k_dram", (B, 3, D, S), BF16, kind="Internal").ap()
        xn_all = c.spent_weights()
        ot, o = c.slot(0), c.slot(1)
        v_all = c.arena[:, 4 * FT * S:]
        o_t = o.rearrange("p a n -> p (a n)").rearrange("p (t n) -> p t n", t=TT)
        half = lambda i: c.arena[:, 2 * 2048 + i * S:2 * 2048 + (i + 1) * S]
        probs = [half(0), half(1)]
        turned = [half(i).rearrange("p (k n) -> p k n", k=TT) for i in (2, 3)]
        stack_at = lambda h: ((h // QUAD) % 2, h % QUAD)
        with nc.Block() as block:

            @block.gpsimd
            def _(pool):
                pool.tensor_copy(ident16[:], c.ident[:])
                pool.memset(future[:], 0.0).then_inc(made)
                pool.wait_ge(made, 1)
                pool.affine_select(out=future[:], in_=future[:], compare_op=ALU.is_ge, fill=NEG, base=0,
                                   pattern=[[-1, P]], channel_multiplier=1)

        norm_both(nc, c, norm_s, xn_all)

        v_tiles = v_all.rearrange("p (t n) -> p t n", t=B * TT)
        spare = lambda t: t[:].rearrange("p a r n -> p (a r n)")[:, 0:3 * FT * S]\
            .rearrange("p (a m n) -> p a m n", a=3, m=FT)
        parts_of = ((q_parts[:], k_parts[:]), (spare(q_stack), spare(k_stack)))
        raw_of = ((c.slot(0), c.slot(1)), (c.slot(2), c.slot(3)))
        with nc.Block() as block:

            @block.sync
            def _(sync):
                for b in range(B):
                    set_round(b, pr)
                    for i in range(3):
                        for n, dram in enumerate((q_dram, k_dram)):
                            sync.wait_ge(*(pr["part"](2 * i + n + 1) if i < 2 else pr["last_part"](n + 1)))
                            sync.dma_start(dram[b, i].rearrange("(m p) n -> p m n", p=P), parts_of[b][n][:, i, :, :])\
                                .then_inc(pr["stored"].sem, 16)
                sync.wait_ge(pr["stored"].sem, B * 6 * 16)

            @block.tensor
            def _(pe):
                for b in range(B):
                    set_round(b, pr)
                    xn = lambda k, first, n: xn_all[:, k, b * S + first:b * S + first + n]
                    for name, base, done in (("b_wq", 0, pr["q_proj"]), ("b_wk", 4, pr["k_proj"])):
                        for n in range(4):
                            m, j = divmod(n, NCH)
                            if b:
                                pe.wait_ge(*pr["k_raw" if base else "v_copied"](n + 1 - 4))
                            for k in range(FT):
                                mm = pe.matmul(c.bank(base + n), c.w(name, k, m * P, P), xn(k, j * CH, CH),
                                               start=(k == 0), stop=(k == 1))
                            mm.then_inc(done.sem)
                    for t2 in range(4):
                        pe.wait_ge(*pr["q_raw"](t2 + 1))
                        for t in (0, 1):
                            for k in range(FT):
                                mm = pe.matmul(c.bank(t2)[:, t * D:(t + 1) * D], xn(k, (2 * t2 + t) * P, P),
                                               c.w("b_wv", k, 0, D), start=(k == 0), stop=(k == 1))
                        mm.then_inc(pr["v_proj"].sem)

            @block.scalar
            def _(act):
                for b in range(B):
                    set_round(b, pr)
                    for t, bias, ready, done, base in ((raw_of[b][0], "b_bq", pr["q_proj"], pr["q_raw"], 0),
                                                       (raw_of[b][1], "b_bk", pr["k_proj"], pr["k_raw"], 4)):
                        for n in range(4):
                            m, j = divmod(n, NCH)
                            act.wait_ge(*ready(n + 1))
                            act.activation(t[:, m, j * CH:(j + 1) * CH], c.bank(base + n), ACT.Identity, bias=c.v(bias, m))\
                               .then_inc(done.sem)
                    for i in range(2):
                        for n in range(2):
                            if i == 0:
                                act.wait_ge(*pr["k_raw" if n else "q_raw"](4))
                            else:
                                act.wait_ge(*pr["rest"](n + 1))
                            act.activation(parts_of[b][n][:, i, :, :], raw_of[b][n], ACT.Copy).then_inc(pr["part"].sem)

            @block.vector
            def _(dve):
                def values(b):
                    for t2 in range(4):
                        dve.wait_ge(*pr["v_proj"](t2 + 1))
                        dve.tensor_copy(v_tiles[:, b * TT + 2 * t2:b * TT + 2 * t2 + 2, :].rearrange("p t n -> p (t n)"),
                                        c.bank(t2)).then_inc(pr["v_copied"].sem)

                def parts(b):
                    for i in range(2):
                        for n in range(2):
                            dve.wait_ge(*pr["part"](2 * i + n + 1))
                            if i == 0:
                                dve.tensor_tensor(raw_of[b][n], raw_of[b][n], parts_of[b][n][:, i, :, :], ALU.subtract)\
                                   .then_inc(pr["rest"].sem)
                            else:
                                dve.tensor_tensor(parts_of[b][n][:, 2, :, :], raw_of[b][n], parts_of[b][n][:, i, :, :],
                                                  ALU.subtract).then_inc(pr["last_part"].sem)

                for b in range(B):
                    set_round(b, pr)
                    for step in (values, parts) if b < B - 1 else (parts, values):
                        step(b)

        with nc.Fori(0, B) as b:
            set_round(b, s)
            x = lambda k, j: c.xT[:, k, bass.ds(b * S + j * CH, CH)]
            turn_bank = lambda i: c.bank(5 + i)
            score = lambda u: c.psum[u % 2]
            out_bank = lambda u: c.bank(4 if u % 2 else 7)
            with nc.Block() as block:

                @block.sync
                def _(sync):
                    q_now, k_now = (t[bass.ds(b, 1)].rearrange("b a f n -> (b a) f n") for t in (q_dram, k_dram))
                    for quad in range(QUADS):
                        if quad >= 2:
                            sync.wait_ge(*s["scores"](last_of_quad[quad - 2]))
                        at = quad % 2
                        by_head = lambda ap: ap.rearrange("a (h d) n -> a d h n", d=DH)
                        rows = slice(quad * QUAD * DH, (quad + 1) * QUAD * DH)
                        for i in range(3):
                            first, n = QPART.index(i) * DH, QPART.count(i)
                            for r in range(n):
                                sync.dma_start(q_stack[first + r * DH:first + (r + 1) * DH, at, :, :],
                                               by_head(q_now[i:i + 1, rows, :])[0]).then_inc(loaded[at].sem, 16)
                        for r, i in enumerate(KPART):
                            sync.dma_start(k_stack[r * DH:(r + 1) * DH, at, :, :],
                                           by_head(k_now[i:i + 1, rows, :])[0]).then_inc(loaded[at].sem, 16)

                @block.tensor
                def _(pe):
                    def scores(u):
                        unit = units[u]
                        if u == 0 or u in last_of_quad:
                            quad = unit.heads[0] // QUAD
                            pe.wait_ge(*loaded[quad % 2](LOADS * 16 * (quad // 2 + 1)))
                        if u >= 2:
                            pe.wait_ge(*s["expd"](u - 1))
                        for i, h in enumerate(unit.heads):
                            a, r = stack_at(h)
                            for first in range(0, unit.keys, CH):
                                n = min(CH, unit.keys - first)
                                last = first + n == unit.keys
                                at = i * unit.pitch + first
                                pe.matmul(score(u)[:, at:at + n], q_stack[:, a, r, unit.qi * P:(unit.qi + 1) * P],
                                          k_stack[:, a, r, first:first + n], start=True, stop=not last)
                            at = i * unit.pitch + unit.qi * P
                            mm = pe.matmul(score(u)[:, at:at + P], ident16[:], future[:], start=False, stop=True)
                        mm.then_inc(s["scores"].sem)

                    def turn(u):
                        unit = units[u]
                        pe.wait_ge(*s["expd"](u + 1))
                        for n, (i, kb) in enumerate(unit.blocks):
                            tile = n // 4
                            if n == 0 and u >= 1:
                                pe.wait_ge(*s["copied1"](u))
                            if n == 4 and nth2[u] >= 1:
                                pe.wait_ge(*s["copied2"](nth2[u]))
                            mm = pe.transpose(turn_bank(tile)[:, (n % 4) * P:(n % 4 + 1) * P],
                                              probs[u % 2][:, i * unit.pitch + kb * P:i * unit.pitch + (kb + 1) * P], c.ident[:])
                            if n == 3:
                                mm.then_inc(s["turned1"].sem)
                        if u in nth2:
                            mm.then_inc(s["turned2"].sem)

                    def values(u):
                        unit = units[u]
                        pe.wait_ge(*s["copied1"](u + 1))
                        if u in nth2:
                            pe.wait_ge(*s["copied2"](nth2[u] + 1))
                        if u >= 2:
                            pe.wait_ge(*s["normed"](u - 1))
                        for n, (i, kb) in enumerate(unit.blocks):
                            h = unit.heads[i]
                            first = h // QUAD * WIDE
                            mm = pe.matmul(out_bank(u)[:, i * WIDE:(i + 1) * WIDE], turned[u % 2][:, n, :],
                                           v_all[:, bass.ds(b * (TT * D) + kb * D + first, WIDE)], start=(kb == 0), stop=(kb == unit.qi))
                        mm.then_inc(s["av"].sem)

                    scores(0)
                    scores(1)
                    for u in range(U + 1):
                        if u < U:
                            turn(u)
                        if u + 2 < U:
                            scores(u + 2)
                        if u >= 1:
                            values(u - 1)
                    pe.wait_ge(*s["normed"](U))
                    for qi in range(TT):
                        i, n = qi % 2, qi // 2
                        pe.wait_ge(*(s["copied2"](len(more) + n) if i else s["copied1"](U + n)))
                        for m in range(FT):
                            mm = pe.transpose(turn_bank(i)[:, m * P:(m + 1) * P], o_t[:, qi, m * P:(m + 1) * P], c.ident[:])
                        mm.then_inc((s["turned2"] if i else s["turned1"]).sem)
                    pe.wait_ge(*s["copied1"](U + TT // 2))
                    pe.wait_ge(*s["copied2"](len(more) + TT // 2))
                    for m in range(FT):
                        for j in range(NCH):
                            for k in range(FT):
                                mm = pe.matmul(c.bank(2 * m + j), c.w("b_wo", k, m * P, P), ot[:, k, j * CH:(j + 1) * CH],
                                               start=(k == 0), stop=(k == 1))
                            mm.then_inc(s["o_done"].sem)

                @block.scalar
                def _(act):
                    def exps(u):
                        unit = units[u]
                        act.wait_ge(*s["shift"](u + 1))
                        if u >= 2:
                            act.wait_ge(*(s["turned2"](nth2[u - 2] + 1) if u - 2 in nth2 else s["turned1"](u - 1)))
                        if u >= 4:
                            act.wait_ge(*s["normed"](u - 3))
                        for i in range(len(unit.heads)):
                            at = slice(i * unit.pitch, i * unit.pitch + unit.keys)
                            ins = act.activation(probs[u % 2][:, at], score(u)[:, at], ACT.Exp, bias=nm[:, u % 4, i:i + 1],
                                                 scale=SCALE, accum_out=rs[:, u % 4, i:i + 1])
                        ins.then_inc(s["expd"].sem)

                    exps(0)
                    exps(1)
                    for u in range(U):
                        if u in nth2:
                            act.wait_ge(*s["turned2"](nth2[u] + 1))
                            if u >= 2:
                                act.wait_ge(*s["av"](u - 1))
                            n = len(units[u].blocks)
                            act.activation(turned[u % 2][:, 4:n, :].rearrange("p k n -> p (k n)"), turn_bank(1)[:, 0:(n - 4) * P],
                                           ACT.Copy).then_inc(s["copied2"].sem)
                        if u + 2 < U:
                            exps(u + 2)
                    for n in range(TT // 2):
                        act.wait_ge(*s["turned2"](len(more) + n + 1))
                        for m in range(FT):
                            ins = act.activation(ot[:, m, (2 * n + 1) * P:(2 * n + 2) * P], turn_bank(1)[:, m * P:(m + 1) * P],
                                                 ACT.Identity, bias=c.v("b_bv", m))
                        ins.then_inc(s["copied2"].sem)

                @block.vector
                def _(dve):
                    def shift(u):
                        unit = units[u]
                        nh = len(unit.heads)
                        dve.wait_ge(*s["scores"](u + 1))
                        if u >= 4:
                            dve.wait_ge(*s["expd"](u - 3))
                        dve.tensor_reduce(mx[:, u % 4, 0:nh], unit.spread(score(u)), AX, ALU.max).then_inc(s["row_max"].sem)
                        dve.wait_ge(*s["row_max"](u + 1))
                        dve.tensor_scalar(nm[:, u % 4, 0:nh], mx[:, u % 4, 0:nh], -SCALE, None, ALU.mult).then_inc(s["shift"].sem)

                    def copy_turned(u):
                        dve.wait_ge(*s["turned1"](u + 1))
                        if u >= 2:
                            dve.wait_ge(*s["av"](u - 1))
                        dve.tensor_copy(turned[u % 2][:, 0:4, :].rearrange("p k n -> p (k n)"), turn_bank(0)).then_inc(s["copied1"].sem)

                    def norm(u):
                        unit = units[u]
                        nh, h0 = len(unit.heads), unit.heads[0]
                        dve.wait_ge(*s["expd"](u + 1))
                        dve.reciprocal(rs[:, u % 4, 0:nh], rs[:, u % 4, 0:nh]).then_inc(s["den_inv"].sem)
                        dve.wait_ge(*s["den_inv"](u + 1))
                        dve.wait_ge(*s["av"](u + 1))
                        first, step = h0 % QUAD * DH, WIDE + DH
                        own = out_bank(u)[:, first:first + nh * step].rearrange("p (h d) -> p h d", h=nh)[:, :, 0:DH]
                        dve.tensor_tensor(o_t[:, unit.qi, h0 * DH:(h0 + nh) * DH].rearrange("p (h d) -> p h d", h=nh), own,
                                          rs[:, u % 4, 0:nh].unsqueeze(2).to_broadcast([P, nh, DH]), ALU.mult).then_inc(s["normed"].sem)

                    shift(0)
                    shift(1)
                    for u in range(U + 2):
                        if u < U:
                            copy_turned(u)
                        if u + 2 < U:
                            shift(u + 2)
                        if u >= 2:
                            norm(u - 2)
                    for n in range(TT // 2):
                        dve.wait_ge(*s["turned1"](U + n + 1))
                        for m in range(FT):
                            ins = dve.tensor_scalar(ot[:, m, 2 * n * P:(2 * n + 1) * P], turn_bank(0)[:, m * P:(m + 1) * P],
                                                    c.v("b_bv", m), None, ALU.add)
                        ins.then_inc(s["copied1"].sem)
                    for m in range(FT):
                        for j in range(NCH):
                            dve.wait_ge(*s["o_done"](2 * m + j + 1))
                            dve.scalar_tensor_tensor(out=x(m, j), in0=c.bank(2 * m + j), scalar=c.v("b_bo", m),
                                                     in1=x(m, j), op0=ALU.add, op1=ALU.add).then_inc(s["x_done"].sem)
        clear_signals(nc, norm_s, pr, s, also=[made])


def context_attention_layer(nc, c):
    H, DH = 16, 16
    SCALE = DH ** -0.5
    HT8 = H // FT
    PAIRS = H // 2
    KC = [P, CF - P]
    with ExitStack() as ctx:
        norm_s = signals(nc, ctx, "yn", norm_signals())
        s = signals(nc, ctx, "y", dict(
            q_proj=4, q_raw=4, scores=TT, row_max=TT, shifted=TT, expd=TT, den_inv=TT,
            turned1=TT + TT // 2, copied1=TT + TT // 2, turned2=TT + TT // 2, copied2=TT + TT // 2,
            av=TT, normed=TT, o_done=4, x_done=4))
        g = signals(nc, ctx, "yc", dict(load=1, zeroed=3, made=3, k=1, v=1, kb=1, out=1))
        set_round(0, g)
        sb = lambda name, shape, dt=F32: ctx.enter_context(nc.sbuf_tensor(name, shape, dt))
        of_head = sb("y_of_head", [P, HT8])
        cx = sb("y_cx", [P, 2, B * KEYS])
        kc = sb("y_kc", [P, FT, B * KEYS])
        k_diag = sb("y_k_diag", [P, B, FT, CH])
        WIDE = 64
        v_diag = sb("y_v_diag", [P, B, PAIRS, WIDE])
        mx = sb("y_mx", [P, 2, H])
        rs = sb("y_rs", [P, 2, H])
        xn_all, q, ot, o = c.spent_weights(), c.slot(1), c.slot(4), c.slot(5)
        o_t = o.rearrange("p a n -> p (a n)").rearrange("p (t n) -> p t n", t=TT)
        quarter = lambda first, i: c.arena[:, first * 2048 + i * S:first * 2048 + (i + 1) * S]
        probs = [quarter(2, 0), quarter(2, 1)]
        turned = [quarter(3, i).rearrange("p (k n) -> p k n", k=PAIRS) for i in range(2)]
        with nc.Block() as block:

            @block.sync
            def _(sync):
                sync.dma_start(cx[:], c.ctx_t).then_inc(g["load"].sem, 16)

            @block.gpsimd
            def _(pool):
                pool.memset(v_diag[:], 0.0).then_inc(g["zeroed"].sem)
                pool.wait_ge(*g["zeroed"](1))
                for i in (0, 1):
                    pool.memset(v_diag[i * KEYS:(i + 1) * KEYS, :, :, 2 * DH + i:2 * DH + i + 1], 1.0)\
                        .then_inc(g["zeroed"].sem)
                    pool.wait_ge(*g["zeroed"](i + 2))
                pool.memset(of_head[:], 1.0).then_inc(g["made"].sem)
                pool.wait_ge(*g["made"](1))
                pool.affine_select(out=of_head[:], in_=of_head[:], compare_op=ALU.is_ge, fill=0.0, base=0,
                                   pattern=[[-DH, HT8]], channel_multiplier=1).then_inc(g["made"].sem)
                pool.wait_ge(*g["made"](2))
                pool.affine_select(out=of_head[:], in_=of_head[:], compare_op=ALU.is_ge, fill=0.0, base=DH - 1,
                                   pattern=[[DH, HT8]], channel_multiplier=-1).then_inc(g["made"].sem)

            @block.tensor
            def _(pe):
                pe.wait_ge(g["load"].sem, 16)
                for m in range(FT):
                    for k in range(2):
                        mm = pe.matmul(c.bank(0)[:, m * P:(m + 1) * P], c.w("y_wk", k, m * P, P, KC[k]), cx[0:KC[k], k, :],
                                       start=(k == 0), stop=(k == 1))
                mm.then_inc(g["k"].sem)
                for b in range(B):
                    for k in range(2):
                        mm = pe.matmul(c.bank(1)[0:KEYS, b * D:(b + 1) * D], cx[0:KC[k], k, b * KEYS:(b + 1) * KEYS],
                                       c.w("y_wv", k, 0, D, KC[k]), start=(k == 0), stop=(k == 1))
                mm.then_inc(g["v"].sem)

            @block.vector
            def _(dve):
                dve.wait_ge(*g["k"](1))
                for m in range(FT):
                    ins = dve.tensor_scalar(kc[:, m, :], c.bank(0)[:, m * P:(m + 1) * P], c.v("y_bk", m), None, ALU.add)
                ins.then_inc(g["kb"].sem)
                dve.wait_ge(*g["kb"](1))
                dve.wait_ge(*g["made"](3))
                dve.wait_ge(*g["zeroed"](3))
                for b in range(B):
                    for m in range(FT):
                        dve.tensor_tensor(k_diag[:, b, m, :].rearrange("p (h n) -> p h n", h=HT8),
                                          kc[:, m, b * KEYS:(b + 1) * KEYS].unsqueeze(1).to_broadcast([P, HT8, KEYS]),
                                          of_head[:].unsqueeze(2).to_broadcast([P, HT8, KEYS]), ALU.mult)
                dve.wait_ge(*g["v"](1))
                for b in range(B):
                    pairs = c.bank(1)[0:KEYS, b * D:(b + 1) * D].rearrange("p (r d) -> p r d", r=PAIRS)
                    for i in (0, 1):
                        dve.tensor_copy(v_diag[i * KEYS:(i + 1) * KEYS, b, :, i * DH:(i + 1) * DH], pairs[:, :, i * DH:(i + 1) * DH])

        norm_both(nc, c, norm_s, xn_all)
        with nc.Fori(0, B) as b:
            set_round(b, s)
            x = lambda k, j: c.xT[:, k, bass.ds(b * S + j * CH, CH)]
            kd = k_diag[:].rearrange("p b m n -> p (b m n)")
            vd = v_diag[:].rearrange("p b r d -> p (b r d)")
            score = lambda u: c.psum[u % 2]
            turn_bank = lambda i: c.bank(5 + i)
            turned_of, copied_of = (s["turned1"], s["turned2"]), (s["copied1"], s["copied2"])
            out_bank = lambda u: c.bank(4 if u % 2 else 7)
            with nc.Block() as block:

                @block.tensor
                def _(pe):
                    for m in range(FT):
                        for j in range(NCH):
                            for k in range(FT):
                                mm = pe.matmul(c.bank(4 + 2 * m + j), c.w("y_wq", k, m * P, P),
                                               xn_all[:, k, bass.ds(b * S + j * CH, CH)], start=(k == 0), stop=(k == 1))
                            mm.then_inc(s["q_proj"].sem)

                    def scores(u):
                        if u == 0:
                            pe.wait_ge(*s["q_raw"](4))
                        if u >= 2:
                            pe.wait_ge(*s["shifted"](u - 1))
                        for m in range(FT):
                            mm = pe.matmul(score(u)[:, m * CH:(m + 1) * CH], q[:, m, u * P:(u + 1) * P],
                                           kd[:, bass.ds(b * (FT * CH) + m * CH, CH)], start=True, stop=True)
                        mm.then_inc(s["scores"].sem)

                    def turn(u):
                        pe.wait_ge(*s["expd"](u + 1))
                        for i in (0, 1):
                            if u >= 1:
                                pe.wait_ge(*copied_of[i](u))
                            for r in range(4):
                                mm = pe.transpose(turn_bank(i)[:, r * P:(r + 1) * P],
                                                  probs[u % 2][:, (4 * i + r) * P:(4 * i + r + 1) * P], c.ident[:])
                            mm.then_inc(turned_of[i].sem)

                    def values(u):
                        for i in (0, 1):
                            pe.wait_ge(*copied_of[i](u + 1))
                        if u >= 2:
                            pe.wait_ge(*s["normed"](u - 1))
                        for r in range(PAIRS):
                            mm = pe.matmul(out_bank(u)[:, r * WIDE:(r + 1) * WIDE], turned[u % 2][:, r, :],
                                           vd[:, bass.ds((b * PAIRS + r) * WIDE, WIDE)], start=True, stop=True)
                        mm.then_inc(s["av"].sem)

                    scores(0)
                    scores(1)
                    for u in range(TT + 1):
                        if u + 2 < TT:
                            scores(u + 2)
                        if u < TT:
                            turn(u)
                        if u >= 1:
                            values(u - 1)
                    for u in range(TT):
                        i, n = u % 2, u // 2
                        pe.wait_ge(*s["normed"](u + 1))
                        pe.wait_ge(*copied_of[i](TT + n))
                        for m in range(FT):
                            mm = pe.transpose(turn_bank(i)[:, m * P:(m + 1) * P], o_t[:, u, m * P:(m + 1) * P], c.ident[:])
                        mm.then_inc(turned_of[i].sem)
                    for i in (0, 1):
                        pe.wait_ge(*copied_of[i](TT + TT // 2))
                    for m in range(FT):
                        for j in range(NCH):
                            for k in range(FT):
                                mm = pe.matmul(c.bank(2 * m + j), c.w("y_wo", k, m * P, P), ot[:, k, j * CH:(j + 1) * CH],
                                               start=(k == 0), stop=(k == 1))
                            mm.then_inc(s["o_done"].sem)

                @block.scalar
                def _(act):
                    for n in range(4):
                        m, j = divmod(n, NCH)
                        act.wait_ge(*s["q_proj"](n + 1))
                        act.activation(q[:, m, j * CH:(j + 1) * CH], c.bank(4 + n), ACT.Identity, bias=c.v("y_bq", m)).then_inc(s["q_raw"].sem)

                    def exps(u):
                        act.wait_ge(*s["shifted"](u + 1))
                        act.activation(probs[u % 2], probs[u % 2], ACT.Exp, scale=SCALE).then_inc(s["expd"].sem)

                    exps(0)
                    exps(1)
                    for u in range(TT):
                        act.wait_ge(*s["turned2"](u + 1))
                        if u >= 2:
                            act.wait_ge(*s["av"](u - 1))
                        act.activation(turned[u % 2][:, 4:8, :].rearrange("p k n -> p (k n)"), turn_bank(1), ACT.Copy)\
                           .then_inc(s["copied2"].sem)
                        if u + 2 < TT:
                            exps(u + 2)
                    for n in range(TT // 2):
                        act.wait_ge(*s["turned2"](TT + n + 1))
                        for m in range(FT):
                            ins = act.activation(ot[:, m, (2 * n + 1) * P:(2 * n + 2) * P], turn_bank(1)[:, m * P:(m + 1) * P],
                                                 ACT.Identity, bias=c.v("y_bv", m))
                        ins.then_inc(s["copied2"].sem)

                @block.vector
                def _(dve):
                    heads = lambda ap: ap.rearrange("p (h n) -> p h n", h=H)
                    wide = lambda ap, n: ap.unsqueeze(2).to_broadcast([P, H, n])

                    def shift(u):
                        dve.wait_ge(*s["scores"](u + 1))
                        dve.tensor_reduce(mx[:, u % 2, :], heads(score(u)[:]), AX, ALU.max).then_inc(s["row_max"].sem)
                        dve.wait_ge(*s["row_max"](u + 1))
                        if u >= 2:
                            dve.wait_ge(*s["turned2"](u - 1))
                        dve.tensor_tensor(heads(probs[u % 2]), heads(score(u)[:]), wide(mx[:, u % 2, :], KEYS), ALU.subtract)\
                           .then_inc(s["shifted"].sem)

                    def copy_turned(u):
                        dve.wait_ge(*s["turned1"](u + 1))
                        if u >= 2:
                            dve.wait_ge(*s["av"](u - 1))
                        dve.tensor_copy(turned[u % 2][:, 0:4, :].rearrange("p k n -> p (k n)"), turn_bank(0))\
                           .then_inc(s["copied1"].sem)

                    def norm(u):
                        out = out_bank(u).rearrange("p (r n) -> p r n", r=PAIRS)
                        by_pair = lambda ap, n: ap.rearrange("p (r i n) -> p r i n", r=PAIRS, i=2, n=n)
                        dve.wait_ge(*s["av"](u + 1))
                        if u >= 2:
                            dve.wait_ge(*s["normed"](u - 1))
                        dve.reciprocal(rs[:, u % 2, :].rearrange("p (r i) -> p r i", i=2), out[:, :, 2 * DH:2 * DH + 2])\
                           .then_inc(s["den_inv"].sem)
                        dve.wait_ge(*s["den_inv"](u + 1))
                        dve.tensor_tensor(by_pair(o_t[:, u, :], DH), out[:, :, 0:2 * DH].rearrange("p r (i n) -> p r i n", i=2),
                                          by_pair(rs[:, u % 2, :], 1).to_broadcast([P, PAIRS, 2, DH]), ALU.mult)\
                           .then_inc(s["normed"].sem)

                    shift(0)
                    shift(1)
                    for u in range(TT + 2):
                        if u < TT:
                            copy_turned(u)
                        if u >= 2:
                            norm(u - 2)
                        if u + 2 < TT:
                            shift(u + 2)
                    for n in range(TT // 2):
                        dve.wait_ge(*s["turned1"](TT + n + 1))
                        for m in range(FT):
                            ins = dve.tensor_scalar(ot[:, m, 2 * n * P:(2 * n + 1) * P], turn_bank(0)[:, m * P:(m + 1) * P],
                                                    c.v("y_bv", m), None, ALU.add)
                        ins.then_inc(s["copied1"].sem)
                    for m in range(FT):
                        for j in range(NCH):
                            dve.wait_ge(*s["o_done"](2 * m + j + 1))
                            dve.scalar_tensor_tensor(out=x(m, j), in0=c.bank(2 * m + j), scalar=c.v("y_bo", m),
                                                     in1=x(m, j), op0=ALU.add, op1=ALU.add).then_inc(s["x_done"].sem)
        clear_signals(nc, norm_s, s, g)


def expert_layer(nc, c):
    TIL = T // P
    GP = GR // 2
    NP_ = TIL * EXP
    RN = FT + GP + 2 + FT * GP
    PIECES = 2 * FT
    NEXT = EXP + 2
    with ExitStack() as ctx:
        sb = lambda name, shape, dt=F32: ctx.enter_context(nc.sbuf_tensor(name, shape, dt))
        norm_s = signals(nc, ctx, "mn", norm_signals())
        s = signals(nc, ctx, "m", dict(turned=TIL // 2, copied=TIL // 2, logits=1, logits_read=1))
        set_round(0, s)
        r = signals(nc, ctx, "r", dict(made=4, step=40, prep=5, w_high=PIECES, w_rest=PIECES, cum1=1, cnt=2, cum2=1))
        set_round(0, r)
        e = signals(nc, ctx, "e", dict(
            made=2 * RN, read=2 * RN, w0_done=2 * HT, w1_done=2 * HT, gelu=2 * HT, hidden=2 * HT, prep=10, prepared=2,
            x_high=2 * FT, w_high=2 * PIECES, w_rest=2 * PIECES))
        w_sig = ctx.enter_context(nc.semaphore("e_weights"))
        wo_sig = [ctx.enter_context(nc.semaphore(f"e_wo{i}")) for i in range(2)]
        stored = ctx.enter_context(nc.semaphore("stored"))
        router_sig = ctx.enter_context(nc.semaphore("m_router_loaded"))
        xn_tok = c.arena[:, 4 * FT * S:].rearrange("p (t n) -> p t n", t=TIL)
        logits = sb("m_logits", [P, TIL, EXP])
        tab = {n: sb(f"m_{n}", [P, TIL, EXP]) for n in ("raw", "rest", "m1", "m2", "p1", "p2", "t")}
        order8 = sb("m_order", [P, EXP])
        col16 = {n: sb(f"m_{n}", [P, TIL]) for n in ("mx", "sm", "g1", "g2", "pick")}
        pos = [sb(f"m_pos{i}", [P, NEXT * TIL]) for i in (1, 2)]
        before = sb("m_before", [P, P])
        ones = sb("m_ones", [P, P])
        iota_i = sb("m_iota_i", [P, CAP], mybir.dt.int32)
        iota = sb("m_iota", [P, CAP])
        disp = sb("m_disp", [P, TIL, CAP])
        comb = sb("m_comb", [P, TIL, P])
        one = sb("m_one", [P, TIL, CAP])
        two = sb("m_two", [P, TIL, CAP])
        back = sb("m_back", [P, TIL, P])
        x_high = sb("m_x_high", [P, FT, CH], F32R)
        x_rest = sb("m_x_rest", [P, FT, CH], F32R)
        gelu = c.arena[:, (HT + 2) * CH:(HT + 4) * CH].rearrange("p (i n) -> p i n", i=2)
        hidden = c.arena[:, 0:HT * CH].rearrange("p (h n) -> p h n", h=HT)
        e_out = c.arena[:, HT * CH:(HT + 2) * CH].rearrange("p (g n) -> p g n", g=GP)
        xn = c.two_slots(0)
        router = sb("m_router", [P, FT, EXP])
        w_raw = [sb(f"m_w{i}", [P, FT, HID]) for i in range(2)]
        wo = [sb(f"m_wo{i}", [P, HT, D]) for i in range(2)]
        FULL = (HT - 1) * P

        pick = lambda m, ex: m[bass.ds(ex, 1)].rearrange("e a b c -> (e a) b c" if len(m.shape) == 4 else "e a b -> (e a) b")

        def load_first(sync, ex):
            for to, of in zip(w_raw, (c.w0, c.w1)):
                sync.dma_start(to[:], pick(of, ex)).then_inc(w_sig, 16)

        def load_last(sync, i, ex):
            rows = pick(c.wo, ex)
            sync.dma_start(wo[i][:, 0:HT - 1, :], rows[0:FULL, :].rearrange("(h p) n -> p h n", p=P)).then_inc(wo_sig[i], 16)
            sync.dma_start(wo[i][0:HLAST, HT - 1, :], rows[FULL:HID, :]).then_inc(wo_sig[i], 16)

        W_LOAD = 2 * 16
        with nc.Block() as block:

            @block.sync
            def _(sync):
                at = c.mats["router"][0]
                sync.dma_start(router[:].rearrange("p k e -> p (k e)"), c.weights_dram[:, at:at + FT * EXP]).then_inc(router_sig, 16)
                load_first(sync, 0)
                for i in range(2):
                    load_last(sync, i, i)

            @block.gpsimd
            def _(pool):
                pool.memset(comb[:], 0.0)
                for i in range(2):
                    pool.memset(pos[i][:], -1.0)
                pool.iota(iota_i[:], pattern=[[1, CAP]], base=0, channel_multiplier=0).then_inc(r["made"].sem)
                pool.memset(ones[:], 1.0).then_inc(r["made"].sem)
                pool.wait_ge(*r["made"](2))
                pool.affine_select(out=before[:], in_=ones[:], compare_op=ALU.is_gt, fill=0.0, base=0,
                                   pattern=[[1, P]], channel_multiplier=-1)
                for i in range(EXP):
                    pool.memset(order8[:, i:i + 1], float(EXP - i))
                pool.tensor_copy(iota[:], iota_i[:]).then_inc(r["made"].sem)

        with ExitStack() as norm_ctx:
            c.ln = norm_ctx.enter_context(nc.sbuf_tensor("m_ln", [P, B * NCH, CH], F32))
            norm_both(nc, c, norm_s, xn)
        w_high = [sb(f"m_w{i}_high", [P, FT, HID], F32R) for i in range(2)]
        w_rest = [sb(f"m_w{i}_rest", [P, FT, HID], F32R) for i in range(2)]

        def split_high(act, sig):
            for n in range(PIECES):
                act.activation(w_high[n // FT][:, n % FT, :], w_raw[n // FT][:, n % FT, :], ACT.Copy).then_inc(sig.sem)

        def split_rest(engine, ready, sig):
            for n in range(PIECES):
                engine.wait_ge(*ready(n + 1))
                engine.tensor_tensor(w_rest[n // FT][:, n % FT, :], w_raw[n // FT][:, n % FT, :],
                                  w_high[n // FT][:, n % FT, :].bitcast(F32), ALU.subtract).then_inc(sig.sem)

        def prepare(dve, ex, done, sig):
            wide_pos = lambda p: p[:, bass.ds(ex * TIL, TIL)].unsqueeze(2).to_broadcast([P, TIL, CAP])
            wide_iota = iota[:].unsqueeze(1).to_broadcast([P, TIL, CAP])
            wide16 = lambda t: t[:].unsqueeze(2).to_broadcast([P, TIL, CAP])
            n = [0]

            def step(f):
                def go():
                    n[0] += 1
                    f().then_inc(sig.sem)
                    dve.wait_ge(*sig(5 * done + n[0]))
                return go
            return [
                step(lambda: dve.tensor_tensor(one[:], wide_pos(pos[0]), wide_iota, ALU.is_equal)),
                step(lambda: dve.tensor_tensor(two[:], wide_pos(pos[1]), wide_iota, ALU.is_equal)),
                step(lambda: dve.tensor_tensor(disp[:], one[:], two[:], ALU.add)),
                step(lambda: dve.tensor_tensor(one[:], one[:], wide16(col16["g1"]), ALU.mult)),
                step(lambda: dve.tensor_tensor(two[:], two[:], wide16(col16["g2"]), ALU.mult)),
            ], lambda: combine_halves(dve)

        def combine_halves(dve):
            for g in range(2):
                for q in range(GP):
                    tiles = slice(4 * q + 2 * g, 4 * q + 2 * g + 2)
                    ins = dve.tensor_tensor(comb[:, tiles, g * CAP:(g + 1) * CAP], one[:, tiles, :], two[:, tiles, :], ALU.add)
            return ins

        with nc.Block() as block:

            @block.tensor
            def _(pe):
                even = lambda t: t.rearrange("p (g t) e -> p g t e", t=2)[:, :, 0, :]
                odd = lambda t: t.rearrange("p (g t) e -> p g t e", t=2)[:, :, 1, :]
                table = lambda i: c.bank(i)[:, 0:NP_].rearrange("p (t e) -> p t e", t=TIL)
                pe.wait_ge(router_sig, 16)
                for t in range(TIL):
                    for k in range(FT):
                        mm = pe.matmul(c.bank(7)[:, t * EXP:(t + 1) * EXP], xn[:, k, t * P:(t + 1) * P],
                                       router[:, k, :], start=(k == 0), stop=(k == 1))
                mm.then_inc(s["logits"].sem)
                for t2 in range(TIL // 2):
                    if t2 >= 4:
                        pe.wait_ge(*s["copied"](t2 - 3))
                    for t in (0, 1):
                        for k in range(FT):
                            mm = pe.transpose(c.bank(2 + t2 % 4)[:, t * D + k * P:t * D + (k + 1) * P],
                                              xn[:, k, (2 * t2 + t) * P:(2 * t2 + t + 1) * P], c.ident[:])
                    mm.then_inc(s["turned"].sem)
                pe.wait_ge(*r["made"](3))
                pe.wait_ge(*r["cum1"](1))
                pe.matmul(table(0), before[:], tab["m1"][:], start=True, stop=False)
                pe.matmul(odd(table(0)), ones[:], even(tab["m1"][:]), start=False, stop=True).then_inc(r["cnt"].sem)
                pe.wait_ge(*r["cum2"](1))
                pe.matmul(table(1), before[:], tab["m2"][:], start=True, stop=False)
                pe.matmul(odd(table(1)), ones[:], even(tab["m2"][:]), start=False, stop=False)
                for to in (even, odd):
                    for of in (even, odd):
                        mm = pe.matmul(to(table(1)), ones[:], of(tab["m1"][:]), start=False, stop=(to is odd and of is odd))
                mm.then_inc(r["cnt"].sem)

            @block.scalar
            def _(act):
                act.wait_ge(*r["step"](2))
                act.activation(tab["raw"][:], tab["raw"][:], ACT.Exp).then_inc(r["step"].sem)
                for t2 in range(TIL // 2):
                    act.wait_ge(*s["turned"](t2 + 1))
                    act.activation(xn_tok[:, 2 * t2:2 * t2 + 2, :].rearrange("p t n -> p (t n)"), c.bank(2 + t2 % 4), ACT.Copy)\
                       .then_inc(s["copied"].sem)
                act.wait_ge(w_sig, W_LOAD)
                split_high(act, r["w_high"])

            @block.gpsimd
            def _(pool):
                pool.wait_ge(w_sig, W_LOAD)
                split_rest(pool, r["w_high"], r["w_rest"])

            @block.vector
            def _(dve):
                n = [0]

                def do(ins):
                    n[0] += 1
                    ins.then_inc(r["step"].sem)
                    dve.wait_ge(*r["step"](n[0]))

                wide = lambda t: t[:].unsqueeze(2).to_broadcast([P, TIL, EXP])
                order_w = order8[:].unsqueeze(1).to_broadcast([P, TIL, EXP])
                raw, rest, t = tab["raw"], tab["rest"], tab["t"]
                dve.wait_ge(*s["logits"](1))
                dve.tensor_copy(logits[:].rearrange("p t e -> p (t e)"), c.bank(7)[:, 0:NP_]).then_inc(s["logits_read"].sem)
                dve.wait_ge(*s["logits_read"](1))
                dve.wait_ge(*r["made"](3))
                do(dve.tensor_reduce(col16["mx"][:], logits[:], AX, ALU.max))
                do(dve.tensor_tensor(raw[:], logits[:], wide(col16["mx"]), ALU.subtract))
                n[0] += 1
                dve.wait_ge(*r["step"](n[0]))
                do(dve.tensor_reduce(col16["sm"][:], raw[:], AX, ALU.add))
                do(dve.reciprocal(col16["sm"][:], col16["sm"][:]))
                do(dve.tensor_tensor(raw[:], raw[:], wide(col16["sm"]), ALU.mult))

                def first_max(values, gate, chosen):
                    do(dve.tensor_reduce(gate[:], values[:], AX, ALU.max))
                    do(dve.tensor_tensor(t[:], values[:], wide(gate), ALU.is_equal))
                    do(dve.tensor_tensor(t[:], t[:], order_w, ALU.mult))
                    do(dve.tensor_reduce(col16["pick"][:], t[:], AX, ALU.max))
                    do(dve.tensor_tensor(chosen[:], t[:], wide(col16["pick"]), ALU.is_equal))

                first_max(raw, col16["g1"], tab["m1"])
                do(dve.tensor_tensor(t[:], raw[:], tab["m1"][:], ALU.mult))
                do(dve.tensor_tensor(rest[:], raw[:], t[:], ALU.subtract))
                first_max(rest, col16["g2"], tab["m2"])
                dve.tensor_copy(t[:], t[:]).then_inc(r["cum1"].sem)

                def keep(i, m, p, bank):
                    do(dve.tensor_copy(p[:].rearrange("p t e -> p (t e)"), c.bank(bank)[:, 0:NP_]))
                    do(dve.tensor_scalar(t[:], p[:], float(CAP), None, ALU.is_lt))
                    do(dve.tensor_tensor(m[:], m[:], t[:], ALU.mult))
                    do(dve.tensor_scalar(p[:], p[:], 1.0, None, ALU.add))
                    do(dve.tensor_tensor(p[:], p[:], m[:], ALU.mult))
                    do(dve.tensor_scalar(pos[i][:, 0:NP_].rearrange("p (e t) -> p t e", t=TIL), p[:], -1.0, None, ALU.add))

                dve.wait_ge(*r["cnt"](1))
                keep(0, tab["m1"], tab["p1"], 0)
                dve.tensor_copy(t[:], t[:]).then_inc(r["cum2"].sem)
                dve.wait_ge(r["cnt"].sem, 2)
                keep(1, tab["m2"], tab["p2"], 1)
                steps, last = prepare(dve, 0, 0, r["prep"])
                for go in steps:
                    go()
                last()

        def expert_round(rd, load):
            with nc.Block() as block:
                H_N = lambda h: P if h < HT - 1 else HLAST

                @block.sync
                def _(sync):
                    for i in range(2):
                        if i == 0 or load:
                            if i == 1:
                                sync.wait_ge(*e["w_rest"](PIECES))
                            load_first(sync, 2 * rd + 1 + i)
                        if load:
                            sync.wait_ge(*e["made"](RN * i + 8))
                            load_last(sync, i, 2 * rd + 2 + i)
                    if not load:
                        for q in range(GP):
                            sync.wait_ge(*e["read"](2 * RN - FT * (GP - 1 - q)))
                            sync.dma_start(c.out[:, :, q * CH:(q + 1) * CH], c.xT[:, :, q * CH:(q + 1) * CH]).then_inc(stored, 16)
                        sync.wait_ge(stored, GP * 16)

                @block.tensor
                def _(pe):
                    ring = [0]

                    def reuse():
                        n = ring[0]
                        ring[0] += 1
                        if n >= 4:
                            pe.wait_ge(*e["read"](n - 3))
                        return c.bank(4 + n % 4)

                    for i in range(2):
                        if i == 1:
                            pe.wait_ge(*e["prepared"](1))
                        for m in range(FT):
                            bank = reuse()
                            for g in range(GR):
                                for t in range(2):
                                    mm = pe.matmul(bank[:, g * CAP:(g + 1) * CAP], xn_tok[:, 2 * g + t, m * P:(m + 1) * P],
                                                   disp[:, 2 * g + t, :], start=(t == 0), stop=(t == 1))
                            mm.then_inc(e["made"].sem)
                        for q in range(GP):
                            bank = reuse()
                            for t in range(4):
                                mm = pe.transpose(bank[:, t * P:(t + 1) * P], comb[:, 4 * q + t, :], c.ident[:])
                            mm.then_inc(e["made"].sem)
                        pe.wait_ge(*e["read"](RN * i + FT))
                        if i == 1:
                            pe.wait_ge(*e["w_rest"](PIECES))
                        for h in range(HT):
                            n = HT * i + h
                            for w, base, free, done in ((0, 0, e["gelu"], e["w0_done"]), (1, 2, e["hidden"], e["w1_done"])):
                                if n >= 2:
                                    pe.wait_ge(*free(n - 1))
                                at = slice(h * P, h * P + H_N(h))
                                for k in range(FT):
                                    for of, x_of in ((w_high[w], x_high), (w_high[w], x_rest), (w_rest[w], x_high)):
                                        mm = pe.matmul(c.bank(base + n % 2)[0:H_N(h), :], of[:, k, at], x_of[:, k, :],
                                                       start=(k == 0 and of is w_high[w] and x_of is x_high),
                                                       stop=(k == FT - 1 and of is not w_high[w]))
                                mm.then_inc(done.sem)
                        pe.wait_ge(wo_sig[i], W_LOAD * (rd + 1))
                        pe.wait_ge(*e["hidden"](HT * (i + 1) - 1))
                        for q2 in range(2):
                            bank = reuse()
                            for q in (0, 1):
                                for h in range(HT):
                                    if q2 == 0 and q == 0 and h == HT - 1:
                                        pe.wait_ge(*e["hidden"](HT * (i + 1)))
                                    mm = pe.matmul(bank[:, q * D:(q + 1) * D],
                                                   hidden[0:H_N(h), h, (2 * q2 + q) * P:(2 * q2 + q + 1) * P],
                                                   wo[i][0:H_N(h), h, :], start=(h == 0), stop=(h == HT - 1))
                            mm.then_inc(e["made"].sem)
                        for q in range(GP):
                            pe.wait_ge(*e["read"](RN * i + 7 + q // 2))
                            for m in range(FT):
                                bank = reuse()
                                pe.matmul(bank, e_out[:, q, m * P:(m + 1) * P],
                                          back[:, 4 * q:4 * q + 4, :].rearrange("p t n -> p (t n)"), start=True, stop=True)\
                                  .then_inc(e["made"].sem)

                @block.scalar
                def _(act):
                    for n in range(2 * HT):
                        i, h = divmod(n, HT)
                        if h == 0:
                            for m in range(FT):
                                act.wait_ge(*e["made"](RN * i + m + 1))
                                act.activation(x_high[:, m, :], c.bank(4 + (RN * i + m) % 4), ACT.Copy).then_inc(e["x_high"].sem)
                        act.wait_ge(*e["w0_done"](n + 1))
                        if n >= 2:
                            act.wait_ge(*e["hidden"](n - 1))
                        act.activation(gelu[0:H_N(h), n % 2, :], c.bank(n % 2)[0:H_N(h), :], ACT.Gelu_apprx_tanh).then_inc(e["gelu"].sem)
                        if h == HT - 1 and (i == 0 or load):
                            act.wait_ge(*e["w1_done"](n + 1))
                            act.wait_ge(w_sig, W_LOAD * (2 * rd + i + 2))
                            split_high(act, e["w_high"])

                @block.vector
                def _(dve):
                    n = [0]

                    def take(f):
                        n[0] += 1
                        dve.wait_ge(*e["made"](n[0]))
                        f(c.bank(4 + (n[0] - 1) % 4)).then_inc(e["read"].sem)

                    for i in range(2):
                        for m in range(FT):
                            dve.wait_ge(*e["x_high"](FT * i + m + 1))
                            take(lambda bank: dve.tensor_tensor(x_rest[:, m, :], bank, x_high[:, m, :].bitcast(F32), ALU.subtract))
                        for q in range(GP):
                            take(lambda bank: dve.tensor_copy(back[:, 4 * q:4 * q + 4, :].rearrange("p t n -> p (t n)"), bank))
                        steps, last = prepare(dve, 2 * rd + 1 + i, i, e["prep"])
                        for h in range(HT):
                            k = HT * i + h
                            dve.wait_ge(*e["gelu"](k + 1))
                            dve.wait_ge(*e["w1_done"](k + 1))
                            dve.tensor_tensor(hidden[0:H_N(h), h, :], gelu[0:H_N(h), k % 2, :], c.bank(2 + k % 2)[0:H_N(h), :],
                                              ALU.mult).then_inc(e["hidden"].sem)
                            if h < len(steps):
                                steps[h]()
                            if h == len(steps):
                                last().then_inc(e["prepared"].sem)
                        if i == 0 or load:
                            dve.wait_ge(w_sig, W_LOAD * (2 * rd + i + 2))
                            split_rest(dve, lambda k: e["w_high"](PIECES * i + k), e["w_rest"])
                        for q2 in range(2):
                            take(lambda bank: dve.tensor_copy(e_out[:, 2 * q2:2 * q2 + 2, :].rearrange("p q n -> p (q n)"), bank))
                        for q in range(GP):
                            for m in range(FT):
                                xs = c.xT[:, m, q * CH:(q + 1) * CH]
                                take(lambda bank: dve.tensor_tensor(xs, bank, xs, ALU.add))

        ROUNDS = EXP // 2
        with nc.Fori(0, ROUNDS - 1) as rd:
            set_round(rd, e)
            expert_round(rd, True)
        set_round(ROUNDS - 1, e)
        expert_round(ROUNDS - 1, False)
        clear_signals(nc, norm_s, s, r, e, also=[w_sig, router_sig, stored] + wo_sig)


def load_everything(nc, ctx, c, x_t, weights, vectors):
    n_first = c.mats["x_wq"][0]
    loaded = ctx.enter_context(nc.semaphore("loaded"))
    c.first_loaded = ctx.enter_context(nc.semaphore("first_loaded"))
    c.others_loaded = ctx.enter_context(nc.semaphore("others_loaded"))
    made = ctx.enter_context(nc.semaphore("made"))
    with nc.Block() as block:

        @block.sync
        def _(sync):
            sync.dma_start(c.xT[:, :, 0:S], x_t[:, :, 0:S]).then_inc(loaded, 16)
            sync.dma_start(c.vectors[:], vectors).then_inc(loaded, 16)
            sync.dma_start(c.weights[:, 0:n_first], weights[:, 0:n_first]).then_inc(c.first_loaded, 16)
            sync.dma_start(c.xT[:, :, S:], x_t[:, :, S:]).then_inc(c.first_loaded, 16)
            sync.wait_ge(loaded, 32)

        @block.gpsimd
        def _(pool):
            pool.memset(c.mean_w[:], 1.0 / D)
            pool.memset(c.eps[:], LN_EPS)
            pool.memset(c.eps_eps[:], LN_EPS * LN_EPS)
            pool.memset(c.ident[:], 0.0).then_inc(made)
            pool.wait_ge(made, 1)
            pool.affine_select(out=c.ident[:], in_=c.ident[:], compare_op=ALU.not_equal, fill=1.0, base=0,
                               pattern=[[-1, P]], channel_multiplier=1).then_inc(made)


def wait_for_weights(nc, c):
    with nc.Block() as block:

        @block.sync
        def _(sync):
            sync.wait_ge(c.first_loaded, 32)
            sync.wait_ge(c.others_loaded, B * 16)


LAYERS = [linear_attention_layer, cross_attention_layer, gated_recurrence_layer, causal_attention_layer,
          context_attention_layer]


def build_program(nc, x_t, ctx_t, mask, weights, vectors, w0, w1, wo, out):
    with ExitStack() as ctx:
        c = Chip(nc, ctx)
        c.ctx_t, c.mask, c.weights_dram, c.w0, c.w1, c.wo, c.out = ctx_t, mask, weights, w0, w1, wo, out
        with ExitStack() as room:
            c.take_room(nc, room)
            load_everything(nc, ctx, c, x_t, weights, vectors)
            for n, layer in enumerate(LAYERS):
                if n == 1:
                    wait_for_weights(nc, c)
                layer(nc, c)
        expert_layer(nc, c)


def kernel(**inputs):
    import numpy as np
    import concourse.bacc as bacc
    from concourse import mybir as _mybir
    from concourse.bass_utils import run_bass_kernel_spmd

    a = {k: np.asarray(v) for k, v in inputs.items()}
    wqkv = a["L1_attn_Wqkv"]
    part = lambda i: wqkv[:, :, 16 * i:16 * (i + 1)].transpose(1, 0, 2).reshape(D, D)
    bias = lambda i: a["L1_attn_bqkv"][:, 16 * i:16 * (i + 1)].reshape(D)
    mats = {
        "a_wq": a["L0_attn_wq"], "a_wk": a["L0_attn_wk"], "a_wv": a["L0_attn_wv"], "a_wo": a["L0_attn_wo"],
        "a_w1": a["L0_attn_w_ff1"], "a_w2": a["L0_attn_w_ff2"], "a_wd": a["L0_attn_w_d"],
        "x_wq": a["L0_xattn_Wq"].T, "x_wkv": a["L0_xattn_Wkv"].T, "x_wlkv": a["L0_xattn_Wlkv"].T,
        "x_wo": a["L0_xattn_Wo"].T,
        "f_wf": a["L0_ffn_wf"].T, "f_uf": a["L0_ffn_uf"].T, "f_wi": a["L0_ffn_wi"].T, "f_ui": a["L0_ffn_ui"].T,
        "f_wc": a["L0_ffn_wc"].T, "f_uc": a["L0_ffn_uc"].T, "f_wo": a["L0_ffn_wo"].T, "f_uo": a["L0_ffn_uo"].T,
        "b_wq": part(0), "b_wk": part(1), "b_wv": part(2), "b_wo": a["L1_attn_Wout"],
        "y_wq": a["L1_xattn_wq"], "y_wk": a["L1_xattn_wk"], "y_wv": a["L1_xattn_wv"], "y_wo": a["L1_xattn_wo"],
        "router": a["L1_ffn_router_w"],
    }
    vecs = {
        "a_g1": a["L0_attn_ln1_g"], "a_b1": a["L0_attn_ln1_b"], "a_bo": a["L0_attn_bo"], "a_g2": a["L0_attn_ln2_g"],
        "a_b2": a["L0_attn_ln2_b"], "a_bf1": a["L0_attn_b_ff1"], "a_bf2": a["L0_attn_b_ff2"], "a_bd": a["L0_attn_b_d"],
        "x_gx": a["L0_xattn_ln_x_g"], "x_bx": a["L0_xattn_ln_x_b"], "x_gl": a["L0_xattn_ln_l_g"],
        "x_bl": a["L0_xattn_ln_l_b"], "x_gq": np.tile(a["L0_xattn_qn_g"], 2), "x_gk": np.tile(a["L0_xattn_kn_g"], 2),
        "x_bo": a["L0_xattn_bo"],
        "f_bf": a["L0_ffn_bf"], "f_bi": a["L0_ffn_bi"], "f_bc": a["L0_ffn_bc"], "f_bo": a["L0_ffn_bo"],
        "f_c0": a["L0_ffn_in_c"],
        "b_bq": bias(0), "b_bk": bias(1), "b_bv": bias(2), "b_bo": a["L1_attn_bout"],
        "y_bq": a["L1_xattn_bq"], "y_bk": a["L1_xattn_bk"], "y_bv": a["L1_xattn_bv"], "y_bo": a["L1_xattn_bo"],
    }

    def tiles(m):
        n = -(-m.shape[0] // P)
        full = np.zeros((n * P, m.shape[1]), m.dtype)
        full[:m.shape[0]] = m
        return full.reshape(n, P, -1).transpose(1, 0, 2).reshape(P, -1)

    ins = {
        "x_t": a["x"].reshape(T, FT, P).transpose(2, 1, 0),
        "ctx_t": tiles(a["ctx_768"].reshape(B * KEYS, CF).T),
        "mask": a["mask_BxS2_bk0"].reshape(1, B * KEYS),
        "weights": np.concatenate([tiles(mats[n]) for n in MATS], 1),
        "vectors": np.concatenate([tiles(vecs[n].reshape(-1, 1)) for n in VECS], 1),
        "w0": a["L1_ffn_w0_kernel"].reshape(EXP, FT, P, HID).transpose(0, 2, 1, 3),
        "w1": a["L1_ffn_w1_kernel"].reshape(EXP, FT, P, HID).transpose(0, 2, 1, 3),
        "wo": a["L1_ffn_wo_kernel"],
    }
    ins = {n: np.ascontiguousarray(v) for n, v in ins.items()}
    nc = bacc.Bacc("TRN2", target_bir_lowering=False, num_devices=1)
    args = [nc.dram_tensor(n, v.shape, _mybir.dt.from_np(v.dtype), kind="ExternalInput").ap() for n, v in ins.items()]
    out = nc.dram_tensor("out", (P, FT, T), F32, kind="ExternalOutput").ap()
    build_program(nc, *args, out)
    got = run_bass_kernel_spmd(nc, [ins], core_ids=[0]).results[0]["out"]
    return got.transpose(2, 1, 0).reshape(B, S, D)
```
